# Optimizing a Trainium2 kernel written in Bass

```python
import numpy as np
import jax
import jax.numpy as jnp

def _softmax(x, axis=-1):
    return jax.nn.softmax(x, axis=axis)

def _gelu(x):
    return jax.nn.gelu(x, approximate=True)

def _silu(x):
    return jax.nn.silu(x)

def _sigmoid(x):
    return jax.nn.sigmoid(x)

def _layernorm(x, axis=-1, eps=1e-05):
    m = jnp.mean(x, axis=axis, keepdims=True)
    v = jnp.var(x, axis=axis, keepdims=True)
    return (x - m) / jnp.sqrt(v + eps)

def _scatter_add(tgt, idx, src, axis=0):
    return tgt.at[idx].add(src)

def _segment_sum(src, seg, n):
    return jax.ops.segment_sum(src, seg, n)
kernel_name = 'mk_adaln_d1_jaxref_r4_aa1b3b'

def setup_inputs(seed: int=0):
    np.random.seed(seed)
    _w = jnp.asarray

    def _L0_attn_setup():
        import jax, jax.numpy as jnp
        import numpy as np
        import math
        EMBED_DIM = 512
        N_HEADS = 16
        HEAD_DIM = EMBED_DIM // N_HEADS
        THETA_BASE = 10000.0

        def _rope_freqs(seq_len):
            i = jnp.arange(HEAD_DIM // 2, dtype=jnp.float32)
            inv_freq = 1.0 / THETA_BASE ** (2.0 * i / HEAD_DIM)
            pos = jnp.arange(seq_len, dtype=jnp.float32)
            th = jnp.outer(pos, inv_freq)
            return (jnp.cos(th), jnp.sin(th))

        def _rope(t, cos, sin):
            b, h, s, d = t.shape
            tr = t.reshape(b, h, s, d // 2, 2)
            x0, x1 = (tr[..., 0], tr[..., 1])
            r0 = x0 * cos - x1 * sin
            r1 = x0 * sin + x1 * cos
            return jnp.stack([r0, r1], axis=-1).reshape(b, h, s, d)
        key = jax.random.key(seed)
        k1, k2, k3 = jax.random.split(key, 3)
        B, S = (2, 512)
        x = jax.random.normal(k1, (B, S, EMBED_DIM), jnp.float32)
        scale = EMBED_DIM ** (-0.5)
        Wqkv = jax.random.normal(k2, (EMBED_DIM, 3 * EMBED_DIM), jnp.float32) * scale
        Wo = jax.random.normal(k3, (EMBED_DIM, EMBED_DIM), jnp.float32) * scale
        return {'x': x, 'Wqkv': Wqkv, 'Wo': Wo}
    _L0_attn_in = _L0_attn_setup()

    def _L0_ffn_setup():
        import jax, jax.numpy as jnp
        import numpy as np
        TOP_K = 6
        CAP_FACTOR = 2

        def _shared_swiglu(x, wg, wu, wd):
            return jax.nn.silu(x @ wg.T) * (x @ wu.T) @ wd.T
        key = jax.random.key(seed)
        ks = jax.random.split(key, 8)
        B, S, D, E, F, FS = (4, 512, 512, 64, 352, 704)
        scale = jnp.float32(0.02)
        return {'hidden_states': jax.random.normal(ks[0], (B, S, D), jnp.float32), 'gate_w': jax.random.normal(ks[1], (E, D), jnp.float32) * scale, 'w_gate': jax.random.normal(ks[2], (E, F, D), jnp.float32) * scale, 'w_up': jax.random.normal(ks[3], (E, F, D), jnp.float32) * scale, 'w_down': jax.random.normal(ks[4], (E, D, F), jnp.float32) * scale, 'sh_gate': jax.random.normal(ks[5], (FS, D), jnp.float32) * scale, 'sh_up': jax.random.normal(ks[6], (FS, D), jnp.float32) * scale, 'sh_down': jax.random.normal(ks[7], (D, FS), jnp.float32) * scale}
    _L0_ffn_in = _L0_ffn_setup()
    _L0_c = _w((lambda *s: np.random.randn(*s).astype(np.float32) * 0.05)(2, 512))
    _L0_wmod = _w((lambda *s: np.random.randn(*s).astype(np.float32) * 0.05)(512, 6 * 512) * 512 ** (-0.5))
    _d = {'L0_attn_x': _L0_attn_in['x'], 'L0_attn_Wqkv': _L0_attn_in['Wqkv'], 'L0_attn_Wo': _L0_attn_in['Wo'], 'L0_ffn_gate_w': _L0_ffn_in['gate_w'], 'L0_ffn_w_gate': _L0_ffn_in['w_gate'], 'L0_ffn_w_up': _L0_ffn_in['w_up'], 'L0_ffn_w_down': _L0_ffn_in['w_down'], 'L0_ffn_sh_gate': _L0_ffn_in['sh_gate'], 'L0_ffn_sh_up': _L0_ffn_in['sh_up'], 'L0_ffn_sh_down': _L0_ffn_in['sh_down'], 'L0_c': _L0_c, 'L0_wmod': _L0_wmod}
    _x0 = _d['L0_attn_x']
    _d['L0_attn_x'] = jax.random.normal(jax.random.fold_in(jax.random.key(seed), 1), (2, 1024, 512), dtype=_x0.dtype)
    del _x0
    return _d

def reference(L0_attn_x, L0_attn_Wqkv, L0_attn_Wo, L0_ffn_gate_w, L0_ffn_w_gate, L0_ffn_w_up, L0_ffn_w_down, L0_ffn_sh_gate, L0_ffn_sh_up, L0_ffn_sh_down, L0_c, L0_wmod):

    def _L0_attn_ref(x, Wqkv, Wo):
        import jax, jax.numpy as jnp
        import numpy as np
        import math
        EMBED_DIM = 512
        N_HEADS = 16
        HEAD_DIM = EMBED_DIM // N_HEADS
        THETA_BASE = 10000.0

        def _rope_freqs(seq_len):
            i = jnp.arange(HEAD_DIM // 2, dtype=jnp.float32)
            inv_freq = 1.0 / THETA_BASE ** (2.0 * i / HEAD_DIM)
            pos = jnp.arange(seq_len, dtype=jnp.float32)
            th = jnp.outer(pos, inv_freq)
            return (jnp.cos(th), jnp.sin(th))

        def _rope(t, cos, sin):
            b, h, s, d = t.shape
            tr = t.reshape(b, h, s, d // 2, 2)
            x0, x1 = (tr[..., 0], tr[..., 1])
            r0 = x0 * cos - x1 * sin
            r1 = x0 * sin + x1 * cos
            return jnp.stack([r0, r1], axis=-1).reshape(b, h, s, d)
        B, S, E = x.shape
        H, D = (N_HEADS, E // N_HEADS)
        qkv = x @ Wqkv
        q, k, v = jnp.split(qkv, 3, axis=-1)
        heads = lambda t: t.reshape(B, S, H, D).transpose(0, 2, 1, 3)
        q, k, v = (heads(q), heads(k), heads(v))
        cos, sin = _rope_freqs(S)
        q = _rope(q, cos, sin)
        k = _rope(k, cos, sin)
        scores = jnp.einsum('bhqd,bhkd->bhqk', q, k) / math.sqrt(D)
        causal = jnp.tril(jnp.ones((S, S), dtype=bool))
        scores = jnp.where(causal, scores, -jnp.inf)
        attn = jax.nn.softmax(scores, axis=-1)
        op = jnp.einsum('bhqk,bhkd->bhqd', attn, v)
        op = op.transpose(0, 2, 1, 3).reshape(B, S, E)
        return op @ Wo

    def _L0_ffn_ref(hidden_states, gate_w, w_gate, w_up, w_down, sh_gate, sh_up, sh_down):
        import jax, jax.numpy as jnp
        import numpy as np
        TOP_K = 6
        CAP_FACTOR = 2

        def _shared_swiglu(x, wg, wu, wd):
            return jax.nn.silu(x @ wg.T) * (x @ wu.T) @ wd.T
        B, S, D = hidden_states.shape
        E = gate_w.shape[0]
        x = hidden_states.reshape(-1, D)
        N = x.shape[0]
        A = N * TOP_K
        C = CAP_FACTOR * ((A + E - 1) // E)
        scores = jax.nn.softmax(x @ gate_w.T, axis=-1)
        topk_w, topk_idx = jax.lax.top_k(scores, TOP_K)
        topk_w = topk_w / (topk_w.sum(-1, keepdims=True) + 1e-20)
        flat_e = topk_idx.reshape(-1)
        flat_w = topk_w.reshape(-1)
        order = jnp.argsort(flat_e)
        se = flat_e[order]
        st = order // TOP_K
        sw = flat_w[order]
        counts = jnp.bincount(flat_e, length=E)
        offsets = jnp.cumsum(counts) - counts
        pos = jnp.arange(A) - offsets[se]
        valid = pos < C
        pos_c = jnp.minimum(pos, C - 1)
        buf = jnp.zeros((E, C, D), x.dtype).at[se, pos_c].add(jnp.where(valid[:, None], x[st], jnp.zeros((), x.dtype)))
        g = jnp.einsum('ecd,efd->ecf', buf, w_gate)
        u = jnp.einsum('ecd,efd->ecf', buf, w_up)
        eo = jnp.einsum('ecf,edf->ecd', jax.nn.silu(g) * u, w_down)
        gathered = eo[se, pos_c] * (sw * valid.astype(sw.dtype))[:, None]
        y = jnp.zeros_like(x).at[st].add(gathered).reshape(B, S, D)
        return y + _shared_swiglu(hidden_states, sh_gate, sh_up, sh_down)
    x = L0_attn_x
    mod = (_silu(L0_c) @ L0_wmod).reshape(L0_c.shape[0], 6, 1, -1)
    sa, ca, ga, sb, cb, gb = (mod[:, 0], mod[:, 1], mod[:, 2], mod[:, 3], mod[:, 4], mod[:, 5])
    ga = (2 * (ga >= 0) - 1) * jnp.maximum(jnp.abs(ga), 0.25)
    gb = (2 * (gb >= 0) - 1) * jnp.maximum(jnp.abs(gb), 0.25)
    h = _layernorm(x, axis=-1) * (1 + ca) + sa
    x = x + ga * _L0_attn_ref(h, L0_attn_Wqkv, L0_attn_Wo)
    h = _layernorm(x, axis=-1) * (1 + cb) + sb
    x = x + gb * _L0_ffn_ref(h, L0_ffn_gate_w, L0_ffn_w_gate, L0_ffn_w_up, L0_ffn_w_down, L0_ffn_sh_gate, L0_ffn_sh_up, L0_ffn_sh_down)
    return x

_drawn_inputs = setup_inputs


def setup_inputs(seed=0):
    import zlib

    import numpy as np

    out = dict(_drawn_inputs(seed))
    spreads = {}
    factors = {'L0_ffn_gate_w': 8.0,
     'L0_ffn_w_gate': 8.0,
     'L0_ffn_w_up': 8.0,
     'L0_ffn_w_down': 8.0,
     'L0_ffn_sh_gate': 4.007,
     'L0_ffn_sh_up': 3.918,
     'L0_ffn_sh_down': 3.912}
    for name, (base, spread) in spreads.items():
        noise = np.random.default_rng([zlib.crc32(name.encode()), seed]).standard_normal(out[name].shape)
        drawn = base * np.exp(spread * noise) if base else spread * noise
        out[name] = jnp.asarray(drawn.astype(out[name].dtype))
    for name, factor in factors.items():
        out[name] = (out[name] * factor).astype(out[name].dtype)
    return out
```

```python
import math
from contextlib import ExitStack

import numpy as np

import concourse.bass as bass
from concourse import mybir

P = 128
BATCH, SEQ, DIM = 2, 1024, 512
TOK = BATCH * SEQ
TILES = TOK // P
BT = SEQ // P
KC = DIM // P
HEADS, HD = 16, 32
EXPERTS, TOPK = 64, 6
CAP = 2 * ((TOK * TOPK + EXPERTS - 1) // EXPERTS)
SLOT_TILES = CAP // P
FF = 352
FCH = (FF + P - 1) // P
SH = 704
SCH = (SH + P - 1) // P
UP = KC * 2 * FF
DOWN = FCH * DIM
EPS = 1e-5
BANK = 512
GT = 4

ACT_SCALE = 16.0
W_SCALE = 64.0
QKV_SCALE = 8.0
P_SCALE = 1024.0
H_SCALE = 4.0
PROD = ACT_SCALE * W_SCALE
MASKED = -1e30
DROPPED = float(1 << 20)

CONSTS = dict(ident=P, mask=P, tri=P, iota=EXPERTS, slot0=EXPERTS, cos=BT * HD, sin=BT * HD, token=TILES)


def columns():
    at, where = 0, {}
    for name, n in CONSTS.items():
        where[name] = (at, at + n)
        at += n
    return where, at


def constants():
    where, n = columns()
    c = np.zeros((P, n), np.float32)
    p, j = np.arange(P)[:, None], np.arange(P)[None, :]

    def put(name, value):
        c[:, where[name][0]:where[name][1]] = value

    put("ident", p == j)
    put("mask", np.where(j > p, MASKED, 0.0))
    put("tri", p < j)
    put("iota", np.arange(EXPERTS)[None, :])
    put("slot0", np.arange(EXPERTS)[None, :] * CAP)
    i = np.arange(HD // 2, dtype=np.float32)
    inv = (np.float32(1.0) / np.float32(10000.0) ** (np.float32(2.0) * i / np.float32(HD))).astype(np.float32)
    th = np.arange(SEQ, dtype=np.float32)[:, None] * inv[None, :]
    s = np.float32(QKV_SCALE / PROD)
    cos = np.repeat(np.cos(th) * s, 2, 1)
    sin = np.repeat(np.sin(th) * s, 2, 1)
    sin[:, 0::2] *= -1
    for name, t in (("cos", cos), ("sin", sin)):
        put(name, t.reshape(BT, P, HD).transpose(1, 0, 2).reshape(P, BT * HD))
    put("token", np.arange(TILES)[None, :] * P + p)
    return c


def empty_slots():
    t = np.zeros((EXPERTS * CAP, 2), np.int32)
    t[:, 0] = TOK + np.arange(EXPERTS * CAP) % CAP
    return t


def wait(engine, sem, value):
    if not (isinstance(value, int) and value <= 0):
        engine.wait_ge(sem, value)


def pairs(engine, n, emit, base=0):
    emit(base, 0, True, False)
    emit(base + 1, 1, False, False)
    with engine.Fori(1, n // 2 - 1) as m:
        emit(m * 2 + base, 0, False, False)
        emit(m * 2 + base + 1, 1, False, False)
    emit(base + n - 2, 0, False, False)
    emit(base + n - 1, 1, False, True)


def peeled(engine, n, emit):
    emit(0)
    with engine.Fori(1, n) as m:
        emit(m)


def loads(g, par):
    return (g - par) * 8 + 16


def adaln_program(nc, t):
    fp32, fp16, bf16 = mybir.dt.float32, mybir.dt.float16, mybir.dt.bfloat16
    i32, u32 = mybir.dt.int32, mybir.dt.uint32
    ALU, ACT, AX = mybir.AluOpType, mybir.ActivationFunctionType, mybir.AxisListType
    where, n_const = columns()
    top = ExitStack()
    with top:
        PS = top.enter_context(nc.psum_tensor("PS", [P, 8, BANK], fp32))

        def sems(stack, names):
            return [stack.enter_context(nc.semaphore(n)) for n in names.split()]

        consts = top.enter_context(nc.sbuf_tensor("consts", [P, n_const], fp32))

        def const(name):
            return consts[:, where[name][0]:where[name][1]]

        ident32 = const("ident")
        cb = top.enter_context(nc.sbuf_tensor("cb", [P, 4, P], bf16))
        ident16 = top.enter_context(nc.sbuf_tensor("ident16", [P, P], fp16))
        stat1 = top.enter_context(nc.sbuf_tensor("stat1", [P, TILES, 2], fp32))
        mod_d = nc.dram_tensor("mod_d", [BATCH, 6 * DIM], fp32).ap()
        (tick,) = sems(top, "tick")

        stat2 = top.enter_context(nc.sbuf_tensor("stat2", [P, TILES, 2], fp32))

        def deviation(dve, raw6, small, stat, step, root):
            me, qe, mo, qo = (raw6[:, :, c] for c in (1, 2, 4, 5))
            nc.vector.tensor_tensor(small[:, 0, :], me, mo, ALU.add).then_inc(step, 1)
            nc.vector.tensor_tensor(small[:, 1, :], me, mo, ALU.subtract).then_inc(step, 1)
            nc.vector.tensor_tensor(small[:, 2, :], qe, qo, ALU.add).then_inc(step, 1)
            dve.wait_ge(step, 3)
            nc.vector.tensor_scalar(stat[:, :, 0], small[:, 0, :], 0.5, None, ALU.mult).then_inc(step, 1)
            nc.vector.scalar_tensor_tensor(small[:, 5, :], small[:, 1, :], 0.25, small[:, 1, :],
                                           ALU.mult, ALU.mult).then_inc(step, 1)
            nc.vector.tensor_scalar(small[:, 6, :], small[:, 2, :], 1.0 / DIM, EPS,
                                    ALU.mult, ALU.add).then_inc(step, 1)
            dve.wait_ge(step, 6)
            nc.vector.tensor_tensor(small[:, 3, :], small[:, 5, :], small[:, 6, :], ALU.add).then_inc(step, 1)
            dve.wait_ge(root, 1)
            nc.vector.reciprocal(small[:, 5, :], small[:, 4, :]).then_inc(step, 1)
            dve.wait_ge(step, 8)
            nc.vector.tensor_tensor(small[:, 6, :], small[:, 5, :], small[:, 5, :], ALU.mult).then_inc(step, 1)
            dve.wait_ge(step, 9)
            nc.vector.scalar_tensor_tensor(small[:, 7, :], small[:, 6, :], -0.5, small[:, 3, :],
                                           ALU.mult, ALU.mult).then_inc(step, 1)
            dve.wait_ge(step, 10)
            nc.vector.scalar_tensor_tensor(stat[:, :, 1], small[:, 7, :], 1.5, small[:, 5, :],
                                           ALU.add, ALU.mult).then_inc(step, 1)

        s2 = ExitStack()
        wqkv_hi = s2.enter_context(nc.sbuf_tensor("wqkv_hi", [P, KC, 3 * DIM], fp16))
        wqkv_lo = s2.enter_context(nc.sbuf_tensor("wqkv_lo", [P, KC, 3 * DIM], fp16))
        with ExitStack() as st:
            def sb(name, shape, dt):
                return st.enter_context(nc.sbuf_tensor(name, shape, dt))

            c_in = sb("c_in", [P, KC * BATCH], fp32)
            c_silu = sb("c_silu", [P, KC, BATCH], fp32)
            wmod = sb("wmod", [P, KC, 6 * DIM], fp32)
            wqkv = sb("wqkv", [P, KC, 3 * DIM], fp32)
            xall = sb("xall", [P, TILES, DIM], fp32)
            rows = sb("rows", [BATCH, 6, DIM], fp32)
            sign = sb("sign", [BATCH, DIM], fp32)
            minus = sb("minus", [BATCH, DIM], fp32)
            size = sb("size", [BATCH, DIM], fp32)
            raw6 = sb("raw6", [P, TILES, 6], fp32)
            small = sb("small", [P, 8, TILES], fp32)
            (c_loaded, const_loaded, wmod_loaded, wqkv_loaded, x_loaded, c_ready, mod_done, row_ready, gate_step,
             rows_stored, cb_ready, wq_hi, wq_lo, stats, step, root) = sems(
                st, "c_loaded const_loaded wmod_loaded wqkv_loaded x_loaded c_ready mod_done row_ready gate_step "
                    "rows_stored cb_ready wq_hi wq_lo stats step root")
            block = st.enter_context(nc.Block())

            @block.sync
            def _(sp):
                sp.dma_start(c_in[:, :], t["c"]).then_inc(c_loaded, 16)
                sp.dma_start(wmod[:, :, :], t["wmod"]).then_inc(wmod_loaded, 16)
                sp.dma_start(wqkv[:, :, :], t["wqkv"]).then_inc(wqkv_loaded, 16)
                sp.wait_ge(row_ready, 6)
                sp.dma_start(mod_d, rows[:, :, :].rearrange("b s d -> b (s d)")).then_inc(rows_stored, 16)
                sp.wait_ge(rows_stored, 16)

            @block.scalar
            def _(act):
                act.dma_start(consts[:, :], t["consts"]).then_inc(const_loaded, 16)
                act.dma_start(xall[:, :, :], t["x"].rearrange("(n p) d -> p n d", p=P)).then_inc(x_loaded, 16)
                act.wait_ge(c_loaded, 16)
                nc.scalar.activation(c_silu[:, :, :].rearrange("p k b -> p (k b)"), c_in[:, :],
                                     ACT.Silu).then_inc(c_ready, 1)
                act.wait_ge(wqkv_loaded, 16)
                for k in range(KC):
                    nc.scalar.activation(wqkv_hi[:, k, :], wqkv[:, k, :], ACT.Copy,
                                         scale=W_SCALE).then_inc(wq_hi, 1)
                act.wait_ge(step, 7)
                nc.scalar.activation(small[:, 4, :], small[:, 3, :], ACT.Sqrt).then_inc(root, 1)

            @block.tensor
            def _(pe):
                pe.wait_ge(c_ready, 1)
                pe.wait_ge(wmod_loaded, 16)
                for g in range(6):
                    for k in range(KC):
                        last = nc.tensor.matmul(PS[0:BATCH, g, :], c_silu[:, k, :],
                                                wmod[:, k, g * DIM:(g + 1) * DIM], start=k == 0, stop=k == KC - 1)
                    last.then_inc(mod_done, 1)

            @block.vector
            def _(dve):
                dve.wait_ge(const_loaded, 16)
                nc.vector.tensor_copy(ident16[:, :], ident32).then_inc(cb_ready, 1)
                for n, name in enumerate(("ident", "mask", "tri")):
                    nc.vector.tensor_copy(cb[:, n, :], const(name)).then_inc(cb_ready, 1)
                nc.vector.memset(cb[:, 3, :], 1.0).then_inc(cb_ready, 1)
                dve.wait_ge(x_loaded, 16)
                with dve.Fori(0, TILES) as n:
                    nc.vector.bn_stats(raw6[:, bass.ds(n, 1), :], xall[:, bass.ds(n, 1), :]).then_inc(stats, 1)
                dve.wait_ge(stats, TILES)
                deviation(dve, raw6, small, stat1, step, root)
                gates = 0
                for g in range(6):
                    dve.wait_ge(mod_done, g + 1)
                    if g % 3 < 2:
                        nc.vector.tensor_scalar(rows[:, g, :], PS[0:BATCH, g, :], float(g % 3), None,
                                                ALU.add).then_inc(row_ready, 1)
                    else:
                        if gates:
                            dve.wait_ge(row_ready, g)
                        nc.vector.tensor_scalar(sign[:, :], PS[0:BATCH, g, :], 0.0, 2.0, ALU.is_ge,
                                                ALU.mult).then_inc(gate_step, 1)
                        nc.vector.tensor_scalar(minus[:, :], PS[0:BATCH, g, :], -1.0, None,
                                                ALU.mult).then_inc(gate_step, 1)
                        dve.wait_ge(gate_step, gates + 2)
                        nc.vector.scalar_tensor_tensor(size[:, :], PS[0:BATCH, g, :], 0.25, minus[:, :],
                                                       ALU.max, ALU.max).then_inc(gate_step, 1)
                        gates += 3
                        dve.wait_ge(gate_step, gates)
                        nc.vector.scalar_tensor_tensor(rows[:, g, :], sign[:, :], -1.0, size[:, :],
                                                       ALU.add, ALU.mult).then_inc(row_ready, 1)
                for k in range(KC):
                    dve.wait_ge(wq_hi, k + 1)
                    nc.vector.scalar_tensor_tensor(wqkv_lo[:, k, :], wqkv[:, k, :], W_SCALE, wqkv_hi[:, k, :],
                                                   ALU.mult, ALU.subtract).then_inc(wq_lo, 1)


        attn_d = nc.dram_tensor("attn_d", [TOK, DIM], fp32).ap()
        with s2:
            def sb(name, shape, dt):
                return s2.enter_context(nc.sbuf_tensor(name, shape, dt))

            QT = sb("QT", [P, HEADS, SEQ], fp16)
            KT = sb("KT", [P, HEADS, SEQ], fp16)
            V = sb("V", [P, BT, HEADS, 2, HD], fp16)
            hT_hi = sb("hT_hi", [P, KC, SEQ], fp16)
            hT_lo = sb("hT_lo", [P, KC, SEQ], fp16)
            mod1 = sb("mod1", [P, BATCH, 2, DIM], fp32)
            xin = sb("xin", [P, 2, DIM], fp32)
            z = sb("z", [P, 2, DIM], fp32)
            zm = sb("zm", [P, 2, DIM], fp32)
            h = sb("h", [P, 2, DIM], fp32)
            rot = sb("rot", [P, 2, 2 * HEADS, HD], fp32)
            qk = sb("qk", [P, 2 * HEADS, HD], fp32)
            qk16 = sb("qk16", [P, 2 * HEADS, 4, HD], fp16)
            O = sb("O", [P, BT, DIM], fp32)
            Pr = sb("Pr", [P, 2, SEQ], fp32)
            PT_hi = sb("PT_hi", [P, 2, BT, P], fp16)
            PT_lo = sb("PT_lo", [P, 2, BT, P], fp16)
            negmax = sb("negmax", [P, 2], fp32)
            bias = sb("bias", [P, 2], fp32)
            exp_scale = sb("exp_scale", [P, 1], fp32)
            rowsum = sb("rowsum", [P, 2, BT], fp32)
            inv = sb("inv", [P, 2, BT], fp32)
            half = sb("half", [P, 2, BT, HD], fp32)
            SCORE = 1.0 / (math.sqrt(HD) * QKV_SCALE * QKV_SCALE)
            GROUPS = [(i, j, min(j + 4, i + 1)) for i in range(BT) for j in range(0, i + 1, 4)]
            GN = len(GROUPS)
            GEND = [max(n for n, g in enumerate(GROUPS) if g[0] == i) + 1 for i in range(BT)]

            (mod_in, xin_a, xin_b, scale_set, z_ready, zm_ready, h_ready, hT_raw, hT_hi_ready, hT_lo_ready,
             qkv_done, cos_done, sin_done, v_hi_ready, v_lo_ready, qk_ready, qk_hi, qk_lo, parts_copied, qkT_done, q_copied, k_copied,
             s_done, max_done, bias_done, exp_done, pT_done, p_hi, p_lo, pv_done, inv_done, half_done, o_done,
             o_stored) = sems(
                s2, "mod_in xin_a xin_b scale_set z_ready zm_ready h_ready hT_raw hT_hi_ready hT_lo_ready qkv_done "
                    "cos_done sin_done v_hi_ready v_lo_ready qk_ready qk_hi qk_lo parts_copied qkT_done q_copied k_copied s_done "
                    "max_done bias_done exp_done pT_done p_hi p_lo pv_done inv_done half_done o_done o_stored")
            xin_loaded = (xin_a, xin_b)
            block = s2.enter_context(nc.Block())

            @block.sync
            def _(sp):
                for b in range(BATCH):
                    sp.dma_start(mod1[:, b, :, :].rearrange("p s d -> p (s d)"),
                                 mod_d[b:b + 1, 0:2 * DIM].partition_broadcast(P)).then_inc(mod_in, 16)
                with sp.Fori(0, BATCH) as b:
                    with sp.Fori(0, BT // 2) as m:
                        for par in range(2):
                            g = b * BT + m * 2 + par
                            sp.wait_ge(z_ready, g - par)
                            sp.dma_start(xin[:, par, :], t["x"][bass.ds(g * P, P), :]).then_inc(xin_loaded[par], 16)
                    sp.wait_ge(o_done, (b + 1) * HEADS)
                    sp.dma_start(attn_d[bass.ds(b * SEQ, SEQ), :].rearrange("(n p) d -> p n d", p=P),
                                 O[:, :, :]).then_inc(o_stored, 16)
                sp.wait_ge(o_stored, 16 * BATCH)

            def score_unit(pe, H, hh, i, first):
                if not first:
                    pe.wait_ge(exp_done, H * BT + i - 1)
                s = PS[:, 2 * (i % 2):2 * (i % 2) + 2, :].rearrange("p a n -> p (a n)")
                q = QT[:, bass.ds(hh, 1), i * P:(i + 1) * P]
                for at in range(0, (i + 1) * P, BANK):
                    end = min(at + BANK, (i + 1) * P)
                    diagonal = end == (i + 1) * P
                    last = nc.tensor.matmul(s[:, at:end], q, KT[:, bass.ds(hh, 1), at:end],
                                            start=True, stop=not diagonal)
                    if diagonal:
                        last = nc.tensor.matmul(s[:, i * P:end], cb[:, 0, :], cb[:, 1, :], start=False, stop=True)
                last.then_inc(s_done, 1)

            def pv_unit(pe, H, hh, hp, i, first):
                pe.wait_ge(p_lo, H * GN + GEND[i])
                if i == 0 and not first:
                    pe.wait_ge(half_done, 2 * (H - 1))
                for j in range(i + 1):
                    for part in (PT_hi, PT_lo):
                        last = nc.tensor.matmul(
                            PS[:, 6 + hp, i * 2 * HD:(i + 1) * 2 * HD], part[:, i % 2, j, :],
                            V[:, j, bass.ds(hh, 1), :, :].rearrange("p h s d -> p (h s d)"),
                            start=j == 0 and part is PT_hi, stop=j == i and part is PT_lo)
                last.then_inc(pv_done, 1)

            def pe_head(pe, b, hh, hp, start, end):
                H = b * HEADS + hh
                if start:
                    score_unit(pe, H, hh, 0, True)
                for i in range(BT):
                    if i + 1 < BT:
                        score_unit(pe, H, hh, i + 1, start and i == 0)
                    elif not end:
                        score_unit(pe, H + 1, hh + 1, 0, False)
                    pe.wait_ge(exp_done, H * BT + i + 1)
                    for n, (gi, lo, hi) in enumerate(GROUPS):
                        if gi != i:
                            continue
                        if n >= 2 or not start:
                            pe.wait_ge(p_lo, H * GN + n - 1)
                        for j in range(lo, hi):
                            last = nc.tensor.transpose(PS[:, 4 + n % 2, (j - lo) * P:(j - lo + 1) * P],
                                                       Pr[:, i % 2, j * P:(j + 1) * P], ident32)
                        last.then_inc(pT_done, 1)
                    if i:
                        pv_unit(pe, H, hh, hp, i - 1, start and True)
                pv_unit(pe, H, hh, hp, BT - 1, start)

            def heads(engine, emit):
                emit(0, 0, True, False)
                emit(1, 1, False, False)
                with engine.Fori(1, HEADS // 2 - 1) as m:
                    emit(m * 2, 0, False, False)
                    emit(m * 2 + 1, 1, False, False)
                emit(HEADS - 2, 0, False, False)
                emit(HEADS - 1, 1, False, True)

            @block.tensor
            def _(pe):
                def transpose_qk(g, tile):
                    pe.wait_ge(parts_copied, 3 * (g + 1))
                    for quarter in range(4):
                        bank = PS[:, 7 - quarter % 2, :].bitcast(fp16)
                        if quarter >= 2:
                            pe.wait_ge(q_copied, 2 * g + quarter - 1)
                        else:
                            pe.wait_ge(k_copied, 2 * g)
                        for n in range(8):
                            head = quarter * 8 + n
                            last = nc.tensor.transpose(bank[:, n * P:(n + 1) * P],
                                                       qk16[:, head, :, :].rearrange("p s d -> p (s d)"),
                                                       ident16[:, :])
                        last.then_inc(qkT_done, 1)

                def project(g, tile, par):
                    pe.wait_ge(hT_lo_ready, g + 1)
                    pe.wait_ge(sin_done, 2 * (g - par) )
                    pe.wait_ge(v_lo_ready, g - par)
                    for n in range(3):
                        for k in range(KC):
                            lhs_hi, lhs_lo = (w[:, k, bass.ds(tile * P, P)] for w in (hT_hi, hT_lo))
                            cols = slice(n * DIM, (n + 1) * DIM)
                            for m, (l, r) in enumerate(((lhs_hi, wqkv_hi), (lhs_hi, wqkv_lo), (lhs_lo, wqkv_hi))):
                                last = nc.tensor.matmul(PS[:, 3 * par + n, :], l, r[:, k, cols],
                                                        start=k == 0 and m == 0, stop=k == KC - 1 and m == 2)
                    last.then_inc(qkv_done, 1)

                with pe.Fori(0, BATCH) as b:
                    with pe.Fori(0, BT // 2) as m:
                        for par in range(2):
                            g = b * BT + m * 2 + par
                            pe.wait_ge(h_ready, g + 1)
                            pe.wait_ge(hT_lo_ready, g)
                            for k in range(KC):
                                last = nc.tensor.transpose(PS[:, 6, k * P:(k + 1) * P],
                                                           h[:, par, k * P:(k + 1) * P], ident32)
                            last.then_inc(hT_raw, 1)
                    project(b * BT, 0, 0)
                    project(b * BT + 1, 1, 1)
                    transpose_qk(b * BT, 0)
                    with pe.Fori(1, BT // 2) as m:
                        for par in range(2):
                            project(b * BT + m * 2 + par, m * 2 + par, par)
                            transpose_qk(b * BT + m * 2 + par - 1, m * 2 + par - 1)
                    transpose_qk(b * BT + BT - 1, BT - 1)
                    pe.wait_ge(q_copied, 2 * BT * (b + 1))
                    pe.wait_ge(k_copied, 2 * BT * (b + 1))
                    heads(pe, lambda hh, hp, start, end: pe_head(pe, b, hh, hp, start, end))

            @block.scalar
            def _(act):
                def exp_unit(H, hp, i, first):
                    act.wait_ge(bias_done, H * BT + i + 1)
                    if not first:
                        act.wait_ge(pT_done, H * GN + (GEND[i - 2] if i >= 2 else GEND[BT - 2 + i] - GN))
                    s = PS[:, 2 * (i % 2):2 * (i % 2) + 2, :].rearrange("p a n -> p (a n)")
                    nc.scalar.activation(Pr[:, i % 2, 0:(i + 1) * P], s[:, 0:(i + 1) * P], ACT.Exp,
                                         bias=bias[:, i % 2:i % 2 + 1], scale=SCORE,
                                         accum_out=rowsum[:, hp, i:i + 1]).then_inc(exp_done, 1)

                def head(b, hh, hp, start, end):
                    H = b * HEADS + hh
                    if start:
                        exp_unit(H, hp, 0, True)
                    for i in range(BT):
                        if i + 1 < BT:
                            exp_unit(H, hp, i + 1, start and i == 0)
                        elif not end:
                            exp_unit(H + 1, 1 - hp, 0, False)
                        if not (start and i < 2):
                            act.wait_ge(pv_done, H * BT + i - 1)
                        for n, (gi, lo, hi) in enumerate(GROUPS):
                            if gi == i:
                                act.wait_ge(pT_done, H * GN + n + 1)
                                nc.scalar.activation(
                                    PT_hi[:, i % 2, lo:hi, :].rearrange("p j n -> p (j n)"),
                                    PS[:, 4 + n % 2, 0:(hi - lo) * P], ACT.Copy, scale=P_SCALE).then_inc(p_hi, 1)

                with act.Fori(0, BATCH) as b:
                    with act.Fori(0, BT) as n:
                        g = b * BT + n
                        act.wait_ge(hT_raw, g + 1)
                        nc.scalar.activation(hT_hi[:, :, bass.ds(n * P, P)],
                                             PS[:, 6, :].rearrange("p (k n) -> p k n", k=KC), ACT.Copy,
                                             scale=ACT_SCALE).then_inc(hT_hi_ready, 1)
                    with act.Fori(0, BT // 2) as m:
                        for par in range(2):
                            g = b * BT + m * 2 + par
                            act.wait_ge(qkv_done, g + 1)
                            nc.scalar.activation(V[:, bass.ds(m * 2 + par, 1), :, 0, :],
                                                 PS[:, 3 * par + 2, :].rearrange("p (h d) -> p h d", h=HEADS),
                                                 ACT.Copy, scale=QKV_SCALE / PROD).then_inc(v_hi_ready, 1)
                            act.wait_ge(qk_ready, g + 1)
                            act.wait_ge(qkT_done, 4 * g)
                            nc.scalar.activation(qk16[:, :, 0, :], qk[:, :, :], ACT.Copy).then_inc(qk_hi, 1)
                            for quarter in range(2):
                                act.wait_ge(qkT_done, 4 * g + quarter + 1)
                                nc.scalar.activation(
                                    QT[:, quarter * 8:quarter * 8 + 8, bass.ds((m * 2 + par) * P, P)],
                                    PS[:, 7 - quarter, :].bitcast(fp16).rearrange("p (h n) -> p h n", h=8),
                                    ACT.Copy).then_inc(q_copied, 1)
                    heads(act, lambda hh, hp, start, end: head(b, hh, hp, start, end))

            @block.vector
            def _(dve):
                nc.vector.memset(exp_scale[:, :], SCORE).then_inc(scale_set, 1)

                def max_unit(H, i, first):
                    dve.wait_ge(s_done, H * BT + i + 1)
                    if not first:
                        dve.wait_ge(bias_done, H * BT + i - 1)
                    s = PS[:, 2 * (i % 2):2 * (i % 2) + 2, :].rearrange("p a n -> p (a n)")
                    nc.vector.tensor_reduce(negmax[:, i % 2:i % 2 + 1], s[:, 0:(i + 1) * P], AX.X, ALU.max,
                                            negate=True).then_inc(max_done, 1)

                def head(b, hh, hp, start, end):
                    H = b * HEADS + hh
                    if start:
                        max_unit(H, 0, True)
                    for i in range(BT):
                        if i + 1 < BT:
                            max_unit(H, i + 1, start and i == 0)
                        elif not end:
                            max_unit(H + 1, 0, False)
                        for n, (gi, lo, hi) in enumerate(GROUPS):
                            if gi == i:
                                dve.wait_ge(p_hi, H * GN + n + 1)
                                nc.vector.scalar_tensor_tensor(
                                    PT_lo[:, i % 2, lo:hi, :].rearrange("p j n -> p (j n)"),
                                    PS[:, 4 + n % 2, 0:(hi - lo) * P], P_SCALE,
                                    PT_hi[:, i % 2, lo:hi, :].rearrange("p j n -> p (j n)"),
                                    ALU.mult, ALU.subtract).then_inc(p_lo, 1)
                    if not start:
                        dve.wait_ge(o_done, H)
                    nc.vector.reciprocal(inv[:, hp, :], rowsum[:, hp, :]).then_inc(inv_done, 1)
                    dve.wait_ge(inv_done, H + 1)
                    dve.wait_ge(pv_done, (H + 1) * BT)
                    o = PS[:, 6 + hp, :].rearrange("p (i s d) -> p i s d", i=BT, s=2)
                    for s in range(2):
                        nc.vector.scalar_tensor_tensor(
                            half[:, s, :, :], o[:, :, s, :], 1.0 / (P_SCALE * QKV_SCALE),
                            inv[:, hp, :].unsqueeze(2).broadcast_to([P, BT, HD]),
                            ALU.mult, ALU.mult).then_inc(half_done, 1)

                with dve.Fori(0, BATCH) as b:
                    dve.wait_ge(mod_in, 16 * BATCH)
                    with dve.Fori(0, BT // 2) as m:
                        for par in range(2):
                            tile = m * 2 + par
                            g = b * BT + tile
                            dve.wait_ge(xin_loaded[par], 16 * (b * (BT // 2) + m + 1))
                            dve.wait_ge(h_ready, g - par)
                            nc.vector.tensor_scalar(z[:, par, :], xin[:, par, :], stat1[:, bass.ds(g, 1), 0],
                                                    stat1[:, bass.ds(g, 1), 1], ALU.subtract,
                                                    ALU.mult).then_inc(z_ready, 1)
                            dve.wait_ge(z_ready, g + 1)
                            nc.vector.tensor_tensor(zm[:, par, :], z[:, par, :], mod1[:, bass.ds(b, 1), 1, :],
                                                    ALU.mult).then_inc(zm_ready, 1)
                            dve.wait_ge(hT_hi_ready, g + 1)
                            nc.vector.scalar_tensor_tensor(
                                hT_lo[:, :, bass.ds(tile * P, P)], PS[:, 6, :].rearrange("p (k n) -> p k n", k=KC),
                                ACT_SCALE, hT_hi[:, :, bass.ds(tile * P, P)],
                                ALU.mult, ALU.subtract).then_inc(hT_lo_ready, 1)
                    with dve.Fori(0, BT // 2) as m:
                        for par in range(2):
                            tile = m * 2 + par
                            g = b * BT + tile
                            dve.wait_ge(qkv_done, g + 1)
                            dve.wait_ge(qk_ready, g)
                            x = PS[:, 3 * par:3 * par + 2, :].rearrange("p a (h d) -> p (a h) d", d=HD)
                            cos, sin = (const(c).rearrange("p (n d) -> p n d", d=HD)[:, bass.ds(tile, 1), :]
                                        .broadcast_to([P, 2 * HEADS, HD]) for c in ("cos", "sin"))
                            nc.vector.tensor_tensor(rot[:, 0, :, :], x, cos, ALU.mult).then_inc(cos_done, 1)
                            for a in range(2):
                                nc.vector.tensor_tensor(rot[:, 1, :, a::2], x[:, :, 1 - a::2], sin[:, :, a::2],
                                                        ALU.mult).then_inc(sin_done, 1)
                            dve.wait_ge(v_hi_ready, g + 1)
                            nc.vector.scalar_tensor_tensor(
                                V[:, bass.ds(tile, 1), :, 1, :],
                                PS[:, 3 * par + 2, :].rearrange("p (h d) -> p h d", h=HEADS), QKV_SCALE / PROD,
                                V[:, bass.ds(tile, 1), :, 0, :], ALU.mult, ALU.subtract).then_inc(v_lo_ready, 1)
                            dve.wait_ge(qk_lo, g + 1)
                            for heads_of, to, src in ((slice(0, HEADS), slice(2, 4), slice(0, 2)),
                                                      (slice(HEADS, 2 * HEADS), 2, 1), (slice(HEADS, 2 * HEADS), 3, 0)):
                                nc.vector.tensor_copy(qk16[:, heads_of, to, :],
                                                      qk16[:, heads_of, src, :]).then_inc(parts_copied, 1)
                            for quarter in range(2):
                                dve.wait_ge(qkT_done, 4 * g + quarter + 3)
                                nc.vector.tensor_copy(
                                    KT[:, quarter * 8:quarter * 8 + 8, bass.ds(tile * P, P)],
                                    PS[:, 7 - quarter, :].bitcast(fp16).rearrange("p (h n) -> p h n", h=8),
                                    ).then_inc(k_copied, 1)
                    heads(dve, lambda hh, hp, start, end: head(b, hh, hp, start, end))

            @block.gpsimd
            def _(pool):
                def bias_unit(H, i, first):
                    pool.wait_ge(max_done, H * BT + i + 1)
                    if not first:
                        pool.wait_ge(exp_done, H * BT + i - 1)
                    nc.gpsimd.tensor_tensor(bias[:, i % 2:i % 2 + 1], negmax[:, i % 2:i % 2 + 1],
                                            exp_scale[:, :], ALU.mult).then_inc(bias_done, 1)

                def head(b, hh, hp, start, end):
                    H = b * HEADS + hh
                    if start:
                        bias_unit(H, 0, True)
                    for i in range(BT):
                        if i + 1 < BT:
                            bias_unit(H, i + 1, start and i == 0)
                        elif not end:
                            bias_unit(H + 1, 0, False)
                    pool.wait_ge(half_done, 2 * (H + 1))
                    pool.sem_inc(tick, 1)
                    nc.gpsimd.tensor_tensor(O[:, :, bass.ds(hh * HD, HD)], half[:, 0, :, :], half[:, 1, :, :],
                                            ALU.add).then_inc(o_done, 1)

                pool.wait_ge(scale_set, 1)
                pool.wait_ge(mod_in, 16 * BATCH)
                with pool.Fori(0, BATCH) as b:
                    with pool.Fori(0, BT // 2) as m:
                        for par in range(2):
                            g = b * BT + m * 2 + par
                            pool.wait_ge(zm_ready, g + 1)
                            pool.wait_ge(hT_raw, g - par)
                            pool.sem_inc(tick, 1)
                            nc.gpsimd.tensor_tensor(h[:, par, :], zm[:, par, :], mod1[:, bass.ds(b, 1), 0, :],
                                                    ALU.add).then_inc(h_ready, 1)
                    with pool.Fori(0, BT) as n:
                        g = b * BT + n
                        pool.wait_ge(sin_done, 2 * (g + 1))
                        pool.wait_ge(qk_lo, g)
                        nc.gpsimd.tensor_tensor(qk[:, :, :], rot[:, 0, :, :], rot[:, 1, :, :],
                                                ALU.add).then_inc(qk_ready, 1)
                        pool.wait_ge(qk_hi, g + 1)
                        nc.gpsimd.tensor_tensor(qk16[:, :, 1, :], qk[:, :, :], qk16[:, :, 0, :],
                                                ALU.subtract).then_inc(qk_lo, 1)
                    pool.wait_ge(o_stored, b * 16)
                    heads(pool, lambda hh, hp, start, end: head(b, hh, hp, start, end))

        x1 = top.enter_context(nc.sbuf_tensor("x1", [P, TILES, DIM], fp32))
        with ExitStack() as st:
            def sb(name, shape, dt):
                return st.enter_context(nc.sbuf_tensor(name, shape, dt))

            wo = sb("wo", [P, KC, DIM], fp32)
            wo_hi = sb("wo_hi", [P, KC, DIM], fp16)
            wo_lo = sb("wo_lo", [P, KC, DIM], fp16)
            gate1 = sb("gate1", [P, BATCH, DIM], fp32)
            oin = sb("oin", [P, 2, DIM], fp32)
            xres = sb("xres", [P, 2, DIM], fp32)
            oT_hi = sb("oT_hi", [P, 2, KC, P], fp16)
            oT_lo = sb("oT_lo", [P, 2, KC, P], fp16)
            gated = sb("gated", [P, 2, DIM], fp32)
            raw6 = sb("raw6b", [P, TILES, 6], fp32)
            small = sb("smallb", [P, 8, TILES], fp32)
            (wo_loaded, gate1_loaded, oin_a, oin_b, xres_a, xres_b, wo_hi_ready, wo_lo_ready, oT_raw, oT_hi_ready,
             oT_lo_ready, out_done, gated_ready, x1_ready, stats, step, root) = sems(
                st, "wo_loaded gate1_loaded oin_a oin_b xres_a xres_b wo_hi_ready wo_lo_ready oT_raw oT_hi_ready "
                    "oT_lo_ready out_done gated_ready x1_ready stats3 step3 root3")
            oin_loaded, xres_loaded = (oin_a, oin_b), (xres_a, xres_b)
            block = st.enter_context(nc.Block())

            @block.sync
            def _(sp):
                sp.dma_start(wo[:, :, :], t["wo"]).then_inc(wo_loaded, 16)

                def load(g, par):
                    wait(sp, oT_raw, g - 1)
                    sp.dma_start(oin[:, par, :], attn_d[bass.ds(g * P, P), :]).then_inc(oin_loaded[par], 16)
                    wait(sp, x1_ready, g - 1)
                    sp.dma_start(xres[:, par, :], t["x"][bass.ds(g * P, P), :]).then_inc(xres_loaded[par], 16)

                pairs(sp, TILES, lambda g, par, first, last: load(g, par))

            @block.scalar
            def _(act):
                for b in range(BATCH):
                    act.dma_start(gate1[:, b, :], mod_d[b:b + 1, 2 * DIM:3 * DIM].partition_broadcast(P)
                                  .rearrange("p a d -> p (a d)")).then_inc(gate1_loaded, 16)
                act.wait_ge(wo_loaded, 16)
                nc.scalar.activation(wo_hi[:, :, :], wo[:, :, :], ACT.Copy, scale=W_SCALE).then_inc(wo_hi_ready, 1)

                def part(g, par):
                    act.wait_ge(oT_raw, g + 1)
                    wait(act, out_done, g - 1)
                    nc.scalar.activation(oT_hi[:, par, :, :].rearrange("p k n -> p (k n)"), PS[:, par, :], ACT.Copy,
                                         scale=ACT_SCALE).then_inc(oT_hi_ready, 1)

                pairs(act, TILES, lambda g, par, first, last: part(g, par))
                act.wait_ge(step, 7)
                nc.scalar.activation(small[:, 4, :], small[:, 3, :], ACT.Sqrt).then_inc(root, 1)

            @block.tensor
            def _(pe):
                def turn(g, par):
                    pe.wait_ge(oin_loaded[par], loads(g, par))
                    wait(pe, oT_lo_ready, g - 1)
                    for k in range(KC):
                        last = nc.tensor.transpose(PS[:, par, k * P:(k + 1) * P], oin[:, par, k * P:(k + 1) * P],
                                                   ident32)
                    last.then_inc(oT_raw, 1)

                def project(g, par):
                    pe.wait_ge(oT_lo_ready, g + 1)
                    wait(pe, gated_ready, g - 1)
                    for k in range(KC):
                        for m, (l, r) in enumerate(((oT_hi, wo_hi), (oT_hi, wo_lo), (oT_lo, wo_hi))):
                            last = nc.tensor.matmul(PS[:, 2 + par, :], l[:, par, k, :], r[:, k, :],
                                                    start=k == 0 and m == 0, stop=k == KC - 1 and m == 2)
                    last.then_inc(out_done, 1)

                def both(g, par, first, last):
                    if first:
                        turn(g, par)
                    if not last:
                        turn(g + 1, 1 - par)
                    project(g, par)

                pe.wait_ge(wo_lo_ready, 1)
                pairs(pe, TILES, both)

            @block.vector
            def _(dve):
                dve.wait_ge(wo_hi_ready, 1)
                nc.vector.scalar_tensor_tensor(wo_lo[:, :, :].rearrange("p k d -> p (k d)"),
                                               wo[:, :, :].rearrange("p k d -> p (k d)"), W_SCALE,
                                               wo_hi[:, :, :].rearrange("p k d -> p (k d)"),
                                               ALU.mult, ALU.subtract).then_inc(wo_lo_ready, 1)
                dve.wait_ge(gate1_loaded, 16 * BATCH)

                def part(g, par):
                    dve.wait_ge(oT_hi_ready, g + 1)
                    nc.vector.scalar_tensor_tensor(oT_lo[:, par, :, :].rearrange("p k n -> p (k n)"), PS[:, par, :],
                                                   ACT_SCALE, oT_hi[:, par, :, :].rearrange("p k n -> p (k n)"),
                                                   ALU.mult, ALU.subtract).then_inc(oT_lo_ready, 1)

                def both(g, par, first, last, b):
                    if first and b == 0:
                        part(g, par)
                    if not (last and b == BATCH - 1):
                        part(g + 1, 1 - par)
                    dve.wait_ge(out_done, g + 1)
                    wait(dve, x1_ready, g - 1)
                    nc.vector.scalar_tensor_tensor(gated[:, par, :], PS[:, 2 + par, :], 1.0 / PROD, gate1[:, b, :],
                                                   ALU.mult, ALU.mult).then_inc(gated_ready, 1)
                    if not (first and b == 0):
                        dve.wait_ge(x1_ready, g)
                        nc.vector.bn_stats(raw6[:, bass.ds(g - 1, 1), :], x1[:, bass.ds(g - 1, 1), :]
                                           ).then_inc(stats, 1)

                for b in range(BATCH):
                    pairs(dve, BT, lambda g, par, first, last: both(g, par, first, last, b), b * BT)
                dve.wait_ge(x1_ready, TILES)
                nc.vector.bn_stats(raw6[:, TILES - 1, :], x1[:, TILES - 1, :]).then_inc(stats, 1)
                dve.wait_ge(stats, TILES)
                deviation(dve, raw6, small, stat2, step, root)

            @block.gpsimd
            def _(pool):
                def add(g, par):
                    pool.wait_ge(xres_loaded[par], loads(g, par))
                    pool.wait_ge(gated_ready, g + 1)
                    pool.sem_inc(tick, 1)
                    nc.gpsimd.tensor_tensor(x1[:, bass.ds(g, 1), :], gated[:, par, :], xres[:, par, :],
                                            ALU.add).then_inc(x1_ready, 1)

                pairs(pool, TILES, lambda g, par, first, last: add(g, par))

        h2_d = nc.dram_tensor("h2_d", [TOK + CAP, DIM], fp32).ap()
        y_d = nc.dram_tensor("y_d", [TOK + CAP, DIM], fp32).ap()
        slots_d = nc.dram_tensor("slots_d", [EXPERTS * CAP, 2], i32).ap()
        with ExitStack() as st:
            def sb(name, shape, dt):
                return st.enter_context(nc.sbuf_tensor(name, shape, dt))

            SHP = SCH * P
            h2T_hi = sb("h2T_hi", [P, KC, TOK], fp16)
            h2T_lo = sb("h2T_lo", [P, KC, TOK], fp16)
            sg_w = [sb("sgw" + c, [P, KC, SHP], fp16) for c in ("_hi", "_lo")]
            su_w = [sb("suw" + c, [P, KC, SHP], fp16) for c in ("_hi", "_lo")]
            sd_w = [sb("sdw" + c, [P, SCH, DIM], fp16) for c in ("_hi", "_lo")]
            gt_w = [sb("gtw" + c, [P, KC, EXPERTS], fp16) for c in ("_hi", "_lo")]
            stage = sb("stage", [P, 2, SHP], fp32)
            mod2 = sb("mod2", [P, BATCH, 2, DIM], fp32)
            zeros = sb("zeros", [P, DIM], fp32)
            z = sb("z2", [P, 2, DIM], fp32)
            h2 = sb("h2", [P, 2, DIM], fp32)
            logits = sb("logits", [P, TILES, EXPERTS], fp32)
            top8 = sb("top8", [P, TILES, 8], fp32)
            top8i = sb("top8i", [P, TILES, 8], u32)
            idx = sb("idx", [P, TILES, 8], fp32)
            e8 = sb("e8", [P, TILES, 8], fp32)
            ez = sb("ez", [P, TILES, EXPERTS], fp32)
            sums = sb("sums", [P, 4, TILES], fp32)
            onehot = sb("onehot", [P, TILES, TOPK, EXPERTS], bf16)
            mask = sb("mask", [P, TILES, EXPERTS], bf16)
            total = sb("total", [P, EXPERTS, TILES], fp32)
            keep = sb("keep", [P, EXPERTS, TILES], fp32)
            cum = sb("cum", [P, EXPERTS, TILES], fp32)
            pos, row = ez, logits
            term = sb("term", [P, TILES, EXPERTS], fp32)
            rowk = sb("rowk", [P, TILES, TOPK], fp32)
            row_i = sb("row_i", [P, TILES * TOPK], i32)
            pair = sb("pair", [P, TILES, TOPK, 2], i32)
            silu = sb("silu", [P, 2, GT * P], fp32)
            hf = sb("hf", [P, 2, GT * P], fp32)
            hs_hi = sb("hs_hi", [P, SCH, GT * P], fp16)
            hs_lo = sb("hs_lo", [P, SCH, GT * P], fp16)
            ysh = sb("ysh", [P, 2, DIM], fp32)
            WEIGHTS = ([("sh_gate", sg_w, k, SHP) for k in range(KC)] + [("sh_up", su_w, k, SHP) for k in range(KC)]
                       + [("sh_down", sd_w, k, DIM) for k in range(SCH)]
                       + [("gate", gt_w, k, EXPERTS) for k in range(KC)])
            WEIGHTS = WEIGHTS[-KC:] + WEIGHTS[:-KC]
            (mod2_loaded, st_a, st_b, w_hi, w_lo, slots_set, pad_stored, zero_set, z_ready, zm_ready, h2_ready, h2s_a,
             h2s_b, hT_raw, hT_hi_r, hT_lo_r, logit_done, logit_ready, rt, shifted, mask_r, pos_read, exp_r, count_done, pairs_ready, scattered,
             gu_done, silu_r, hf_r, hs_hi_r, hs_lo_r, dn_done, y_r, ys_a, ys_b) = sems(
                st, "mod2_loaded st_a st_b w_hi w_lo slots_set pad_stored zero_set z_ready4 zm_ready4 h2_ready h2s_a "
                    "h2s_b hT_raw4 hT_hi_r hT_lo_r logit_done logit_ready rt shifted mask_r pos_read exp_r count_done pairs_ready scattered "
                    "gu_done silu_r hf_r hs_hi_r hs_lo_r dn_done y_r ys_a ys_b")
            staged, h2_stored, y_stored = (st_a, st_b), (h2s_a, h2s_b), (ys_a, ys_b)
            GROUP = TILES // GT
            block = st.enter_context(nc.Block())

            @block.sync
            def _(sp):
                sp.dma_start(slots_d, t["slots"]).then_inc(slots_set, 16)
                for n, (name, _, k, width) in enumerate(WEIGHTS):
                    wait(sp, w_lo, n - 1)
                    sp.dma_start(stage[:, n % 2, 0:width], t[name][:, k, :]).then_inc(staged[n % 2], 16)
                sp.wait_ge(zero_set, 1)
                for n in range(SLOT_TILES):
                    for d in (h2_d, y_d):
                        sp.dma_start(d[TOK + n * P:TOK + (n + 1) * P, :], zeros[:, :]).then_inc(pad_stored, 16)

                def store_h2(g, par):
                    sp.wait_ge(h2_ready, g + 1)
                    sp.dma_start(h2_d[bass.ds(g * P, P), :], h2[:, par, :]).then_inc(h2_stored[par], 16)

                def store_y(g, par):
                    sp.wait_ge(y_r, g + 1)
                    sp.dma_start(y_d[bass.ds(g * P, P), :], ysh[:, par, :]).then_inc(y_stored[par], 16)

                pairs(sp, TILES, lambda g, par, first, last: store_h2(g, par))
                pairs(sp, TILES, lambda g, par, first, last: store_y(g, par))
                sp.wait_ge(pad_stored, 16 * 2 * SLOT_TILES)
                for par in range(2):
                    sp.wait_ge(h2_stored[par], 16 * TILES // 2)
                    sp.wait_ge(y_stored[par], 16 * TILES // 2)

            @block.scalar
            def _(act):
                for b in range(BATCH):
                    act.dma_start(mod2[:, b, :, :].rearrange("p s d -> p (s d)"),
                                  mod_d[b:b + 1, 3 * DIM:5 * DIM].partition_broadcast(P)
                                  .rearrange("p a d -> p (a d)")).then_inc(mod2_loaded, 16)
                for n, (_, parts, k, width) in enumerate(WEIGHTS):
                    act.wait_ge(staged[n % 2], 16 * (n // 2 + 1))
                    nc.scalar.activation(parts[0][:, k, :], stage[:, n % 2, 0:width], ACT.Copy,
                                         scale=W_SCALE).then_inc(w_hi, 1)

                def part(g, par):
                    act.wait_ge(hT_raw, g + 1)
                    nc.scalar.activation(h2T_hi[:, :, bass.ds(g * P, P)],
                                         PS[:, par, :].rearrange("p (k n) -> p k n", k=KC), ACT.Copy,
                                         scale=ACT_SCALE).then_inc(hT_hi_r, 1)

                pairs(act, TILES, lambda g, par, first, last: part(g, par))
                act.wait_ge(shifted, 2)
                nc.scalar.activation(ez[:, :, :], ez[:, :, :], ACT.Exp).then_inc(exp_r, 1)
                nc.scalar.activation(e8[:, :, :], e8[:, :, :], ACT.Exp).then_inc(exp_r, 1)

                def shared(q):
                    for j in range(SCH):
                        n = q * SCH + j
                        act.wait_ge(gu_done, n + 1)
                        wait(act, hf_r, n - 1)
                        nc.scalar.activation(silu[:, j % 2, :], PS[:, 2 * (j % 2), :], ACT.Silu,
                                             scale=1.0 / PROD).then_inc(silu_r, 1)
                        act.wait_ge(hf_r, n + 1)
                        wait(act, dn_done, q * GT)
                        nc.scalar.activation(hs_hi[:, j, :], hf[:, j % 2, :], ACT.Copy).then_inc(hs_hi_r, 1)
                    for c in range(GT):
                        g = q * GT + c
                        act.wait_ge(dn_done, g + 1)
                        wait(act, y_stored[c % 2], (g - c % 2) * 8)
                        nc.scalar.activation(ysh[:, c % 2, :], PS[:, 4 + c % 2, :], ACT.Copy,
                                             scale=1.0 / (H_SCALE * W_SCALE)).then_inc(y_r, 1)

                peeled(act, GROUP, shared)

            @block.tensor
            def _(pe):
                def turn(g, par):
                    pe.wait_ge(h2_ready, g + 1)
                    wait(pe, hT_lo_r, g - 1)
                    for k in range(KC):
                        last = nc.tensor.transpose(PS[:, par, k * P:(k + 1) * P], h2[:, par, k * P:(k + 1) * P],
                                                   ident32)
                    last.then_inc(hT_raw, 1)

                def route(g, par):
                    pe.wait_ge(hT_lo_r, g + 1)
                    wait(pe, logit_ready, g - 1)
                    for k in range(KC):
                        for m, (l, r) in enumerate(((h2T_hi, gt_w[0]), (h2T_hi, gt_w[1]), (h2T_lo, gt_w[0]))):
                            last = nc.tensor.matmul(PS[:, 2 + par, 0:EXPERTS], l[:, k, bass.ds(g * P, P)], r[:, k, :],
                                                    start=k == 0 and m == 0, stop=k == KC - 1 and m == 2)
                    last.then_inc(logit_done, 1)

                def both(g, par, first, last):
                    if first:
                        turn(g, par)
                    if not last:
                        turn(g + 1, 1 - par)
                    route(g, par)

                pe.wait_ge(w_lo, len(WEIGHTS))
                pairs(pe, TILES, both)
                pe.wait_ge(mask_r, 1)
                flat = mask[:, :, :].rearrange("p n e -> p (n e)")
                for m, bank in ((cb[:, 2, :], 4), (cb[:, 3, :], 6)):
                    for half_ in range(2):
                        nc.tensor.matmul(PS[:, bank + half_, :], m, flat[:, half_ * BANK:(half_ + 1) * BANK],
                                         start=True, stop=True).then_inc(count_done, 1)

                def shared(q):
                    for j in range(SCH):
                        n = q * SCH + j
                        wait(pe, hf_r, n - 1)
                        for bank, w in enumerate((sg_w, su_w)):
                            for k in range(KC):
                                cols = slice(j * P, (j + 1) * P)
                                toks = bass.ds(q * GT * P, GT * P)
                                for m, (l, r) in enumerate(((w[0], h2T_hi), (w[0], h2T_lo), (w[1], h2T_hi))):
                                    last = nc.tensor.matmul(PS[:, 2 * (j % 2) + bank, :], l[:, k, cols],
                                                            r[:, k, toks], start=k == 0 and m == 0,
                                                            stop=k == KC - 1 and m == 2)
                        last.then_inc(gu_done, 1)
                    pe.wait_ge(hs_lo_r, (q + 1) * SCH)
                    pe.wait_ge(pos_read, 1)
                    for c in range(GT):
                        wait(pe, y_r, q * GT + c - 1)
                        for j in range(SCH):
                            for m, (l, r) in enumerate(((hs_hi, sd_w[0]), (hs_hi, sd_w[1]), (hs_lo, sd_w[0]))):
                                last = nc.tensor.matmul(PS[:, 4 + c % 2, :], l[:, j, c * P:(c + 1) * P], r[:, j, :],
                                                        start=j == 0 and m == 0, stop=j == SCH - 1 and m == 2)
                        last.then_inc(dn_done, 1)

                peeled(pe, GROUP, shared)

            @block.vector
            def _(dve):
                nc.vector.memset(zeros[:, :], 0.0).then_inc(zero_set, 1)
                for n, (_, parts, k, width) in enumerate(WEIGHTS):
                    dve.wait_ge(w_hi, n + 1)
                    nc.vector.scalar_tensor_tensor(parts[1][:, k, :], stage[:, n % 2, 0:width], W_SCALE,
                                                   parts[0][:, k, :], ALU.mult, ALU.subtract).then_inc(w_lo, 1)
                dve.wait_ge(mod2_loaded, 16 * BATCH)

                def normed(g, par, b):
                    wait(dve, h2_ready, g - 1)
                    nc.vector.tensor_scalar(z[:, par, :], x1[:, bass.ds(g, 1), :].rearrange("p a d -> p (a d)"),
                                            stat2[:, bass.ds(g, 1), 0], stat2[:, bass.ds(g, 1), 1],
                                            ALU.subtract, ALU.mult).then_inc(z_ready, 1)
                    dve.wait_ge(z_ready, g + 1)
                    nc.vector.tensor_tensor(z[:, par, :], z[:, par, :], mod2[:, b, 1, :], ALU.mult).then_inc(zm_ready, 1)

                def part(g, par, first):
                    dve.wait_ge(hT_hi_r, g + 1)
                    nc.vector.scalar_tensor_tensor(
                        h2T_lo[:, :, bass.ds(g * P, P)], PS[:, par, :].rearrange("p (k n) -> p k n", k=KC), ACT_SCALE,
                        h2T_hi[:, :, bass.ds(g * P, P)], ALU.mult, ALU.subtract).then_inc(hT_lo_r, 1)
                    if not first:
                        keep_logits(g - 1, 1 - par)

                def keep_logits(g, par):
                    dve.wait_ge(logit_done, g + 1)
                    nc.vector.tensor_scalar(logits[:, bass.ds(g, 1), :].rearrange("p a e -> p (a e)"),
                                            PS[:, 2 + par, 0:EXPERTS], 1.0 / PROD, None,
                                            ALU.mult).then_inc(logit_ready, 1)

                def both(g, par, first, last, b):
                    if first and b == 0:
                        normed(g, par, b)
                    if not last:
                        normed(g + 1, 1 - par, b)
                    elif b < BATCH - 1:
                        normed(g + 1, 1 - par, b + 1)
                    part(g, par, first and b == 0)

                for b in range(BATCH):
                    pairs(dve, BT, lambda g, par, first, last: both(g, par, first, last, b), b * BT)
                keep_logits(TILES - 1, 1)
                dve.wait_ge(logit_ready, TILES)

                linked = [0]

                def link(ins):
                    linked[0] += 1
                    ins.then_inc(rt, 1)
                    dve.wait_ge(rt, linked[0])

                for g in range(TILES):
                    link(nc.vector.max(top8[:, g, :], logits[:, g, :]))
                for g in range(TILES):
                    link(nc.vector.max_index(top8i[:, g, :], top8[:, g, :], logits[:, g, :]))
                best = top8[:, :, 0:1]
                nc.vector.tensor_tensor(ez[:, :, :], logits[:, :, :], best.broadcast_to([P, TILES, EXPERTS]),
                                        ALU.subtract).then_inc(shifted, 1)
                nc.vector.tensor_tensor(e8[:, :, :], top8[:, :, :], best.broadcast_to([P, TILES, 8]),
                                        ALU.subtract).then_inc(shifted, 1)
                link(nc.vector.tensor_copy(idx[:, :, :], top8i[:, :, :]))
                kshape = [P, TILES, TOPK, EXPERTS]
                iota = const("iota").unsqueeze(1).unsqueeze(1).broadcast_to(kshape)
                chosen = idx[:, :, 0:TOPK].unsqueeze(3).broadcast_to(kshape)
                link(nc.vector.tensor_tensor(onehot[:, :, :, :], iota, chosen, ALU.is_equal))
                nc.vector.tensor_reduce(mask[:, :, :], onehot[:, :, :, :].rearrange("p n k e -> p n e k"), AX.X,
                                        ALU.max).then_inc(mask_r, 1)
                dve.wait_ge(exp_r, 2)
                link(nc.vector.tensor_reduce(sums[:, 0, :], ez[:, :, :], AX.X, ALU.add))
                link(nc.vector.reciprocal(sums[:, 1, :], sums[:, 0, :]))
                link(nc.vector.tensor_tensor(e8[:, :, :], e8[:, :, :],
                                             sums[:, 1, :].unsqueeze(2).broadcast_to([P, TILES, 8]), ALU.mult))
                link(nc.vector.tensor_reduce(sums[:, 2, :], e8[:, :, 0:TOPK], AX.X, ALU.add))
                link(nc.vector.tensor_scalar(sums[:, 2, :], sums[:, 2, :], 1e-20, None, ALU.add))
                link(nc.vector.reciprocal(sums[:, 3, :], sums[:, 2, :]))
                link(nc.vector.scalar_tensor_tensor(
                    pair[:, :, :, 1].bitcast(fp32), e8[:, :, 0:TOPK], 1.0 / (H_SCALE * W_SCALE),
                    sums[:, 3, :].unsqueeze(2).broadcast_to([P, TILES, TOPK]), ALU.mult, ALU.mult))
                link(nc.vector.tensor_copy(pair[:, :, :, 0],
                                           const("token").unsqueeze(2).broadcast_to([P, TILES, TOPK])))
                link(nc.vector.memset(keep[:, :, :], 1.0))
                link(nc.vector.memset(keep[:, :, 0:1], 0.0))
                dve.wait_ge(count_done, 4)
                link(nc.vector.tensor_copy(total[:, :, :], PS[:, 6:8, :].rearrange("p a (n e) -> p e (a n)", e=EXPERTS)))
                flat = "p e n -> p (e n)"
                link(nc.vector.tensor_tensor_scan(cum[:, :, :].rearrange(flat), keep[:, :, :].rearrange(flat),
                                                  total[:, :, :].rearrange(flat), 0.0, ALU.mult, ALU.add))
                link(nc.vector.tensor_tensor(cum[:, :, :], cum[:, :, :], total[:, :, :], ALU.subtract))
                nc.vector.tensor_tensor(pos[:, :, :], PS[:, 4:6, :].rearrange("p a (n e) -> p (a n) e", e=EXPERTS),
                                        cum[:, :, :].rearrange("p e n -> p n e"), ALU.add).then_inc(pos_read, 1)
                dve.wait_ge(pos_read, 1)
                step_back = float(1 - SLOT_TILES * P)
                link(nc.vector.scalar_tensor_tensor(row[:, :, :], pos[:, :, :], float(SLOT_TILES),
                                                    const("slot0").unsqueeze(1).broadcast_to([P, TILES, EXPERTS]),
                                                    ALU.mult, ALU.add))
                for edge, value in ((P, step_back), (2 * P, step_back), (CAP, DROPPED)):
                    link(nc.vector.tensor_scalar(term[:, :, :], pos[:, :, :], float(edge), value, ALU.is_ge,
                                                 ALU.mult))
                    link(nc.vector.tensor_tensor(row[:, :, :], row[:, :, :], term[:, :, :], ALU.add))
                for k in range(TOPK):
                    link(nc.vector.tensor_tensor(term[:, :, :], onehot[:, :, k, :], row[:, :, :], ALU.mult))
                    link(nc.vector.tensor_reduce(rowk[:, :, k], term[:, :, :], AX.X, ALU.add))
                nc.vector.tensor_copy(row_i[:, :], rowk[:, :, :].rearrange("p n k -> p (n k)")).then_inc(pairs_ready, 1)

                def shared(q):
                    for j in range(SCH):
                        n = q * SCH + j
                        dve.wait_ge(silu_r, n + 1)
                        wait(dve, hs_lo_r, n - 1)
                        nc.vector.scalar_tensor_tensor(hf[:, j % 2, :], PS[:, 2 * (j % 2) + 1, :], H_SCALE / PROD,
                                                       silu[:, j % 2, :], ALU.mult, ALU.mult).then_inc(hf_r, 1)
                        dve.wait_ge(hs_hi_r, n + 1)
                        nc.vector.tensor_tensor(hs_lo[:, j, :], hf[:, j % 2, :], hs_hi[:, j, :],
                                                ALU.subtract).then_inc(hs_lo_r, 1)

                peeled(dve, GROUP, shared)

            @block.gpsimd
            def _(pool):
                pool.wait_ge(mod2_loaded, 16 * BATCH)

                def shift(g, par, b):
                    pool.wait_ge(zm_ready, g + 1)
                    wait(pool, hT_raw, g - 1)
                    if not isinstance(g, int) or g >= 2:
                        pool.wait_ge(h2_stored[par], (g - par) * 8)
                    nc.gpsimd.tensor_tensor(h2[:, par, :], z[:, par, :], mod2[:, b, 0, :], ALU.add).then_inc(h2_ready, 1)

                for b in range(BATCH):
                    pairs(pool, BT, lambda g, par, first, last: shift(g, par, b), b * BT)
                pool.wait_ge(slots_set, 16)
                pool.wait_ge(pairs_ready, 1)
                for n in range(TILES * TOPK):
                    nc.gpsimd.indirect_dma_start(
                        out=slots_d, out_offset=bass.IndirectOffsetOnAxis(ap=row_i[:, n:n + 1], axis=0),
                        in_=pair[:, n // TOPK, n % TOPK, :], in_offset=None, bounds_check=EXPERTS * CAP - 1,
                        oob_is_err=False).then_inc(scattered, 16)
                pool.wait_ge(scattered, 16 * TILES * TOPK)

        with ExitStack() as st:
            def sb(name, shape, dt):
                return st.enter_context(nc.sbuf_tensor(name, shape, dt))

            raw_up = sb("raw_up", [P, 2, KC, 2 * FF], fp32)
            raw_dn = sb("raw_dn", [P, 2, FCH, DIM], fp32)
            up_hi = sb("up_hi", [P, 2, KC, 2 * FF], fp16)
            up_lo = sb("up_lo", [P, 2, KC, 2 * FF], fp16)
            dn_hi = sb("dn_hi", [P, 2, FCH, DIM], fp16)
            dn_lo = sb("dn_lo", [P, 2, FCH, DIM], fp16)
            slot_in = sb("slot_in", [P, 2, SLOT_TILES, 2], i32)
            slot_out = sb("slot_out", [P, 2, SLOT_TILES, 2], i32)
            xg = sb("xg", [P, 2, SLOT_TILES, DIM], fp32)
            xT_hi = sb("xT_hi", [P, 2, KC, CAP], fp16)
            xT_lo = sb("xT_lo", [P, 2, KC, CAP], fp16)
            silu = sb("silu5", [P, 2, CAP], fp32)
            hf = sb("hf5", [P, 2, CAP], fp32)
            h_hi = sb("h_hi", [P, 2, FCH, CAP], fp16)
            h_lo = sb("h_lo", [P, 2, FCH, CAP], fp16)
            y = sb("y", [P, 2, SLOT_TILES, DIM], fp32)
            WIDTH = [min(P, FF - j * P) for j in range(FCH)]
            (si_a, si_b, so_a, so_b, ru_a, ru_b, rd_a, rd_b, xg_a, xg_b, add_a, add_b, turned, x_hi_r, x_lo_r, up_hi_r,
             up_lo_r, dn_hi_r, dn_lo_r, gu_done, silu_r, hf_r, h_hi_r, h_lo_r, dn_done, y_r) = sems(
                st, "si_a si_b so_a so_b ru_a ru_b rd_a rd_b xg_a xg_b add_a add_b turned x_hi_r x_lo_r up_hi_r "
                    "up_lo_r dn_hi_r dn_lo_r gu_done5 silu_r5 hf_r5 h_hi_r h_lo_r dn_done5 y_r5")
            si_loaded, so_loaded, up_loaded, dn_loaded = (si_a, si_b), (so_a, so_b), (ru_a, ru_b), (rd_a, rd_b)
            gathered, added = (xg_a, xg_b), (add_a, add_b)
            part_of = "(p c) w -> p (c w)"
            block = st.enter_context(nc.Block())

            def table(e):
                return slots_d[bass.ds(e * CAP, CAP), :].rearrange(part_of, p=P)

            def experts_w(e, lo, hi):
                return t["experts"][bass.ds(e, 1), :, lo:hi].rearrange("a p n -> (a p) n")

            @block.sync
            def _(sp):
                def out_rows(e, par):
                    wait(sp, added[par], (e - par) * 24)
                    sp.dma_start(slot_out[:, par, :, :].rearrange("p c w -> p (c w)"),
                                 table(e)).then_inc(so_loaded[par], 16)

                def load(e, par, first, last):
                    wait(sp, gathered[par], (e - par) * 24)
                    sp.dma_start(slot_in[:, par, :, :].rearrange("p c w -> p (c w)"),
                                 table(e)).then_inc(si_loaded[par], 16)
                    wait(sp, up_lo_r, (e - 1) * KC)
                    sp.dma_start(raw_up[:, par, :, :].rearrange("p k n -> p (k n)"),
                                 experts_w(e, 0, UP)).then_inc(up_loaded[par], 16)
                    wait(sp, dn_lo_r, e - 1)
                    sp.dma_start(raw_dn[:, par, :, :].rearrange("p k n -> p (k n)"),
                                 experts_w(e, UP, UP + DOWN)).then_inc(dn_loaded[par], 16)
                    if not first:
                        out_rows(e - 1, 1 - par)
                    if last:
                        out_rows(e, par)

                pairs(sp, EXPERTS, load)

            @block.gpsimd
            def _(pool):
                def gather(e, par):
                    pool.wait_ge(si_loaded[par], loads(e, par))
                    wait(pool, turned, (e - 1) * SLOT_TILES)
                    pool.sem_inc(tick, 1)
                    for c in range(SLOT_TILES):
                        nc.gpsimd.indirect_dma_start(
                            out=xg[:, par, c, :], out_offset=None, in_=h2_d,
                            in_offset=bass.IndirectOffsetOnAxis(ap=slot_in[:, par, c, 0:1], axis=0)
                        ).then_inc(gathered[par], 16)

                def low_parts(e, par):
                    for j in range(FCH):
                        n, w = e * FCH + j, WIDTH[j]
                        pool.wait_ge(h_hi_r, n + 1)
                        nc.gpsimd.tensor_tensor(h_lo[0:w, par, j, :], hf[0:w, (par * FCH + j) % 2, :],
                                                h_hi[0:w, par, j, :], ALU.subtract).then_inc(h_lo_r, 1)

                def add(e, par):
                    pool.wait_ge(y_r, (e + 1) * SLOT_TILES)
                    wait(pool, added[1 - par], (e - par) * 24 if par == 0 else (e - par) * 24 + 48)
                    pool.sem_inc(tick, 1)
                    for c in range(SLOT_TILES):
                        nc.gpsimd.indirect_dma_start(
                            out=y_d, out_offset=bass.IndirectOffsetOnAxis(ap=slot_out[:, par, c, 0:1], axis=0),
                            in_=y[:, par, c, :], in_offset=None, compute_op=ALU.add,
                            bounds_check=TOK + CAP - 1, oob_is_err=True).then_inc(added[par], 16)

                def turn(e, par, first, last):
                    if first:
                        gather(e, par)
                    if not last:
                        gather(e + 1, 1 - par)
                    low_parts(e, par)
                    if not first:
                        add(e - 1, 1 - par)

                pairs(pool, EXPERTS, turn)
                add(EXPERTS - 1, 1)
                for par in range(2):
                    pool.wait_ge(added[par], 24 * EXPERTS)

            @block.tensor
            def _(pe):
                def transpose_x(e, par):
                    pe.wait_ge(gathered[par], (e - par) * 24 + 48)
                    for c in range(SLOT_TILES):
                        wait(pe, x_lo_r, e * SLOT_TILES + (1 if c == 2 else 0))
                        for k in range(KC):
                            last = nc.tensor.transpose(PS[:, 6 + c % 2, k * P:(k + 1) * P],
                                                       xg[:, par, c, k * P:(k + 1) * P], ident32)
                        last.then_inc(turned, 1)

                def up(e, par):
                    pe.wait_ge(x_lo_r, (e + 1) * SLOT_TILES)
                    pe.wait_ge(up_lo_r, (e + 1) * KC)
                    for j in range(FCH):
                        n, w, at = e * FCH + j, WIDTH[j], 2 * ((par * FCH + j) % 2)
                        wait(pe, hf_r, n - 1)
                        for side in range(2):
                            cols = slice(side * FF + j * P, side * FF + j * P + w)
                            for k in range(KC):
                                for m, (l, r) in enumerate(((up_hi, xT_hi), (up_hi, xT_lo), (up_lo, xT_hi))):
                                    last = nc.tensor.matmul(PS[0:w, at + side, 0:CAP], l[:, par, k, cols],
                                                            r[:, par, k, :], start=k == 0 and m == 0,
                                                            stop=k == KC - 1 and m == 2)
                        last.then_inc(gu_done, 1)

                def down(e, par):
                    pe.wait_ge(h_lo_r, (e + 1) * FCH)
                    pe.wait_ge(dn_lo_r, e + 1)
                    for c in range(SLOT_TILES):
                        wait(pe, y_r, e * SLOT_TILES + c - 1)
                        for j in range(FCH):
                            w = WIDTH[j]
                            for m, (l, r) in enumerate(((h_hi, dn_hi), (h_hi, dn_lo), (h_lo, dn_hi))):
                                last = nc.tensor.matmul(PS[:, 4 + (par * SLOT_TILES + c) % 2, :],
                                                        l[0:w, par, j, c * P:(c + 1) * P], r[0:w, par, j, :],
                                                        start=j == 0 and m == 0, stop=j == FCH - 1 and m == 2)
                        last.then_inc(dn_done, 1)

                def turn(e, par, first, last):
                    if first:
                        transpose_x(e, par)
                    if not last:
                        transpose_x(e + 1, 1 - par)
                    up(e, par)
                    if not first:
                        down(e - 1, 1 - par)

                pairs(pe, EXPERTS, turn)
                down(EXPERTS - 1, 1)

            @block.scalar
            def _(act):
                def x_part(e, par):
                    for c in range(SLOT_TILES):
                        act.wait_ge(turned, e * SLOT_TILES + c + 1)
                        nc.scalar.activation(xT_hi[:, par, :, c * P:(c + 1) * P],
                                             PS[:, 6 + c % 2, :].rearrange("p (k n) -> p k n", k=KC), ACT.Copy,
                                             scale=ACT_SCALE).then_inc(x_hi_r, 1)

                def up_part(e, par, ks):
                    act.wait_ge(up_loaded[par], loads(e, par))
                    for k in ks:
                        nc.scalar.activation(up_hi[:, par, k, :], raw_up[:, par, k, :], ACT.Copy,
                                             scale=W_SCALE).then_inc(up_hi_r, 1)

                def gate(e, par, j):
                    n, w, at = e * FCH + j, WIDTH[j], 2 * ((par * FCH + j) % 2)
                    act.wait_ge(gu_done, n + 1)
                    wait(act, hf_r, n - 1)
                    nc.scalar.activation(silu[0:w, (par * FCH + j) % 2, :], PS[0:w, at, 0:CAP], ACT.Silu,
                                         scale=1.0 / PROD).then_inc(silu_r, 1)

                def h_part(e, par, j):
                    n, w = e * FCH + j, WIDTH[j]
                    act.wait_ge(hf_r, n + 1)
                    nc.scalar.activation(h_hi[0:w, par, j, :], hf[0:w, (par * FCH + j) % 2, :],
                                         ACT.Copy).then_inc(h_hi_r, 1)

                def weigh(e, par):
                    act.wait_ge(so_loaded[par], loads(e, par))
                    for c in range(SLOT_TILES):
                        act.wait_ge(dn_done, e * SLOT_TILES + c + 1)
                        if c == 0:
                            wait(act, added[par], (e - par) * 24)
                        nc.scalar.activation(y[:, par, c, :], PS[:, 4 + (par * SLOT_TILES + c) % 2, :], ACT.Copy,
                                             scale=slot_out[:, par, c, 1:2].bitcast(fp32)).then_inc(y_r, 1)

                def dn_part(e, par):
                    act.wait_ge(dn_loaded[par], loads(e, par))
                    nc.scalar.activation(dn_hi[:, par, :, :], raw_dn[:, par, :, :], ACT.Copy,
                                         scale=W_SCALE).then_inc(dn_hi_r, 1)

                def turn(e, par, first, last):
                    if first:
                        x_part(e, par)
                        up_part(e, par, range(KC))
                    if not last:
                        x_part(e + 1, 1 - par)
                        up_part(e + 1, 1 - par, range(0, 2))
                    gate(e, par, 0)
                    if not last:
                        up_part(e + 1, 1 - par, range(2, KC))
                    h_part(e, par, 0)
                    gate(e, par, 1)
                    dn_part(e, par)
                    h_part(e, par, 1)
                    gate(e, par, 2)
                    h_part(e, par, 2)
                    if not first:
                        weigh(e - 1, 1 - par)

                pairs(act, EXPERTS, turn)
                weigh(EXPERTS - 1, 1)

            @block.vector
            def _(dve):
                def x_part(e, par):
                    for c in range(SLOT_TILES):
                        dve.wait_ge(x_hi_r, e * SLOT_TILES + c + 1)
                        nc.vector.scalar_tensor_tensor(
                            xT_lo[:, par, :, c * P:(c + 1) * P],
                            PS[:, 6 + c % 2, :].rearrange("p (k n) -> p k n", k=KC), ACT_SCALE,
                            xT_hi[:, par, :, c * P:(c + 1) * P], ALU.mult, ALU.subtract).then_inc(x_lo_r, 1)

                def up_part(e, par, ks):
                    for k in ks:
                        dve.wait_ge(up_hi_r, e * KC + k + 1)
                        nc.vector.scalar_tensor_tensor(up_lo[:, par, k, :], raw_up[:, par, k, :], W_SCALE,
                                                       up_hi[:, par, k, :], ALU.mult,
                                                       ALU.subtract).then_inc(up_lo_r, 1)

                def hidden(e, par, j):
                    n, w, at = e * FCH + j, WIDTH[j], 2 * ((par * FCH + j) % 2)
                    dve.wait_ge(silu_r, n + 1)
                    wait(dve, h_lo_r, n - 1)
                    nc.vector.scalar_tensor_tensor(hf[0:w, (par * FCH + j) % 2, :], PS[0:w, at + 1, 0:CAP],
                                                   H_SCALE / PROD, silu[0:w, (par * FCH + j) % 2, :],
                                                   ALU.mult, ALU.mult).then_inc(hf_r, 1)

                def dn_part(e, par):
                    dve.wait_ge(dn_hi_r, e + 1)
                    flat = "p k n -> p (k n)"
                    nc.vector.scalar_tensor_tensor(dn_lo[:, par, :, :].rearrange(flat),
                                                   raw_dn[:, par, :, :].rearrange(flat), W_SCALE,
                                                   dn_hi[:, par, :, :].rearrange(flat), ALU.mult,
                                                   ALU.subtract).then_inc(dn_lo_r, 1)

                def turn(e, par, first, last):
                    if first:
                        x_part(e, par)
                        up_part(e, par, range(KC))
                    if not last:
                        x_part(e + 1, 1 - par)
                        up_part(e + 1, 1 - par, range(0, 2))
                    hidden(e, par, 0)
                    if not last:
                        up_part(e + 1, 1 - par, range(2, KC))
                    hidden(e, par, 1)
                    dn_part(e, par)
                    hidden(e, par, 2)

                pairs(dve, EXPERTS, turn)

        with ExitStack() as st:
            def sb(name, shape, dt):
                return st.enter_context(nc.sbuf_tensor(name, shape, dt))

            gate2 = sb("gate2", [P, BATCH, DIM], fp32)
            yin = sb("yin", [P, TILES, DIM], fp32)
            names = [f"yin{n}" for n in range(TILES)]
            yin_loaded = sems(st, " ".join(names))
            gate2_loaded, scaled, done, stored = sems(st, "gate2_loaded scaled6 done6 stored6")
            block = st.enter_context(nc.Block())

            @block.sync
            def _(sp):
                for n in range(TILES):
                    sp.dma_start(yin[:, n, :], y_d[n * P:(n + 1) * P, :]).then_inc(yin_loaded[n], 16)

            @block.scalar
            def _(act):
                for b in range(BATCH):
                    act.dma_start(gate2[:, b, :], mod_d[b:b + 1, 5 * DIM:6 * DIM].partition_broadcast(P)
                                  .rearrange("p a d -> p (a d)")).then_inc(gate2_loaded, 16)
                for n in range(TILES):
                    act.wait_ge(done, n + 1)
                    act.dma_start(t["out"][n * P:(n + 1) * P, :], x1[:, n, :]).then_inc(stored, 16)
                act.wait_ge(stored, 16 * TILES)

            @block.vector
            def _(dve):
                dve.wait_ge(gate2_loaded, 16 * BATCH)
                for n in range(TILES):
                    dve.wait_ge(yin_loaded[n], 16)
                    nc.vector.tensor_tensor(yin[:, n, :], yin[:, n, :], gate2[:, n // BT, :], ALU.mult
                                            ).then_inc(scaled, 1)
                    dve.wait_ge(scaled, n + 1)
                    nc.vector.tensor_tensor(x1[:, n, :], x1[:, n, :], yin[:, n, :], ALU.add).then_inc(done, 1)


_OUT = (BATCH, SEQ, DIM)


def laid_out(inputs):
    def split(w, chunks):
        return np.ascontiguousarray(w.reshape(chunks, P, -1).transpose(1, 0, 2))

    def padded(w, rows):
        return np.concatenate([w, np.zeros((rows - w.shape[0], w.shape[1]), w.dtype)], 0)

    a = {k[3:]: np.asarray(v) for k, v in inputs.items()}
    wg = a["ffn_w_gate"].transpose(0, 2, 1).reshape(EXPERTS, KC, P, 1, FF)
    wu = a["ffn_w_up"].transpose(0, 2, 1).reshape(EXPERTS, KC, P, 1, FF)
    up = np.concatenate([wg, wu], 3).transpose(0, 2, 1, 3, 4).reshape(EXPERTS, P, UP)
    wd = a["ffn_w_down"].transpose(0, 2, 1)
    wd = np.concatenate([wd, np.zeros((EXPERTS, FCH * P - FF, DIM), wd.dtype)], 1)
    down = wd.reshape(EXPERTS, FCH, P, DIM).transpose(0, 2, 1, 3).reshape(EXPERTS, P, DOWN)
    return {
        "x": np.ascontiguousarray(a["attn_x"].reshape(TOK, DIM)),
        "c": np.ascontiguousarray(a["c"].T.reshape(KC, P, BATCH).transpose(1, 0, 2).reshape(P, KC * BATCH)),
        "wmod": split(a["wmod"], KC),
        "wqkv": split(a["attn_Wqkv"], KC),
        "wo": split(a["attn_Wo"], KC),
        "gate": split(a["ffn_gate_w"].T, KC),
        "sh_gate": split(padded(a["ffn_sh_gate"], SCH * P).T, KC),
        "sh_up": split(padded(a["ffn_sh_up"], SCH * P).T, KC),
        "sh_down": split(padded(a["ffn_sh_down"].T, SCH * P), SCH),
        "experts": np.ascontiguousarray(np.concatenate([up, down], 2)),
        "consts": constants(),
        "slots": empty_slots(),
    }


def kernel(**inputs):
    import concourse.bacc as bacc
    from concourse.bass_utils import run_bass_kernel_spmd

    nc = bacc.Bacc("TRN2", target_bir_lowering=False, num_devices=1)
    arrays = laid_out(inputs)
    t = {k: nc.dram_tensor("in_" + k, v.shape, mybir.dt.from_np(v.dtype), kind="ExternalInput").ap()
         for k, v in arrays.items()}
    t["out"] = nc.dram_tensor("out", (TOK, DIM), mybir.dt.float32, kind="ExternalOutput").ap()
    adaln_program(nc, t)
    r = run_bass_kernel_spmd(nc, [{"in_" + k: v for k, v in arrays.items()}], core_ids=[0])
    return r.results[0]["out"].reshape(_OUT)
```

```python
import math
from contextlib import ExitStack

import numpy as np

import concourse.bass as bass
from concourse import mybir

P = 128
BATCH, SEQ, DIM = 2, 1024, 512
TOK = BATCH * SEQ
TILES = TOK // P
BT = SEQ // P
KC = DIM // P
HEADS, HD = 16, 32
EXPERTS, TOPK = 64, 6
CAP = 2 * ((TOK * TOPK + EXPERTS - 1) // EXPERTS)
SLOT_TILES = CAP // P
MAIN_TILES = SLOT_TILES - 1
FF = 352
FCH = (FF + P - 1) // P
SH = 704
SCH = (SH + P - 1) // P
UP = KC * 2 * FF
DOWN = FCH * DIM
EPS = 1e-5
BANK = 512
GT = 4

ACT_SCALE = 16.0
W_SCALE = 64.0
QKV_SCALE = 8.0
P_SCALE = 1024.0
H_SCALE = 4.0
PROD = ACT_SCALE * W_SCALE
MASKED = -1e30
DROPPED = float(1 << 20)

CONSTS = dict(ident=P, mask=P, tri=P, iota=EXPERTS, slot0=EXPERTS, cos=BT * HD, sin=BT * HD, token=TILES)


def columns():
    at, where = 0, {}
    for name, n in CONSTS.items():
        where[name] = (at, at + n)
        at += n
    return where, at


def constants():
    where, n = columns()
    c = np.zeros((P, n), np.float32)
    p, j = np.arange(P)[:, None], np.arange(P)[None, :]

    def put(name, value):
        c[:, where[name][0]:where[name][1]] = value

    put("ident", p == j)
    put("mask", np.where(j > p, MASKED, 0.0))
    put("tri", p < j)
    put("iota", np.arange(EXPERTS)[None, :])
    put("slot0", np.arange(EXPERTS)[None, :] * SLOT_TILES)
    i = np.arange(HD // 2, dtype=np.float32)
    inv = (np.float32(1.0) / np.float32(10000.0) ** (np.float32(2.0) * i / np.float32(HD))).astype(np.float32)
    th = np.arange(SEQ, dtype=np.float32)[:, None] * inv[None, :]
    s = np.float32(QKV_SCALE / PROD)
    cos = np.repeat(np.cos(th) * s, 2, 1)
    sin = np.repeat(np.sin(th) * s, 2, 1)
    sin[:, 0::2] *= -1
    for name, t in (("cos", cos), ("sin", sin)):
        put(name, t.reshape(BT, P, HD).transpose(1, 0, 2).reshape(P, BT * HD))
    put("token", np.arange(TILES)[None, :] * P + p)
    return c


def empty_slots():
    t = np.zeros((P, EXPERTS, SLOT_TILES, 2), np.int32)
    t[..., 0] = TOK + np.arange(P)[:, None, None] + P * np.arange(SLOT_TILES)[None, None, :]
    return t.reshape(EXPERTS * CAP, 2)


def wait(engine, sem, value):
    if not (isinstance(value, int) and value <= 0):
        engine.wait_ge(sem, value)


def pairs(engine, n, emit, base=0):
    emit(base, 0, True, False)
    emit(base + 1, 1, False, False)
    with engine.Fori(1, n // 2 - 1) as m:
        emit(m * 2 + base, 0, False, False)
        emit(m * 2 + base + 1, 1, False, False)
    emit(base + n - 2, 0, False, False)
    emit(base + n - 1, 1, False, True)


def peeled(engine, n, emit):
    emit(0)
    with engine.Fori(1, n) as m:
        emit(m)


def loads(g, par):
    return (g - par) * 8 + 16


def adaln_program(nc, t):
    fp32, fp16, bf16 = mybir.dt.float32, mybir.dt.float16, mybir.dt.bfloat16
    i32, u32 = mybir.dt.int32, mybir.dt.uint32
    ALU, ACT, AX = mybir.AluOpType, mybir.ActivationFunctionType, mybir.AxisListType
    where, n_const = columns()
    top = ExitStack()
    with top:
        PS = top.enter_context(nc.psum_tensor("PS", [P, 8, BANK], fp32))

        def sems(stack, names):
            made = [nc.alloc_semaphore(n) for n in names.split()]
            stack.callback(nc.all_engine_barrier)
            stack.callback(nc.clear_and_free_semaphores, made)
            return made

        consts = top.enter_context(nc.sbuf_tensor("consts", [P, n_const], fp32))

        def const(name):
            return consts[:, where[name][0]:where[name][1]]

        ident32 = const("ident")
        cb = top.enter_context(nc.sbuf_tensor("cb", [P, 4, P], bf16))
        ident16 = top.enter_context(nc.sbuf_tensor("ident16", [P, P], fp16))
        stat1 = top.enter_context(nc.sbuf_tensor("stat1", [P, TILES, 2], fp32))
        mod_d = nc.dram_tensor("mod_d", [BATCH, 6 * DIM], fp32).ap()
        overflow = top.enter_context(nc.sbuf_tensor("overflow", [P, 1], i32))
        (tick,) = sems(top, "tick")

        stat2 = top.enter_context(nc.sbuf_tensor("stat2", [P, TILES, 2], fp32))

        def deviation(dve, raw6, small, stat, step, root):
            me, qe, mo, qo = (raw6[:, :, c] for c in (1, 2, 4, 5))
            nc.vector.tensor_tensor(small[:, 0, :], me, mo, ALU.add).then_inc(step, 1)
            nc.vector.tensor_tensor(small[:, 1, :], me, mo, ALU.subtract).then_inc(step, 1)
            nc.vector.tensor_tensor(small[:, 2, :], qe, qo, ALU.add).then_inc(step, 1)
            dve.wait_ge(step, 3)
            nc.vector.tensor_scalar(stat[:, :, 0], small[:, 0, :], 0.5, None, ALU.mult).then_inc(step, 1)
            nc.vector.scalar_tensor_tensor(small[:, 5, :], small[:, 1, :], 0.25, small[:, 1, :],
                                           ALU.mult, ALU.mult).then_inc(step, 1)
            nc.vector.tensor_scalar(small[:, 6, :], small[:, 2, :], 1.0 / DIM, EPS,
                                    ALU.mult, ALU.add).then_inc(step, 1)
            dve.wait_ge(step, 6)
            nc.vector.tensor_tensor(small[:, 3, :], small[:, 5, :], small[:, 6, :], ALU.add).then_inc(step, 1)
            dve.wait_ge(root, 1)
            nc.vector.reciprocal(small[:, 5, :], small[:, 4, :]).then_inc(step, 1)
            dve.wait_ge(step, 8)
            nc.vector.tensor_tensor(small[:, 6, :], small[:, 5, :], small[:, 5, :], ALU.mult).then_inc(step, 1)
            dve.wait_ge(step, 9)
            nc.vector.scalar_tensor_tensor(small[:, 7, :], small[:, 6, :], -0.5, small[:, 3, :],
                                           ALU.mult, ALU.mult).then_inc(step, 1)
            dve.wait_ge(step, 10)
            nc.vector.scalar_tensor_tensor(stat[:, :, 1], small[:, 7, :], 1.5, small[:, 5, :],
                                           ALU.add, ALU.mult).then_inc(step, 1)

        s2 = ExitStack()
        wqkv_hi = s2.enter_context(nc.sbuf_tensor("wqkv_hi", [P, KC, 3 * DIM], fp16))
        wqkv_lo = s2.enter_context(nc.sbuf_tensor("wqkv_lo", [P, KC, 3 * DIM], fp16))
        with ExitStack() as st:
            def sb(name, shape, dt):
                return st.enter_context(nc.sbuf_tensor(name, shape, dt))

            c_in = sb("c_in", [P, KC * BATCH], fp32)
            c_silu = sb("c_silu", [P, KC, BATCH], fp32)
            wmod = sb("wmod", [P, KC, 6 * DIM], fp32)
            wqkv = sb("wqkv", [P, KC, 3 * DIM], fp32)
            xall = sb("xall", [P, TILES, DIM], fp32)
            rows = sb("rows", [BATCH, 6, DIM], fp32)
            sign = sb("sign", [BATCH, DIM], fp32)
            minus = sb("minus", [BATCH, DIM], fp32)
            size = sb("size", [BATCH, DIM], fp32)
            raw6 = sb("raw6", [P, TILES, 6], fp32)
            small = sb("small", [P, 8, TILES], fp32)
            (c_loaded, const_loaded, wmod_loaded, wqkv_loaded, x_loaded, c_ready, mod_done, row_ready, gate_step,
             rows_stored, cb_ready, wq_hi, wq_lo, stats, step, root) = sems(
                st, "c_loaded const_loaded wmod_loaded wqkv_loaded x_loaded c_ready mod_done row_ready gate_step "
                    "rows_stored cb_ready wq_hi wq_lo stats step root")
            block = st.enter_context(nc.Block())

            @block.sync
            def _(sp):
                sp.dma_start(c_in[:, :], t["c"]).then_inc(c_loaded, 16)
                sp.dma_start(wmod[:, :, :], t["wmod"]).then_inc(wmod_loaded, 16)
                sp.dma_start(wqkv[:, :, :], t["wqkv"]).then_inc(wqkv_loaded, 16)
                sp.wait_ge(row_ready, 6)
                sp.dma_start(mod_d, rows[:, :, :].rearrange("b s d -> b (s d)")).then_inc(rows_stored, 16)
                sp.wait_ge(rows_stored, 16)

            @block.scalar
            def _(act):
                act.dma_start(consts[:, :], t["consts"]).then_inc(const_loaded, 16)
                act.dma_start(xall[:, :, :], t["x"].rearrange("(n p) d -> p n d", p=P)).then_inc(x_loaded, 16)
                act.wait_ge(c_loaded, 16)
                nc.scalar.activation(c_silu[:, :, :].rearrange("p k b -> p (k b)"), c_in[:, :],
                                     ACT.Silu).then_inc(c_ready, 1)
                act.wait_ge(wqkv_loaded, 16)
                for k in range(KC):
                    nc.scalar.activation(wqkv_hi[:, k, :], wqkv[:, k, :], ACT.Copy,
                                         scale=W_SCALE).then_inc(wq_hi, 1)
                act.wait_ge(step, 7)
                nc.scalar.activation(small[:, 4, :], small[:, 3, :], ACT.Sqrt).then_inc(root, 1)

            @block.tensor
            def _(pe):
                pe.wait_ge(c_ready, 1)
                pe.wait_ge(wmod_loaded, 16)
                for g in range(6):
                    for k in range(KC):
                        last = nc.tensor.matmul(PS[0:BATCH, g, :], c_silu[:, k, :],
                                                wmod[:, k, g * DIM:(g + 1) * DIM], start=k == 0, stop=k == KC - 1)
                    last.then_inc(mod_done, 1)

            @block.vector
            def _(dve):
                dve.wait_ge(const_loaded, 16)
                nc.vector.tensor_copy(ident16[:, :], ident32).then_inc(cb_ready, 1)
                for n, name in enumerate(("ident", "mask", "tri")):
                    nc.vector.tensor_copy(cb[:, n, :], const(name)).then_inc(cb_ready, 1)
                nc.vector.memset(cb[:, 3, :], 1.0).then_inc(cb_ready, 1)
                dve.wait_ge(x_loaded, 16)
                with dve.Fori(0, TILES) as n:
                    nc.vector.bn_stats(raw6[:, bass.ds(n, 1), :], xall[:, bass.ds(n, 1), :]).then_inc(stats, 1)
                dve.wait_ge(stats, TILES)
                deviation(dve, raw6, small, stat1, step, root)
                gates = 0
                for g in range(6):
                    dve.wait_ge(mod_done, g + 1)
                    if g % 3 < 2:
                        nc.vector.tensor_scalar(rows[:, g, :], PS[0:BATCH, g, :], float(g % 3), None,
                                                ALU.add).then_inc(row_ready, 1)
                    else:
                        if gates:
                            dve.wait_ge(row_ready, g)
                        nc.vector.tensor_scalar(sign[:, :], PS[0:BATCH, g, :], 0.0, 2.0, ALU.is_ge,
                                                ALU.mult).then_inc(gate_step, 1)
                        nc.vector.tensor_scalar(minus[:, :], PS[0:BATCH, g, :], -1.0, None,
                                                ALU.mult).then_inc(gate_step, 1)
                        dve.wait_ge(gate_step, gates + 2)
                        nc.vector.scalar_tensor_tensor(size[:, :], PS[0:BATCH, g, :], 0.25, minus[:, :],
                                                       ALU.max, ALU.max).then_inc(gate_step, 1)
                        gates += 3
                        dve.wait_ge(gate_step, gates)
                        nc.vector.scalar_tensor_tensor(rows[:, g, :], sign[:, :], -1.0, size[:, :],
                                                       ALU.add, ALU.mult).then_inc(row_ready, 1)
                for k in range(KC):
                    dve.wait_ge(wq_hi, k + 1)
                    nc.vector.scalar_tensor_tensor(wqkv_lo[:, k, :], wqkv[:, k, :], W_SCALE, wqkv_hi[:, k, :],
                                                   ALU.mult, ALU.subtract).then_inc(wq_lo, 1)


        attn_d = nc.dram_tensor("attn_d", [TOK, DIM], fp32).ap()
        with s2:
            def sb(name, shape, dt):
                return s2.enter_context(nc.sbuf_tensor(name, shape, dt))

            QT = sb("QT", [P, HEADS, SEQ], fp16)
            KT = sb("KT", [P, HEADS, SEQ], fp16)
            V = sb("V", [P, BT, HEADS, 2, HD], fp16)
            hT_hi = sb("hT_hi", [P, KC, SEQ], fp16)
            hT_lo = sb("hT_lo", [P, KC, SEQ], fp16)
            mod1 = sb("mod1", [P, BATCH, 2, DIM], fp32)
            xin = sb("xin", [P, 2, DIM], fp32)
            z = sb("z", [P, 2, DIM], fp32)
            zm = sb("zm", [P, 2, DIM], fp32)
            h = sb("h", [P, 2, DIM], fp32)
            rot = sb("rot", [P, 2, 2 * HEADS, HD], fp32)
            qk = sb("qk", [P, 2 * HEADS, HD], fp32)
            qk16 = sb("qk16", [P, 2 * HEADS, 4, HD], fp16)
            O = sb("O", [P, BT, DIM], fp32)
            Pr = sb("Pr", [P, 2, SEQ], fp32)
            PT_hi = sb("PT_hi", [P, 2, BT, P], fp16)
            PT_lo = sb("PT_lo", [P, 2, BT, P], fp16)
            negmax = sb("negmax", [P, 2], fp32)
            bias = sb("bias", [P, 2], fp32)
            exp_scale = sb("exp_scale", [P, 1], fp32)
            rowsum = sb("rowsum", [P, 2, BT], fp32)
            inv = sb("inv", [P, 2, BT], fp32)
            half = sb("half", [P, 2, BT, HD], fp32)
            SCORE = 1.0 / (math.sqrt(HD) * QKV_SCALE * QKV_SCALE)
            GROUPS = [(i, j, min(j + 4, i + 1)) for i in range(BT) for j in range(0, i + 1, 4)]
            GN = len(GROUPS)
            GEND = [max(n for n, g in enumerate(GROUPS) if g[0] == i) + 1 for i in range(BT)]

            (mod_in, xin_a, xin_b, scale_set, z_ready, zm_ready, h_ready, hT_raw, hT_hi_ready, hT_lo_ready,
             qkv_done, cos_done, sin_done, v_hi_ready, v_lo_ready, qk_ready, qk_hi, qk_lo, parts_copied, qkT_done, q_copied, k_copied,
             s_done, max_done, bias_done, exp_done, pT_done, p_hi, p_lo, pv_done, inv_done, half_done, o_done,
             o_stored) = sems(
                s2, "mod_in xin_a xin_b scale_set z_ready zm_ready h_ready hT_raw hT_hi_ready hT_lo_ready qkv_done "
                    "cos_done sin_done v_hi_ready v_lo_ready qk_ready qk_hi qk_lo parts_copied qkT_done q_copied k_copied s_done "
                    "max_done bias_done exp_done pT_done p_hi p_lo pv_done inv_done half_done o_done o_stored")
            xin_loaded = (xin_a, xin_b)
            block = s2.enter_context(nc.Block())

            @block.sync
            def _(sp):
                for b in range(BATCH):
                    sp.dma_start(mod1[:, b, :, :].rearrange("p s d -> p (s d)"),
                                 mod_d[b:b + 1, 0:2 * DIM].partition_broadcast(P)).then_inc(mod_in, 16)
                with sp.Fori(0, BATCH) as b:
                    with sp.Fori(0, BT // 2) as m:
                        for par in range(2):
                            g = b * BT + m * 2 + par
                            sp.wait_ge(z_ready, g - par)
                            sp.dma_start(xin[:, par, :], t["x"][bass.ds(g * P, P), :]).then_inc(xin_loaded[par], 16)
                    sp.wait_ge(o_done, (b + 1) * HEADS)
                    sp.dma_start(attn_d[bass.ds(b * SEQ, SEQ), :].rearrange("(n p) d -> p n d", p=P),
                                 O[:, :, :]).then_inc(o_stored, 16)
                sp.wait_ge(o_stored, 16 * BATCH)

            def score_unit(pe, H, hh, i, first):
                if not first:
                    pe.wait_ge(exp_done, H * BT + i - 1)
                s = PS[:, 2 * (i % 2):2 * (i % 2) + 2, :].rearrange("p a n -> p (a n)")
                q = QT[:, bass.ds(hh, 1), i * P:(i + 1) * P]
                for at in range(0, (i + 1) * P, BANK):
                    end = min(at + BANK, (i + 1) * P)
                    diagonal = end == (i + 1) * P
                    last = nc.tensor.matmul(s[:, at:end], q, KT[:, bass.ds(hh, 1), at:end],
                                            start=True, stop=not diagonal)
                    if diagonal:
                        last = nc.tensor.matmul(s[:, i * P:end], cb[:, 0, :], cb[:, 1, :], start=False, stop=True)
                last.then_inc(s_done, 1)

            def pv_unit(pe, H, hh, hp, i, first):
                pe.wait_ge(p_lo, H * GN + GEND[i])
                if i == 0 and not first:
                    pe.wait_ge(half_done, 2 * (H - 1))
                for j in range(i + 1):
                    for part in (PT_hi, PT_lo):
                        last = nc.tensor.matmul(
                            PS[:, 6 + hp, i * 2 * HD:(i + 1) * 2 * HD], part[:, i % 2, j, :],
                            V[:, j, bass.ds(hh, 1), :, :].rearrange("p h s d -> p (h s d)"),
                            start=j == 0 and part is PT_hi, stop=j == i and part is PT_lo)
                last.then_inc(pv_done, 1)

            def pe_head(pe, b, hh, hp, start, end):
                H = b * HEADS + hh
                if start:
                    score_unit(pe, H, hh, 0, True)
                for i in range(BT):
                    if i + 1 < BT:
                        score_unit(pe, H, hh, i + 1, start and i == 0)
                    elif not end:
                        score_unit(pe, H + 1, hh + 1, 0, False)
                    pe.wait_ge(exp_done, H * BT + i + 1)
                    for n, (gi, lo, hi) in enumerate(GROUPS):
                        if gi != i:
                            continue
                        if n >= 2 or not start:
                            pe.wait_ge(p_lo, H * GN + n - 1)
                        for j in range(lo, hi):
                            last = nc.tensor.transpose(PS[:, 4 + n % 2, (j - lo) * P:(j - lo + 1) * P],
                                                       Pr[:, i % 2, j * P:(j + 1) * P], ident32)
                        last.then_inc(pT_done, 1)
                    if i:
                        pv_unit(pe, H, hh, hp, i - 1, start and True)
                pv_unit(pe, H, hh, hp, BT - 1, start)

            def heads(engine, emit):
                emit(0, 0, True, False)
                emit(1, 1, False, False)
                with engine.Fori(1, HEADS // 2 - 1) as m:
                    emit(m * 2, 0, False, False)
                    emit(m * 2 + 1, 1, False, False)
                emit(HEADS - 2, 0, False, False)
                emit(HEADS - 1, 1, False, True)

            @block.tensor
            def _(pe):
                def transpose_qk(g, tile):
                    pe.wait_ge(parts_copied, 3 * (g + 1))
                    for quarter in range(4):
                        bank = PS[:, 7 - quarter % 2, :].bitcast(fp16)
                        if quarter >= 2:
                            pe.wait_ge(q_copied, 2 * g + quarter - 1)
                        else:
                            pe.wait_ge(k_copied, 2 * g)
                        for n in range(8):
                            head = quarter * 8 + n
                            last = nc.tensor.transpose(bank[:, n * P:(n + 1) * P],
                                                       qk16[:, head, :, :].rearrange("p s d -> p (s d)"),
                                                       ident16[:, :])
                        last.then_inc(qkT_done, 1)

                def project(g, tile, par):
                    pe.wait_ge(hT_lo_ready, g + 1)
                    pe.wait_ge(sin_done, 2 * (g - par) )
                    pe.wait_ge(v_lo_ready, g - par)
                    for n in range(3):
                        for k in range(KC):
                            lhs_hi, lhs_lo = (w[:, k, bass.ds(tile * P, P)] for w in (hT_hi, hT_lo))
                            cols = slice(n * DIM, (n + 1) * DIM)
                            for m, (l, r) in enumerate(((lhs_hi, wqkv_hi), (lhs_hi, wqkv_lo), (lhs_lo, wqkv_hi))):
                                last = nc.tensor.matmul(PS[:, 3 * par + n, :], l, r[:, k, cols],
                                                        start=k == 0 and m == 0, stop=k == KC - 1 and m == 2)
                    last.then_inc(qkv_done, 1)

                with pe.Fori(0, BATCH) as b:
                    with pe.Fori(0, BT // 2) as m:
                        for par in range(2):
                            g = b * BT + m * 2 + par
                            pe.wait_ge(h_ready, g + 1)
                            pe.wait_ge(hT_lo_ready, g)
                            for k in range(KC):
                                last = nc.tensor.transpose(PS[:, 6, k * P:(k + 1) * P],
                                                           h[:, par, k * P:(k + 1) * P], ident32)
                            last.then_inc(hT_raw, 1)
                    project(b * BT, 0, 0)
                    project(b * BT + 1, 1, 1)
                    transpose_qk(b * BT, 0)
                    with pe.Fori(1, BT // 2) as m:
                        for par in range(2):
                            project(b * BT + m * 2 + par, m * 2 + par, par)
                            transpose_qk(b * BT + m * 2 + par - 1, m * 2 + par - 1)
                    transpose_qk(b * BT + BT - 1, BT - 1)
                    pe.wait_ge(q_copied, 2 * BT * (b + 1))
                    pe.wait_ge(k_copied, 2 * BT * (b + 1))
                    heads(pe, lambda hh, hp, start, end: pe_head(pe, b, hh, hp, start, end))

            @block.scalar
            def _(act):
                def exp_unit(H, hp, i, first):
                    act.wait_ge(bias_done, H * BT + i + 1)
                    if not first:
                        act.wait_ge(pT_done, H * GN + (GEND[i - 2] if i >= 2 else GEND[BT - 2 + i] - GN))
                    s = PS[:, 2 * (i % 2):2 * (i % 2) + 2, :].rearrange("p a n -> p (a n)")
                    nc.scalar.activation(Pr[:, i % 2, 0:(i + 1) * P], s[:, 0:(i + 1) * P], ACT.Exp,
                                         bias=bias[:, i % 2:i % 2 + 1], scale=SCORE,
                                         accum_out=rowsum[:, hp, i:i + 1]).then_inc(exp_done, 1)

                def head(b, hh, hp, start, end):
                    H = b * HEADS + hh
                    if start:
                        exp_unit(H, hp, 0, True)
                    for i in range(BT):
                        if i + 1 < BT:
                            exp_unit(H, hp, i + 1, start and i == 0)
                        elif not end:
                            exp_unit(H + 1, 1 - hp, 0, False)
                        if not (start and i < 2):
                            act.wait_ge(pv_done, H * BT + i - 1)
                        for n, (gi, lo, hi) in enumerate(GROUPS):
                            if gi == i:
                                act.wait_ge(pT_done, H * GN + n + 1)
                                nc.scalar.activation(
                                    PT_hi[:, i % 2, lo:hi, :].rearrange("p j n -> p (j n)"),
                                    PS[:, 4 + n % 2, 0:(hi - lo) * P], ACT.Copy, scale=P_SCALE).then_inc(p_hi, 1)

                with act.Fori(0, BATCH) as b:
                    with act.Fori(0, BT) as n:
                        g = b * BT + n
                        act.wait_ge(hT_raw, g + 1)
                        nc.scalar.activation(hT_hi[:, :, bass.ds(n * P, P)],
                                             PS[:, 6, :].rearrange("p (k n) -> p k n", k=KC), ACT.Copy,
                                             scale=ACT_SCALE).then_inc(hT_hi_ready, 1)
                    with act.Fori(0, BT // 2) as m:
                        for par in range(2):
                            g = b * BT + m * 2 + par
                            act.wait_ge(qkv_done, g + 1)
                            nc.scalar.activation(V[:, bass.ds(m * 2 + par, 1), :, 0, :],
                                                 PS[:, 3 * par + 2, :].rearrange("p (h d) -> p h d", h=HEADS),
                                                 ACT.Copy, scale=QKV_SCALE / PROD).then_inc(v_hi_ready, 1)
                            act.wait_ge(qk_ready, g + 1)
                            act.wait_ge(qkT_done, 4 * g)
                            nc.scalar.activation(qk16[:, :, 0, :], qk[:, :, :], ACT.Copy).then_inc(qk_hi, 1)
                            for quarter in range(2):
                                act.wait_ge(qkT_done, 4 * g + quarter + 1)
                                nc.scalar.activation(
                                    QT[:, quarter * 8:quarter * 8 + 8, bass.ds((m * 2 + par) * P, P)],
                                    PS[:, 7 - quarter, :].bitcast(fp16).rearrange("p (h n) -> p h n", h=8),
                                    ACT.Copy).then_inc(q_copied, 1)
                    heads(act, lambda hh, hp, start, end: head(b, hh, hp, start, end))

            @block.vector
            def _(dve):
                nc.vector.memset(exp_scale[:, :], SCORE).then_inc(scale_set, 1)

                def max_unit(H, i, first):
                    dve.wait_ge(s_done, H * BT + i + 1)
                    if not first:
                        dve.wait_ge(bias_done, H * BT + i - 1)
                    s = PS[:, 2 * (i % 2):2 * (i % 2) + 2, :].rearrange("p a n -> p (a n)")
                    nc.vector.tensor_reduce(negmax[:, i % 2:i % 2 + 1], s[:, 0:(i + 1) * P], AX.X, ALU.max,
                                            negate=True).then_inc(max_done, 1)

                def head(b, hh, hp, start, end):
                    H = b * HEADS + hh
                    if start:
                        max_unit(H, 0, True)
                    for i in range(BT):
                        if i + 1 < BT:
                            max_unit(H, i + 1, start and i == 0)
                        elif not end:
                            max_unit(H + 1, 0, False)
                        for n, (gi, lo, hi) in enumerate(GROUPS):
                            if gi == i:
                                dve.wait_ge(p_hi, H * GN + n + 1)
                                nc.vector.scalar_tensor_tensor(
                                    PT_lo[:, i % 2, lo:hi, :].rearrange("p j n -> p (j n)"),
                                    PS[:, 4 + n % 2, 0:(hi - lo) * P], P_SCALE,
                                    PT_hi[:, i % 2, lo:hi, :].rearrange("p j n -> p (j n)"),
                                    ALU.mult, ALU.subtract).then_inc(p_lo, 1)
                    if not start:
                        dve.wait_ge(o_done, H)
                    nc.vector.reciprocal(inv[:, hp, :], rowsum[:, hp, :]).then_inc(inv_done, 1)
                    dve.wait_ge(inv_done, H + 1)
                    dve.wait_ge(pv_done, (H + 1) * BT)
                    o = PS[:, 6 + hp, :].rearrange("p (i s d) -> p i s d", i=BT, s=2)
                    for s in range(2):
                        nc.vector.scalar_tensor_tensor(
                            half[:, s, :, :], o[:, :, s, :], 1.0 / (P_SCALE * QKV_SCALE),
                            inv[:, hp, :].unsqueeze(2).broadcast_to([P, BT, HD]),
                            ALU.mult, ALU.mult).then_inc(half_done, 1)

                with dve.Fori(0, BATCH) as b:
                    dve.wait_ge(mod_in, 16 * BATCH)
                    with dve.Fori(0, BT // 2) as m:
                        for par in range(2):
                            tile = m * 2 + par
                            g = b * BT + tile
                            dve.wait_ge(xin_loaded[par], 16 * (b * (BT // 2) + m + 1))
                            dve.wait_ge(h_ready, g - par)
                            nc.vector.tensor_scalar(z[:, par, :], xin[:, par, :], stat1[:, bass.ds(g, 1), 0],
                                                    stat1[:, bass.ds(g, 1), 1], ALU.subtract,
                                                    ALU.mult).then_inc(z_ready, 1)
                            dve.wait_ge(z_ready, g + 1)
                            nc.vector.tensor_tensor(zm[:, par, :], z[:, par, :], mod1[:, bass.ds(b, 1), 1, :],
                                                    ALU.mult).then_inc(zm_ready, 1)
                            dve.wait_ge(hT_hi_ready, g + 1)
                            nc.vector.scalar_tensor_tensor(
                                hT_lo[:, :, bass.ds(tile * P, P)], PS[:, 6, :].rearrange("p (k n) -> p k n", k=KC),
                                ACT_SCALE, hT_hi[:, :, bass.ds(tile * P, P)],
                                ALU.mult, ALU.subtract).then_inc(hT_lo_ready, 1)
                    with dve.Fori(0, BT // 2) as m:
                        for par in range(2):
                            tile = m * 2 + par
                            g = b * BT + tile
                            dve.wait_ge(qkv_done, g + 1)
                            dve.wait_ge(qk_ready, g)
                            x = PS[:, 3 * par:3 * par + 2, :].rearrange("p a (h d) -> p (a h) d", d=HD)
                            cos, sin = (const(c).rearrange("p (n d) -> p n d", d=HD)[:, bass.ds(tile, 1), :]
                                        .broadcast_to([P, 2 * HEADS, HD]) for c in ("cos", "sin"))
                            nc.vector.tensor_tensor(rot[:, 0, :, :], x, cos, ALU.mult).then_inc(cos_done, 1)
                            for a in range(2):
                                nc.vector.tensor_tensor(rot[:, 1, :, a::2], x[:, :, 1 - a::2], sin[:, :, a::2],
                                                        ALU.mult).then_inc(sin_done, 1)
                            dve.wait_ge(v_hi_ready, g + 1)
                            nc.vector.scalar_tensor_tensor(
                                V[:, bass.ds(tile, 1), :, 1, :],
                                PS[:, 3 * par + 2, :].rearrange("p (h d) -> p h d", h=HEADS), QKV_SCALE / PROD,
                                V[:, bass.ds(tile, 1), :, 0, :], ALU.mult, ALU.subtract).then_inc(v_lo_ready, 1)
                            dve.wait_ge(qk_lo, g + 1)
                            for heads_of, to, src in ((slice(0, HEADS), slice(2, 4), slice(0, 2)),
                                                      (slice(HEADS, 2 * HEADS), 2, 1), (slice(HEADS, 2 * HEADS), 3, 0)):
                                nc.vector.tensor_copy(qk16[:, heads_of, to, :],
                                                      qk16[:, heads_of, src, :]).then_inc(parts_copied, 1)
                            for quarter in range(2):
                                dve.wait_ge(qkT_done, 4 * g + quarter + 3)
                                nc.vector.tensor_copy(
                                    KT[:, quarter * 8:quarter * 8 + 8, bass.ds(tile * P, P)],
                                    PS[:, 7 - quarter, :].bitcast(fp16).rearrange("p (h n) -> p h n", h=8),
                                    ).then_inc(k_copied, 1)
                    heads(dve, lambda hh, hp, start, end: head(b, hh, hp, start, end))

            @block.gpsimd
            def _(pool):
                def bias_unit(H, i, first):
                    pool.wait_ge(max_done, H * BT + i + 1)
                    if not first:
                        pool.wait_ge(exp_done, H * BT + i - 1)
                    nc.gpsimd.tensor_tensor(bias[:, i % 2:i % 2 + 1], negmax[:, i % 2:i % 2 + 1],
                                            exp_scale[:, :], ALU.mult).then_inc(bias_done, 1)

                def head(b, hh, hp, start, end):
                    H = b * HEADS + hh
                    if start:
                        bias_unit(H, 0, True)
                    for i in range(BT):
                        if i + 1 < BT:
                            bias_unit(H, i + 1, start and i == 0)
                        elif not end:
                            bias_unit(H + 1, 0, False)
                    pool.wait_ge(half_done, 2 * (H + 1))
                    pool.sem_inc(tick, 1)
                    nc.gpsimd.tensor_tensor(O[:, :, bass.ds(hh * HD, HD)], half[:, 0, :, :], half[:, 1, :, :],
                                            ALU.add).then_inc(o_done, 1)

                pool.wait_ge(scale_set, 1)
                pool.wait_ge(mod_in, 16 * BATCH)
                with pool.Fori(0, BATCH) as b:
                    with pool.Fori(0, BT // 2) as m:
                        for par in range(2):
                            g = b * BT + m * 2 + par
                            pool.wait_ge(zm_ready, g + 1)
                            pool.wait_ge(hT_raw, g - par)
                            pool.sem_inc(tick, 1)
                            nc.gpsimd.tensor_tensor(h[:, par, :], zm[:, par, :], mod1[:, bass.ds(b, 1), 0, :],
                                                    ALU.add).then_inc(h_ready, 1)
                    with pool.Fori(0, BT) as n:
                        g = b * BT + n
                        pool.wait_ge(sin_done, 2 * (g + 1))
                        pool.wait_ge(qk_lo, g)
                        nc.gpsimd.tensor_tensor(qk[:, :, :], rot[:, 0, :, :], rot[:, 1, :, :],
                                                ALU.add).then_inc(qk_ready, 1)
                        pool.wait_ge(qk_hi, g + 1)
                        nc.gpsimd.tensor_tensor(qk16[:, :, 1, :], qk[:, :, :], qk16[:, :, 0, :],
                                                ALU.subtract).then_inc(qk_lo, 1)
                    pool.wait_ge(o_stored, b * 16)
                    heads(pool, lambda hh, hp, start, end: head(b, hh, hp, start, end))

        x1 = top.enter_context(nc.sbuf_tensor("x1", [P, TILES, DIM], fp32))
        with ExitStack() as st:
            def sb(name, shape, dt):
                return st.enter_context(nc.sbuf_tensor(name, shape, dt))

            wo = sb("wo", [P, KC, DIM], fp32)
            wo_hi = sb("wo_hi", [P, KC, DIM], fp16)
            wo_lo = sb("wo_lo", [P, KC, DIM], fp16)
            gate1 = sb("gate1", [P, BATCH, DIM], fp32)
            oin = sb("oin", [P, 2, DIM], fp32)
            xres = sb("xres", [P, 2, DIM], fp32)
            oT_hi = sb("oT_hi", [P, 2, KC, P], fp16)
            oT_lo = sb("oT_lo", [P, 2, KC, P], fp16)
            gated = sb("gated", [P, 2, DIM], fp32)
            raw6 = sb("raw6b", [P, TILES, 6], fp32)
            small = sb("smallb", [P, 8, TILES], fp32)
            (wo_loaded, gate1_loaded, oin_a, oin_b, xres_a, xres_b, wo_hi_ready, wo_lo_ready, oT_raw, oT_hi_ready,
             oT_lo_ready, out_done, gated_ready, x1_ready, stats, step, root) = sems(
                st, "wo_loaded gate1_loaded oin_a oin_b xres_a xres_b wo_hi_ready wo_lo_ready oT_raw oT_hi_ready "
                    "oT_lo_ready out_done gated_ready x1_ready stats3 step3 root3")
            oin_loaded, xres_loaded = (oin_a, oin_b), (xres_a, xres_b)
            block = st.enter_context(nc.Block())

            @block.sync
            def _(sp):
                sp.dma_start(wo[:, :, :], t["wo"]).then_inc(wo_loaded, 16)

                def load(g, par):
                    wait(sp, oT_raw, g - 1)
                    sp.dma_start(oin[:, par, :], attn_d[bass.ds(g * P, P), :]).then_inc(oin_loaded[par], 16)
                    wait(sp, x1_ready, g - 1)
                    sp.dma_start(xres[:, par, :], t["x"][bass.ds(g * P, P), :]).then_inc(xres_loaded[par], 16)

                pairs(sp, TILES, lambda g, par, first, last: load(g, par))

            @block.scalar
            def _(act):
                for b in range(BATCH):
                    act.dma_start(gate1[:, b, :], mod_d[b:b + 1, 2 * DIM:3 * DIM].partition_broadcast(P)
                                  .rearrange("p a d -> p (a d)")).then_inc(gate1_loaded, 16)
                act.wait_ge(wo_loaded, 16)
                nc.scalar.activation(wo_hi[:, :, :], wo[:, :, :], ACT.Copy, scale=W_SCALE).then_inc(wo_hi_ready, 1)

                def part(g, par):
                    act.wait_ge(oT_raw, g + 1)
                    wait(act, out_done, g - 1)
                    nc.scalar.activation(oT_hi[:, par, :, :].rearrange("p k n -> p (k n)"), PS[:, par, :], ACT.Copy,
                                         scale=ACT_SCALE).then_inc(oT_hi_ready, 1)

                pairs(act, TILES, lambda g, par, first, last: part(g, par))
                act.wait_ge(step, 7)
                nc.scalar.activation(small[:, 4, :], small[:, 3, :], ACT.Sqrt).then_inc(root, 1)

            @block.tensor
            def _(pe):
                def turn(g, par):
                    pe.wait_ge(oin_loaded[par], loads(g, par))
                    wait(pe, oT_lo_ready, g - 1)
                    for k in range(KC):
                        last = nc.tensor.transpose(PS[:, par, k * P:(k + 1) * P], oin[:, par, k * P:(k + 1) * P],
                                                   ident32)
                    last.then_inc(oT_raw, 1)

                def project(g, par):
                    pe.wait_ge(oT_lo_ready, g + 1)
                    wait(pe, gated_ready, g - 1)
                    for k in range(KC):
                        for m, (l, r) in enumerate(((oT_hi, wo_hi), (oT_hi, wo_lo), (oT_lo, wo_hi))):
                            last = nc.tensor.matmul(PS[:, 2 + par, :], l[:, par, k, :], r[:, k, :],
                                                    start=k == 0 and m == 0, stop=k == KC - 1 and m == 2)
                    last.then_inc(out_done, 1)

                def both(g, par, first, last):
                    if first:
                        turn(g, par)
                    if not last:
                        turn(g + 1, 1 - par)
                    project(g, par)

                pe.wait_ge(wo_lo_ready, 1)
                pairs(pe, TILES, both)

            @block.vector
            def _(dve):
                dve.wait_ge(wo_hi_ready, 1)
                nc.vector.scalar_tensor_tensor(wo_lo[:, :, :].rearrange("p k d -> p (k d)"),
                                               wo[:, :, :].rearrange("p k d -> p (k d)"), W_SCALE,
                                               wo_hi[:, :, :].rearrange("p k d -> p (k d)"),
                                               ALU.mult, ALU.subtract).then_inc(wo_lo_ready, 1)
                dve.wait_ge(gate1_loaded, 16 * BATCH)

                def part(g, par):
                    dve.wait_ge(oT_hi_ready, g + 1)
                    nc.vector.scalar_tensor_tensor(oT_lo[:, par, :, :].rearrange("p k n -> p (k n)"), PS[:, par, :],
                                                   ACT_SCALE, oT_hi[:, par, :, :].rearrange("p k n -> p (k n)"),
                                                   ALU.mult, ALU.subtract).then_inc(oT_lo_ready, 1)

                def both(g, par, first, last, b):
                    if first and b == 0:
                        part(g, par)
                    if not (last and b == BATCH - 1):
                        part(g + 1, 1 - par)
                    dve.wait_ge(out_done, g + 1)
                    wait(dve, x1_ready, g - 1)
                    nc.vector.scalar_tensor_tensor(gated[:, par, :], PS[:, 2 + par, :], 1.0 / PROD, gate1[:, b, :],
                                                   ALU.mult, ALU.mult).then_inc(gated_ready, 1)
                    if not (first and b == 0):
                        dve.wait_ge(x1_ready, g)
                        nc.vector.bn_stats(raw6[:, bass.ds(g - 1, 1), :], x1[:, bass.ds(g - 1, 1), :]
                                           ).then_inc(stats, 1)

                for b in range(BATCH):
                    pairs(dve, BT, lambda g, par, first, last: both(g, par, first, last, b), b * BT)
                dve.wait_ge(x1_ready, TILES)
                nc.vector.bn_stats(raw6[:, TILES - 1, :], x1[:, TILES - 1, :]).then_inc(stats, 1)
                dve.wait_ge(stats, TILES)
                deviation(dve, raw6, small, stat2, step, root)

            @block.gpsimd
            def _(pool):
                def add(g, par):
                    pool.wait_ge(xres_loaded[par], loads(g, par))
                    pool.wait_ge(gated_ready, g + 1)
                    pool.sem_inc(tick, 1)
                    nc.gpsimd.tensor_tensor(x1[:, bass.ds(g, 1), :], gated[:, par, :], xres[:, par, :],
                                            ALU.add).then_inc(x1_ready, 1)

                pairs(pool, TILES, lambda g, par, first, last: add(g, par))

        h2_d = nc.dram_tensor("h2_d", [TOK + CAP, 2 * DIM], fp16).ap()
        y_d = nc.dram_tensor("y_d", [TOK + CAP, DIM], fp32).ap()
        slots_d = nc.dram_tensor("slots_d", [EXPERTS * CAP, 2], i32).ap()
        with ExitStack() as st:
            def sb(name, shape, dt):
                return st.enter_context(nc.sbuf_tensor(name, shape, dt))

            SHP = SCH * P
            h2T_hi = sb("h2T_hi", [P, KC, TOK], fp16)
            h2T_lo = sb("h2T_lo", [P, KC, TOK], fp16)
            sg_w = [sb("sgw" + c, [P, KC, SHP], fp16) for c in ("_hi", "_lo")]
            su_w = [sb("suw" + c, [P, KC, SHP], fp16) for c in ("_hi", "_lo")]
            sd_w = [sb("sdw" + c, [P, SCH, DIM], fp16) for c in ("_hi", "_lo")]
            gt_w = [sb("gtw" + c, [P, KC, EXPERTS], fp16) for c in ("_hi", "_lo")]
            stage = sb("stage", [P, 2, SHP], fp32)
            mod2 = sb("mod2", [P, BATCH, 2, DIM], fp32)
            zeros = sb("zeros", [P, DIM], fp32)
            z = sb("z2", [P, 2, DIM], fp32)
            h2 = sb("h2", [P, 2, DIM], fp32)
            h2p = sb("h2p", [P, 2, 2, DIM], fp16)
            logits = sb("logits", [P, TILES, EXPERTS], fp32)
            top8 = sb("top8", [P, TILES, 8], fp32)
            top8i = sb("top8i", [P, TILES, 8], u32)
            idx = sb("idx", [P, TILES, 8], fp32)
            e8 = sb("e8", [P, TILES, 8], fp32)
            ez = sb("ez", [P, TILES, EXPERTS], fp32)
            sums = sb("sums", [P, 4, TILES], fp32)
            onehot = sb("onehot", [P, TILES, TOPK, EXPERTS], bf16)
            mask = sb("mask", [P, TILES, EXPERTS], bf16)
            total = sb("total", [P, EXPERTS, TILES], fp32)
            keep = sb("keep", [P, EXPERTS, TILES], fp32)
            cum = sb("cum", [P, EXPERTS, TILES], fp32)
            pos, row = ez, logits
            term = sb("term", [P, TILES, EXPERTS], fp32)
            rowk = sb("rowk", [P, TILES, TOPK], fp32)
            row_i = sb("row_i", [P, TILES * TOPK], i32)
            pair = sb("pair", [P, TILES, TOPK, 2], i32)
            silu = sb("silu", [P, 2, GT * P], fp32)
            hf = sb("hf", [P, 2, GT * P], fp32)
            hs_hi = sb("hs_hi", [P, SCH, GT * P], fp16)
            hs_lo = sb("hs_lo", [P, SCH, GT * P], fp16)
            ysh = sb("ysh", [P, 2, DIM], fp32)
            WEIGHTS = ([("sh_gate", sg_w, k, SHP) for k in range(KC)] + [("sh_up", su_w, k, SHP) for k in range(KC)]
                       + [("sh_down", sd_w, k, DIM) for k in range(SCH)]
                       + [("gate", gt_w, k, EXPERTS) for k in range(KC)])
            WEIGHTS = WEIGHTS[-KC:] + WEIGHTS[:-KC]
            (mod2_loaded, st_a, st_b, w_hi, w_lo, slots_set, pad_stored, zero_set, z_ready, zm_ready, h2_ready, h2_hi, h2_lo, h2s_a,
             h2s_b, hT_raw, hT_hi_r, hT_lo_r, logit_done, logit_ready, rt, shifted, mask_r, pos_read, exp_r, count_done, pairs_ready, scattered,
             gu_done, silu_r, hf_r, hs_hi_r, hs_lo_r, dn_done, y_r, ys_a, ys_b) = sems(
                st, "mod2_loaded st_a st_b w_hi w_lo slots_set pad_stored zero_set z_ready4 zm_ready4 h2_ready h2_hi h2_lo h2s_a "
                    "h2s_b hT_raw4 hT_hi_r hT_lo_r logit_done logit_ready rt shifted mask_r pos_read exp_r count_done pairs_ready scattered "
                    "gu_done silu_r hf_r hs_hi_r hs_lo_r dn_done y_r ys_a ys_b")
            staged, h2_stored, y_stored = (st_a, st_b), (h2s_a, h2s_b), (ys_a, ys_b)
            GROUP = TILES // GT
            block = st.enter_context(nc.Block())

            @block.sync
            def _(sp):
                sp.dma_start(slots_d, t["slots"]).then_inc(slots_set, 16)
                for n, (name, _, k, width) in enumerate(WEIGHTS):
                    wait(sp, w_lo, n - 1)
                    sp.dma_start(stage[:, n % 2, 0:width], t[name][:, k, :]).then_inc(staged[n % 2], 16)
                sp.wait_ge(zero_set, 1)
                for n in range(SLOT_TILES):
                    for d, zero in ((h2_d, zeros[:, :].bitcast(fp16)), (y_d, zeros[:, :])):
                        sp.dma_start(d[TOK + n * P:TOK + (n + 1) * P, :], zero).then_inc(pad_stored, 16)

                def store_h2(g, par):
                    sp.wait_ge(h2_lo, g + 1)
                    sp.dma_start(h2_d[bass.ds(g * P, P), :], h2p[:, par, :, :].rearrange("p s d -> p (s d)")
                                 ).then_inc(h2_stored[par], 16)

                def store_y(g, par):
                    sp.wait_ge(y_r, g + 1)
                    sp.dma_start(y_d[bass.ds(g * P, P), :], ysh[:, par, :]).then_inc(y_stored[par], 16)

                pairs(sp, TILES, lambda g, par, first, last: store_h2(g, par))
                pairs(sp, TILES, lambda g, par, first, last: store_y(g, par))
                sp.wait_ge(pad_stored, 16 * 2 * SLOT_TILES)
                for par in range(2):
                    sp.wait_ge(h2_stored[par], 16 * TILES // 2)
                    sp.wait_ge(y_stored[par], 16 * TILES // 2)

            @block.scalar
            def _(act):
                for b in range(BATCH):
                    act.dma_start(mod2[:, b, :, :].rearrange("p s d -> p (s d)"),
                                  mod_d[b:b + 1, 3 * DIM:5 * DIM].partition_broadcast(P)
                                  .rearrange("p a d -> p (a d)")).then_inc(mod2_loaded, 16)
                for n, (_, parts, k, width) in enumerate(WEIGHTS):
                    act.wait_ge(staged[n % 2], 16 * (n // 2 + 1))
                    nc.scalar.activation(parts[0][:, k, :], stage[:, n % 2, 0:width], ACT.Copy,
                                         scale=W_SCALE).then_inc(w_hi, 1)

                def split_hi(g, par):
                    act.wait_ge(h2_ready, g + 1)
                    wait(act, hT_raw, g - 1)
                    if not isinstance(g, int) or g >= 2:
                        act.wait_ge(h2_stored[par], (g - par) * 8)
                    nc.scalar.activation(h2p[:, par, 0, :], h2[:, par, :], ACT.Copy,
                                         scale=ACT_SCALE).then_inc(h2_hi, 1)

                def part(g, par, first, last):
                    if first:
                        split_hi(g, par)
                    if not last:
                        split_hi(g + 1, 1 - par)
                    act.wait_ge(hT_raw, g + 1)
                    nc.scalar.activation(h2T_hi[:, :, bass.ds(g * P, P)],
                                         PS[:, par, :].bitcast(fp16)[:, 0:DIM].rearrange("p (k n) -> p k n", k=KC),
                                         ACT.Copy).then_inc(hT_hi_r, 1)

                pairs(act, TILES, part)
                act.wait_ge(shifted, 2)
                nc.scalar.activation(ez[:, :, :], ez[:, :, :], ACT.Exp).then_inc(exp_r, 1)
                nc.scalar.activation(e8[:, :, :], e8[:, :, :], ACT.Exp).then_inc(exp_r, 1)

                def shared(q):
                    for j in range(SCH):
                        n = q * SCH + j
                        act.wait_ge(gu_done, n + 1)
                        wait(act, hf_r, n - 1)
                        nc.scalar.activation(silu[:, j % 2, :], PS[:, 2 * (j % 2), :], ACT.Silu,
                                             scale=1.0 / PROD).then_inc(silu_r, 1)
                        act.wait_ge(hf_r, n + 1)
                        wait(act, dn_done, q * GT)
                        nc.scalar.activation(hs_hi[:, j, :], hf[:, j % 2, :], ACT.Copy).then_inc(hs_hi_r, 1)
                    for c in range(GT):
                        g = q * GT + c
                        act.wait_ge(dn_done, g + 1)
                        wait(act, y_stored[c % 2], (g - c % 2) * 8)
                        nc.scalar.activation(ysh[:, c % 2, :], PS[:, 4 + c % 2, :], ACT.Copy,
                                             scale=1.0 / (H_SCALE * W_SCALE)).then_inc(y_r, 1)

                peeled(act, GROUP, shared)

            @block.tensor
            def _(pe):
                def turn(g, par):
                    pe.wait_ge(h2_lo, g + 1)
                    wait(pe, hT_lo_r, g - 1)
                    for s in range(2):
                        for k in range(KC):
                            last = nc.tensor.transpose(
                                PS[:, par, :].bitcast(fp16)[:, (s * KC + k) * P:(s * KC + k + 1) * P],
                                h2p[:, par, s, k * P:(k + 1) * P], ident16[:, :])
                    last.then_inc(hT_raw, 1)

                def route(g, par):
                    pe.wait_ge(hT_lo_r, g + 1)
                    wait(pe, logit_ready, g - 1)
                    for k in range(KC):
                        for m, (l, r) in enumerate(((h2T_hi, gt_w[0]), (h2T_hi, gt_w[1]), (h2T_lo, gt_w[0]))):
                            last = nc.tensor.matmul(PS[:, 2 + par, 0:EXPERTS], l[:, k, bass.ds(g * P, P)], r[:, k, :],
                                                    start=k == 0 and m == 0, stop=k == KC - 1 and m == 2)
                    last.then_inc(logit_done, 1)

                def both(g, par, first, last):
                    if first:
                        turn(g, par)
                    if not last:
                        turn(g + 1, 1 - par)
                    route(g, par)

                pe.wait_ge(w_lo, len(WEIGHTS))
                pairs(pe, TILES, both)
                pe.wait_ge(mask_r, 1)
                flat = mask[:, :, :].rearrange("p n e -> p (n e)")
                for m, bank in ((cb[:, 2, :], 4), (cb[:, 3, :], 6)):
                    for half_ in range(2):
                        nc.tensor.matmul(PS[:, bank + half_, :], m, flat[:, half_ * BANK:(half_ + 1) * BANK],
                                         start=True, stop=True).then_inc(count_done, 1)

                def shared(q):
                    for j in range(SCH):
                        n = q * SCH + j
                        wait(pe, hf_r, n - 1)
                        for bank, w in enumerate((sg_w, su_w)):
                            for k in range(KC):
                                cols = slice(j * P, (j + 1) * P)
                                toks = bass.ds(q * GT * P, GT * P)
                                for m, (l, r) in enumerate(((w[0], h2T_hi), (w[0], h2T_lo), (w[1], h2T_hi))):
                                    last = nc.tensor.matmul(PS[:, 2 * (j % 2) + bank, :], l[:, k, cols],
                                                            r[:, k, toks], start=k == 0 and m == 0,
                                                            stop=k == KC - 1 and m == 2)
                        last.then_inc(gu_done, 1)
                    pe.wait_ge(hs_lo_r, (q + 1) * SCH)
                    pe.wait_ge(pos_read, 1)
                    for c in range(GT):
                        wait(pe, y_r, q * GT + c - 1)
                        for j in range(SCH):
                            for m, (l, r) in enumerate(((hs_hi, sd_w[0]), (hs_hi, sd_w[1]), (hs_lo, sd_w[0]))):
                                last = nc.tensor.matmul(PS[:, 4 + c % 2, :], l[:, j, c * P:(c + 1) * P], r[:, j, :],
                                                        start=j == 0 and m == 0, stop=j == SCH - 1 and m == 2)
                        last.then_inc(dn_done, 1)

                peeled(pe, GROUP, shared)

            @block.vector
            def _(dve):
                nc.vector.memset(zeros[:, :], 0.0).then_inc(zero_set, 1)
                for n, (_, parts, k, width) in enumerate(WEIGHTS):
                    dve.wait_ge(w_hi, n + 1)
                    nc.vector.scalar_tensor_tensor(parts[1][:, k, :], stage[:, n % 2, 0:width], W_SCALE,
                                                   parts[0][:, k, :], ALU.mult, ALU.subtract).then_inc(w_lo, 1)
                dve.wait_ge(mod2_loaded, 16 * BATCH)

                def normed(g, par, b):
                    wait(dve, h2_ready, g - 1)
                    nc.vector.tensor_scalar(z[:, par, :], x1[:, bass.ds(g, 1), :].rearrange("p a d -> p (a d)"),
                                            stat2[:, bass.ds(g, 1), 0], stat2[:, bass.ds(g, 1), 1],
                                            ALU.subtract, ALU.mult).then_inc(z_ready, 1)
                    dve.wait_ge(z_ready, g + 1)
                    nc.vector.tensor_tensor(z[:, par, :], z[:, par, :], mod2[:, b, 1, :], ALU.mult).then_inc(zm_ready, 1)

                def part(g, par, first):
                    dve.wait_ge(h2_hi, g + 1)
                    nc.vector.scalar_tensor_tensor(h2p[:, par, 1, :], h2[:, par, :], ACT_SCALE, h2p[:, par, 0, :],
                                                   ALU.mult, ALU.subtract).then_inc(h2_lo, 1)
                    dve.wait_ge(hT_hi_r, g + 1)
                    nc.vector.tensor_copy(
                        h2T_lo[:, :, bass.ds(g * P, P)],
                        PS[:, par, :].bitcast(fp16)[:, DIM:2 * DIM].rearrange("p (k n) -> p k n", k=KC)
                        ).then_inc(hT_lo_r, 1)
                    if not first:
                        keep_logits(g - 1, 1 - par)

                def keep_logits(g, par):
                    dve.wait_ge(logit_done, g + 1)
                    nc.vector.tensor_scalar(logits[:, bass.ds(g, 1), :].rearrange("p a e -> p (a e)"),
                                            PS[:, 2 + par, 0:EXPERTS], 1.0 / PROD, None,
                                            ALU.mult).then_inc(logit_ready, 1)

                def both(g, par, first, last, b):
                    if first and b == 0:
                        normed(g, par, b)
                    if not last:
                        normed(g + 1, 1 - par, b)
                    elif b < BATCH - 1:
                        normed(g + 1, 1 - par, b + 1)
                    part(g, par, first and b == 0)

                for b in range(BATCH):
                    pairs(dve, BT, lambda g, par, first, last: both(g, par, first, last, b), b * BT)
                keep_logits(TILES - 1, 1)
                dve.wait_ge(logit_ready, TILES)

                linked = [0]

                def link(ins):
                    linked[0] += 1
                    ins.then_inc(rt, 1)
                    dve.wait_ge(rt, linked[0])

                for g in range(TILES):
                    link(nc.vector.max(top8[:, g, :], logits[:, g, :]))
                for g in range(TILES):
                    link(nc.vector.max_index(top8i[:, g, :], top8[:, g, :], logits[:, g, :]))
                best = top8[:, :, 0:1]
                nc.vector.tensor_tensor(ez[:, :, :], logits[:, :, :], best.broadcast_to([P, TILES, EXPERTS]),
                                        ALU.subtract).then_inc(shifted, 1)
                nc.vector.tensor_tensor(e8[:, :, :], top8[:, :, :], best.broadcast_to([P, TILES, 8]),
                                        ALU.subtract).then_inc(shifted, 1)
                link(nc.vector.tensor_copy(idx[:, :, :], top8i[:, :, :]))
                kshape = [P, TILES, TOPK, EXPERTS]
                iota = const("iota").unsqueeze(1).unsqueeze(1).broadcast_to(kshape)
                chosen = idx[:, :, 0:TOPK].unsqueeze(3).broadcast_to(kshape)
                link(nc.vector.tensor_tensor(onehot[:, :, :, :], iota, chosen, ALU.is_equal))
                nc.vector.tensor_reduce(mask[:, :, :], onehot[:, :, :, :].rearrange("p n k e -> p n e k"), AX.X,
                                        ALU.max).then_inc(mask_r, 1)
                dve.wait_ge(exp_r, 2)
                link(nc.vector.tensor_reduce(sums[:, 0, :], ez[:, :, :], AX.X, ALU.add))
                link(nc.vector.reciprocal(sums[:, 1, :], sums[:, 0, :]))
                link(nc.vector.tensor_tensor(e8[:, :, :], e8[:, :, :],
                                             sums[:, 1, :].unsqueeze(2).broadcast_to([P, TILES, 8]), ALU.mult))
                link(nc.vector.tensor_reduce(sums[:, 2, :], e8[:, :, 0:TOPK], AX.X, ALU.add))
                link(nc.vector.tensor_scalar(sums[:, 2, :], sums[:, 2, :], 1e-20, None, ALU.add))
                link(nc.vector.reciprocal(sums[:, 3, :], sums[:, 2, :]))
                link(nc.vector.scalar_tensor_tensor(
                    pair[:, :, :, 1].bitcast(fp32), e8[:, :, 0:TOPK], 1.0 / (H_SCALE * W_SCALE),
                    sums[:, 3, :].unsqueeze(2).broadcast_to([P, TILES, TOPK]), ALU.mult, ALU.mult))
                link(nc.vector.tensor_copy(pair[:, :, :, 0],
                                           const("token").unsqueeze(2).broadcast_to([P, TILES, TOPK])))
                link(nc.vector.memset(keep[:, :, :], 1.0))
                link(nc.vector.memset(keep[:, :, 0:1], 0.0))
                dve.wait_ge(count_done, 4)
                link(nc.vector.tensor_copy(total[:, :, :], PS[:, 6:8, :].rearrange("p a (n e) -> p e (a n)", e=EXPERTS)))
                flat = "p e n -> p (e n)"
                link(nc.vector.tensor_tensor_scan(cum[:, :, :].rearrange(flat), keep[:, :, :].rearrange(flat),
                                                  total[:, :, :].rearrange(flat), 0.0, ALU.mult, ALU.add))
                link(nc.vector.tensor_reduce(sums[:, 0, 0:1], cum[:, :, TILES - 1], AX.X, ALU.max))
                link(nc.vector.tensor_scalar(overflow[:, :], sums[:, 0, 0:1], float(MAIN_TILES * P), None, ALU.is_gt))
                link(nc.vector.tensor_tensor(cum[:, :, :], cum[:, :, :], total[:, :, :], ALU.subtract))
                nc.vector.tensor_tensor(pos[:, :, :], PS[:, 4:6, :].rearrange("p a (n e) -> p (a n) e", e=EXPERTS),
                                        cum[:, :, :].rearrange("p e n -> p n e"), ALU.add).then_inc(pos_read, 1)
                dve.wait_ge(pos_read, 1)
                step_back = float(1 - EXPERTS * SLOT_TILES * P)
                link(nc.vector.scalar_tensor_tensor(row[:, :, :], pos[:, :, :], float(EXPERTS * SLOT_TILES),
                                                    const("slot0").unsqueeze(1).broadcast_to([P, TILES, EXPERTS]),
                                                    ALU.mult, ALU.add))
                for edge, value in ((P, step_back), (2 * P, step_back), (CAP, DROPPED)):
                    link(nc.vector.tensor_scalar(term[:, :, :], pos[:, :, :], float(edge), value, ALU.is_ge,
                                                 ALU.mult))
                    link(nc.vector.tensor_tensor(row[:, :, :], row[:, :, :], term[:, :, :], ALU.add))
                for k in range(TOPK):
                    link(nc.vector.tensor_tensor(term[:, :, :], onehot[:, :, k, :], row[:, :, :], ALU.mult))
                    link(nc.vector.tensor_reduce(rowk[:, :, k], term[:, :, :], AX.X, ALU.add))
                nc.vector.tensor_copy(row_i[:, :], rowk[:, :, :].rearrange("p n k -> p (n k)")).then_inc(pairs_ready, 1)

                def shared(q):
                    for j in range(SCH):
                        n = q * SCH + j
                        dve.wait_ge(silu_r, n + 1)
                        wait(dve, hs_lo_r, n - 1)
                        nc.vector.scalar_tensor_tensor(hf[:, j % 2, :], PS[:, 2 * (j % 2) + 1, :], H_SCALE / PROD,
                                                       silu[:, j % 2, :], ALU.mult, ALU.mult).then_inc(hf_r, 1)
                        dve.wait_ge(hs_hi_r, n + 1)
                        nc.vector.tensor_tensor(hs_lo[:, j, :], hf[:, j % 2, :], hs_hi[:, j, :],
                                                ALU.subtract).then_inc(hs_lo_r, 1)

                peeled(dve, GROUP, shared)

            @block.gpsimd
            def _(pool):
                pool.wait_ge(mod2_loaded, 16 * BATCH)

                def shift(g, par, b):
                    pool.wait_ge(zm_ready, g + 1)
                    wait(pool, h2_lo, g - 1)
                    nc.gpsimd.tensor_tensor(h2[:, par, :], z[:, par, :], mod2[:, b, 0, :], ALU.add).then_inc(h2_ready, 1)

                for b in range(BATCH):
                    pairs(pool, BT, lambda g, par, first, last: shift(g, par, b), b * BT)
                pool.wait_ge(slots_set, 16)
                pool.wait_ge(pairs_ready, 1)
                for n in range(TILES * TOPK):
                    nc.gpsimd.indirect_dma_start(
                        out=slots_d, out_offset=bass.IndirectOffsetOnAxis(ap=row_i[:, n:n + 1], axis=0),
                        in_=pair[:, n // TOPK, n % TOPK, :], in_offset=None, bounds_check=EXPERTS * CAP - 1,
                        oob_is_err=False).then_inc(scattered, 16)
                pool.wait_ge(scattered, 16 * TILES * TOPK)

        up_shape, dn_shape = [P, 2, KC, 2 * FF], [P, 2, FCH, DIM]
        with ExitStack() as st:
            def sb(name, shape, dt):
                return st.enter_context(nc.sbuf_tensor(name, shape, dt))

            raw_up, raw_dn = sb("raw_up", up_shape, fp32), sb("raw_dn", dn_shape, fp32)
            up_hi, up_lo = sb("up_hi", up_shape, fp16), sb("up_lo", up_shape, fp16)
            dn_hi, dn_lo = sb("dn_hi", dn_shape, fp16), sb("dn_lo", dn_shape, fp16)
            slots = sb("slots", [P, EXPERTS * SLOT_TILES, 2], i32)
            from_row = sb("from_row", [P, 2, MAIN_TILES], i32)
            to_row = sb("to_row", [P, 2, MAIN_TILES], i32)
            xg = sb("xg", [P, 2, MAIN_TILES, 2 * KC, P], fp16)
            xT = sb("xT", [P, 2, 2 * KC, MAIN_TILES, P], fp16)
            silu = sb("silu5", [P, FCH, MAIN_TILES * P], fp32)
            hf = sb("hf5", [P, FCH, MAIN_TILES * P], fp32)
            h_hi = sb("h_hi", [P, 2, FCH, MAIN_TILES * P], fp16)
            h_lo = sb("h_lo", [P, 2, FCH, MAIN_TILES * P], fp16)
            y = sb("y", [P, 2, MAIN_TILES, DIM], fp32)
            WIDTH = [min(P, FF - j * P) for j in range(FCH)]
            HALVES = 2
            KH = KC // HALVES
            UP_BANK, DN_BANK, X_BANK = 0, FCH, FCH + MAIN_TILES

            def expert_pass(tiles, tag, rare):
                NT = len(tiles)
                N = NT * P
                with ExitStack() as ps:
                    names = ("slots_in rows_set ru_a ru_b rd_a rd_b xg_a xg_b add_a add_b turned x_even x_odd up_hi_r up_lo_r "
                             "dn_hi_r dn_lo_r gu_done silu_r hf_r h_hi_r h_lo_r dn_done y_r").split()
                    (slots_in, rows_set, ru_a, ru_b, rd_a, rd_b, xg_a, xg_b, add_a, add_b, turned, x_even, x_odd, up_hi_r,
                     up_lo_r, dn_hi_r, dn_lo_r, gu_done, silu_r, hf_r, h_hi_r, h_lo_r, dn_done, y_r) = sems(
                        ps, " ".join(n + tag for n in names))
                    up_loaded, dn_loaded, gathered, added = (ru_a, ru_b), (rd_a, rd_b), (xg_a, xg_b), (add_a, add_b)
                    block = ps.enter_context(nc.Block())

                    def all_of(e, par):
                        return (e - par) * 8 * NT + 16 * NT

                    def guarded(engine, body):
                        if not rare:
                            body()
                        else:
                            late = engine.value_load(overflow[0:1, 0:1], min_val=0, max_val=1)
                            with engine.If(late > 0):
                                body()

                    def weight_of(e, c):
                        return slots[:, bass.ds(e * SLOT_TILES + c, 1), 1].bitcast(fp32)

                    def weights_of(e, lo, hi):
                        return t["experts"][bass.ds(e, 1), :, lo:hi].rearrange("a p n -> (a p) n")

                    def x_out(e, par, i):
                        return (xT[:, par, :, i, :],
                                PS[:, X_BANK + i, :].bitcast(fp16).rearrange("p (k n) -> p k n", k=2 * KC))

                    @block.sync
                    def _(sp):
                        def load(e, par, first, last):
                            wait(sp, up_lo_r, (e - 1) * HALVES)
                            sp.dma_start(raw_up[:, par, :, :].rearrange("p k n -> p (k n)"),
                                         weights_of(e, 0, UP)).then_inc(up_loaded[par], 16)
                            wait(sp, dn_lo_r, e - 1)
                            sp.dma_start(raw_dn[:, par, :, :].rearrange("p k n -> p (k n)"),
                                         weights_of(e, UP, UP + DOWN)).then_inc(dn_loaded[par], 16)

                        guarded(sp, lambda: pairs(sp, EXPERTS, load))

                    @block.gpsimd
                    def _(pool):
                        def rows(to, e, par, count):
                            nc.gpsimd.tensor_copy(to[:, par, 0:NT], slots[:, bass.ds(e * SLOT_TILES + tiles[0], NT), 0]
                                                  ).then_inc(rows_set, 1)
                            pool.wait_ge(rows_set, count)
                            pool.sem_inc(tick, 1)

                        def gather(e, par, count):
                            wait(pool, turned, (e - 1) * NT)
                            pool.sem_inc(tick, 1)
                            rows(from_row, e, par, count)
                            for i, c in enumerate(tiles):
                                nc.gpsimd.indirect_dma_start(
                                    out=xg[:, par, i, :, :].rearrange("p k n -> p (k n)"), out_offset=None, in_=h2_d,
                                    in_offset=bass.IndirectOffsetOnAxis(
                                        ap=from_row[:, par, i:i + 1], axis=0)
                                ).then_inc(gathered[par], 16)

                        def low_parts(e, par):
                            for j in range(FCH):
                                pool.wait_ge(h_hi_r, e * FCH + j + 1)
                                nc.gpsimd.tensor_tensor(h_lo[0:WIDTH[j], par, j, 0:N], hf[0:WIDTH[j], j, 0:N],
                                                        h_hi[0:WIDTH[j], par, j, 0:N],
                                                        ALU.subtract).then_inc(h_lo_r, 1)

                        def add(e, par, count):
                            wait(pool, added[1 - par], all_of(e - 1, 1 - par))
                            pool.sem_inc(tick, 1)
                            rows(to_row, e, par, count)
                            pool.wait_ge(y_r, (e + 1) * NT)
                            pool.sem_inc(tick, 1)
                            for i, c in enumerate(tiles):
                                nc.gpsimd.indirect_dma_start(
                                    out=y_d, out_offset=bass.IndirectOffsetOnAxis(
                                        ap=to_row[:, par, i:i + 1], axis=0),
                                    in_=y[:, par, i, :], in_offset=None, compute_op=ALU.add,
                                    bounds_check=TOK + CAP - 1, oob_is_err=True).then_inc(added[par], 16)

                        def turn(e, par, first, last):
                            if first:
                                gather(e, par, 1)
                                gather(e + 1, 1 - par, 2)
                            if not isinstance(e, int) or e + 2 < EXPERTS:
                                gather(e + 2, par, e * 2 + 2 + (1 if first else 0))
                            low_parts(e, par)
                            if not first:
                                late = max(0, e + 3 - EXPERTS) if isinstance(e, int) else 0
                                add(e - 1, 1 - par, e * 2 + 3 - late)

                        def body():
                            pool.wait_ge(slots_in, 16)
                            pairs(pool, EXPERTS, turn)
                            add(EXPERTS - 1, 1, 2 * EXPERTS)
                            for par in range(2):
                                pool.wait_ge(added[par], 8 * NT * EXPERTS)

                        guarded(pool, body)

                    @block.tensor
                    def _(pe):
                        def turn_x(e, par, i):
                            pe.wait_ge(gathered[par], all_of(e, par))
                            wait(pe, (x_even, x_odd)[i], e)
                            for k in range(2 * KC):
                                last = nc.tensor.transpose(x_out(e, par, i)[1][:, k, :], xg[:, par, i, k, :],
                                                           ident16[:, :])
                            last.then_inc(turned, 1)

                        def up(e, par, j):
                            w = WIDTH[j]
                            wait(pe, hf_r, e * FCH + j + 1 - FCH)
                            for side in range(2):
                                cols = slice(side * FF + j * P, side * FF + j * P + w)
                                for k in range(KC):
                                    for m, (l, r) in enumerate(((up_hi, k), (up_hi, KC + k), (up_lo, k))):
                                        last = nc.tensor.matmul(
                                            PS[0:w, UP_BANK + j, side * N:(side + 1) * N], l[:, par, k, cols],
                                            xT[:, par, r, 0:NT, :],
                                            start=k == 0 and m == 0, stop=k == KC - 1 and m == 2)
                            last.then_inc(gu_done, 1)

                        def down(e, par):
                            pe.wait_ge(h_lo_r, (e + 1) * FCH)
                            pe.wait_ge(dn_lo_r, e + 1)
                            for i in range(NT):
                                wait(pe, y_r, (e - 1) * NT + i + 1)
                                for j in range(FCH):
                                    w = WIDTH[j]
                                    for m, (l, r) in enumerate(((h_hi, dn_hi), (h_hi, dn_lo), (h_lo, dn_hi))):
                                        last = nc.tensor.matmul(PS[:, DN_BANK + i, :],
                                                                l[0:w, par, j, i * P:(i + 1) * P], r[0:w, par, j, :],
                                                                start=j == 0 and m == 0, stop=j == FCH - 1 and m == 2)
                                last.then_inc(dn_done, 1)

                        def turn(e, par, first, last):
                            if first:
                                for i in range(NT):
                                    turn_x(e, par, i)
                            pe.wait_ge(x_even, e + 1)
                            if NT > 1:
                                pe.wait_ge(x_odd, e + 1)
                            pe.wait_ge(up_lo_r, (e + 1) * HALVES)
                            for j in range(FCH):
                                up(e, par, j)
                                if j < NT and not last:
                                    turn_x(e + 1, 1 - par, j)
                            if not first:
                                down(e - 1, 1 - par)

                        def body():
                            pairs(pe, EXPERTS, turn)
                            down(EXPERTS - 1, 1)

                        guarded(pe, body)

                    @block.scalar
                    def _(act):
                        act.dma_start(slots[:, :, :].rearrange("p n w -> p (n w)"), slots_d.rearrange("(p n) w -> p (n w)", p=P)).then_inc(slots_in, 16)

                        def x_part(e, par):
                            act.wait_ge(turned, e * NT + 1)
                            to, src = x_out(e, par, 0)
                            nc.scalar.activation(to, src, ACT.Copy).then_inc(x_even, 1)

                        def up_part(e, par, half):
                            act.wait_ge(up_loaded[par], loads(e, par))
                            ks = slice(half * KH, (half + 1) * KH)
                            nc.scalar.activation(up_hi[:, par, ks, :], raw_up[:, par, ks, :], ACT.Copy,
                                                 scale=W_SCALE).then_inc(up_hi_r, 1)

                        def gate(e, par, j):
                            n, w = e * FCH + j, WIDTH[j]
                            act.wait_ge(gu_done, n + 1)
                            wait(act, hf_r, n + 1 - FCH)
                            nc.scalar.activation(silu[0:w, j, 0:N], PS[0:w, UP_BANK + j, 0:N], ACT.Silu,
                                                 scale=1.0 / PROD).then_inc(silu_r, 1)

                        def h_part(e, par, j):
                            act.wait_ge(hf_r, e * FCH + j + 1)
                            nc.scalar.activation(h_hi[0:WIDTH[j], par, j, 0:N], hf[0:WIDTH[j], j, 0:N],
                                                 ACT.Copy).then_inc(h_hi_r, 1)

                        def weigh(e, par):
                            wait(act, added[par], all_of(e - 2, par))
                            for i, c in enumerate(tiles):
                                act.wait_ge(dn_done, e * NT + i + 1)
                                nc.scalar.activation(
                                    y[:, par, i, :], PS[:, DN_BANK + i, :], ACT.Copy,
                                    scale=weight_of(e, c)).then_inc(y_r, 1)

                        def dn_part(e, par):
                            act.wait_ge(dn_loaded[par], loads(e, par))
                            nc.scalar.activation(dn_hi[:, par, :, :], raw_dn[:, par, :, :], ACT.Copy,
                                                 scale=W_SCALE).then_inc(dn_hi_r, 1)

                        def turn(e, par, first, last):
                            if first:
                                x_part(e, par)
                                for half in range(HALVES):
                                    up_part(e, par, half)
                            if not last:
                                up_part(e + 1, 1 - par, 0)
                            gate(e, par, 0)
                            if not last:
                                x_part(e + 1, 1 - par)
                                up_part(e + 1, 1 - par, 1)
                            gate(e, par, 1)
                            h_part(e, par, 0)
                            dn_part(e, par)
                            gate(e, par, 2)
                            h_part(e, par, 1)
                            h_part(e, par, 2)
                            if not first:
                                weigh(e - 1, 1 - par)

                        def body():
                            act.wait_ge(slots_in, 16)
                            pairs(act, EXPERTS, turn)
                            weigh(EXPERTS - 1, 1)

                        if rare:
                            act.wait_ge(slots_in, 16)
                        guarded(act, body)

                    @block.vector
                    def _(dve):
                        def x_part(e, par):
                            if NT > 1:
                                dve.wait_ge(turned, e * NT + 2)
                                to, src = x_out(e, par, 1)
                                nc.vector.tensor_copy(to, src).then_inc(x_odd, 1)

                        def up_part(e, par, half):
                            dve.wait_ge(up_hi_r, e * HALVES + half + 1)
                            flat, ks = "p k n -> p (k n)", slice(half * KH, (half + 1) * KH)
                            nc.vector.scalar_tensor_tensor(up_lo[:, par, ks, :].rearrange(flat),
                                                           raw_up[:, par, ks, :].rearrange(flat), W_SCALE,
                                                           up_hi[:, par, ks, :].rearrange(flat), ALU.mult,
                                                           ALU.subtract).then_inc(up_lo_r, 1)

                        def hidden(e, par, j):
                            n, w = e * FCH + j, WIDTH[j]
                            dve.wait_ge(silu_r, n + 1)
                            wait(dve, h_lo_r, n + 1 - FCH)
                            nc.vector.scalar_tensor_tensor(hf[0:w, j, 0:N], PS[0:w, UP_BANK + j, N:2 * N],
                                                           H_SCALE / PROD, silu[0:w, j, 0:N],
                                                           ALU.mult, ALU.mult).then_inc(hf_r, 1)

                        def dn_part(e, par):
                            dve.wait_ge(dn_hi_r, e + 1)
                            flat = "p k n -> p (k n)"
                            nc.vector.scalar_tensor_tensor(dn_lo[:, par, :, :].rearrange(flat),
                                                           raw_dn[:, par, :, :].rearrange(flat), W_SCALE,
                                                           dn_hi[:, par, :, :].rearrange(flat), ALU.mult,
                                                           ALU.subtract).then_inc(dn_lo_r, 1)

                        def turn(e, par, first, last):
                            if first:
                                x_part(e, par)
                                for half in range(HALVES):
                                    up_part(e, par, half)
                            if not last:
                                up_part(e + 1, 1 - par, 0)
                            hidden(e, par, 0)
                            hidden(e, par, 1)
                            if not last:
                                x_part(e + 1, 1 - par)
                                up_part(e + 1, 1 - par, 1)
                            dn_part(e, par)
                            hidden(e, par, 2)

                        guarded(dve, lambda: pairs(dve, EXPERTS, turn))

            expert_pass(range(MAIN_TILES), "_m", False)
            expert_pass(range(MAIN_TILES, SLOT_TILES), "_r", True)

        with ExitStack() as st:
            def sb(name, shape, dt):
                return st.enter_context(nc.sbuf_tensor(name, shape, dt))

            gate2 = sb("gate2", [P, BATCH, DIM], fp32)
            yin = sb("yin", [P, TILES, DIM], fp32)
            STEPS = 4
            PER = TILES // STEPS
            yin_loaded = sems(st, " ".join(f"yin{n}" for n in range(STEPS)))
            gate2_loaded, scaled, done, stored = sems(st, "gate2_loaded scaled6 done6 stored6")
            block = st.enter_context(nc.Block())

            @block.sync
            def _(sp):
                for n in range(STEPS):
                    sp.dma_start(yin[:, n * PER:(n + 1) * PER, :],
                                 y_d[n * PER * P:(n + 1) * PER * P, :].rearrange("(n p) d -> p n d", p=P)
                                 ).then_inc(yin_loaded[n], 16)

            @block.scalar
            def _(act):
                for b in range(BATCH):
                    act.dma_start(gate2[:, b, :], mod_d[b:b + 1, 5 * DIM:6 * DIM].partition_broadcast(P)
                                  .rearrange("p a d -> p (a d)")).then_inc(gate2_loaded, 16)
                for n in range(STEPS):
                    act.wait_ge(done, (n + 1) * PER)
                    act.dma_start(t["out"][n * PER * P:(n + 1) * PER * P, :].rearrange("(n p) d -> p n d", p=P),
                                  x1[:, n * PER:(n + 1) * PER, :]).then_inc(stored, 16)
                act.wait_ge(stored, 16 * STEPS)

            @block.vector
            def _(dve):
                dve.wait_ge(gate2_loaded, 16 * BATCH)
                for n in range(TILES):
                    dve.wait_ge(yin_loaded[n // PER], 16)
                    nc.vector.tensor_tensor(yin[:, n, :], yin[:, n, :], gate2[:, n // BT, :], ALU.mult
                                            ).then_inc(scaled, 1)
                    dve.wait_ge(scaled, n + 1)
                    nc.vector.tensor_tensor(x1[:, n, :], x1[:, n, :], yin[:, n, :], ALU.add).then_inc(done, 1)


_OUT = (BATCH, SEQ, DIM)


def laid_out(inputs):
    def split(w, chunks):
        return np.ascontiguousarray(w.reshape(chunks, P, -1).transpose(1, 0, 2))

    def padded(w, rows):
        return np.concatenate([w, np.zeros((rows - w.shape[0], w.shape[1]), w.dtype)], 0)

    a = {k[3:]: np.asarray(v) for k, v in inputs.items()}
    wg = a["ffn_w_gate"].transpose(0, 2, 1).reshape(EXPERTS, KC, P, 1, FF)
    wu = a["ffn_w_up"].transpose(0, 2, 1).reshape(EXPERTS, KC, P, 1, FF)
    up = np.concatenate([wg, wu], 3).transpose(0, 2, 1, 3, 4).reshape(EXPERTS, P, UP)
    wd = a["ffn_w_down"].transpose(0, 2, 1)
    wd = np.concatenate([wd, np.zeros((EXPERTS, FCH * P - FF, DIM), wd.dtype)], 1)
    down = wd.reshape(EXPERTS, FCH, P, DIM).transpose(0, 2, 1, 3).reshape(EXPERTS, P, DOWN)
    return {
        "x": np.ascontiguousarray(a["attn_x"].reshape(TOK, DIM)),
        "c": np.ascontiguousarray(a["c"].T.reshape(KC, P, BATCH).transpose(1, 0, 2).reshape(P, KC * BATCH)),
        "wmod": split(a["wmod"], KC),
        "wqkv": split(a["attn_Wqkv"], KC),
        "wo": split(a["attn_Wo"], KC),
        "gate": split(a["ffn_gate_w"].T, KC),
        "sh_gate": split(padded(a["ffn_sh_gate"], SCH * P).T, KC),
        "sh_up": split(padded(a["ffn_sh_up"], SCH * P).T, KC),
        "sh_down": split(padded(a["ffn_sh_down"].T, SCH * P), SCH),
        "experts": np.ascontiguousarray(np.concatenate([up, down], 2)),
        "consts": constants(),
        "slots": empty_slots(),
    }


def kernel(**inputs):
    import concourse.bacc as bacc
    from concourse.bass_utils import run_bass_kernel_spmd

    nc = bacc.Bacc("TRN2", target_bir_lowering=False, num_devices=1)
    arrays = laid_out(inputs)
    t = {k: nc.dram_tensor("in_" + k, v.shape, mybir.dt.from_np(v.dtype), kind="ExternalInput").ap()
         for k, v in arrays.items()}
    t["out"] = nc.dram_tensor("out", (TOK, DIM), mybir.dt.float32, kind="ExternalOutput").ap()
    adaln_program(nc, t)
    r = run_bass_kernel_spmd(nc, [{"in_" + k: v for k, v in arrays.items()}], core_ids=[0])
    return r.results[0]["out"].reshape(_OUT)
```

```python
import math
from contextlib import ExitStack

import numpy as np

import concourse.bass as bass
from concourse import mybir

P = 128
BATCH, SEQ, DIM = 2, 1024, 512
TOK = BATCH * SEQ
TILES = TOK // P
BT = SEQ // P
KC = DIM // P
HEADS, HD = 16, 32
QK_ROWS = 3 * HD
SUMMED = 2 * HD + 1
VW = SUMMED + 1
EXPERTS, TOPK = 64, 6
CAP = 2 * ((TOK * TOPK + EXPERTS - 1) // EXPERTS)
SLOT_TILES = CAP // P
MAIN_TILES = SLOT_TILES - 1
FF = 352
FCH = (FF + P - 1) // P
SH = 704
SCH = (SH + P - 1) // P
SHP = SCH * P
FFN_AT = [KC * EXPERTS * (n > 0) + KC * SHP * max(0, n - 1) for n in range(4)]
FFN_COLS = FFN_AT[3] + SCH * DIM
FFN_STEP = FFN_COLS // TILES
assert FFN_STEP * TILES == FFN_COLS
UP = KC * 2 * FF
DOWN = FCH * DIM
EPS = 1e-5
BANK = 512
GT = 4

ACT_SCALE = 16.0
W_SCALE = 64.0
QKV_SCALE = 8.0
P_SCALE = 1024.0
H_SCALE = 4.0
PROD = ACT_SCALE * W_SCALE
MASKED = -1e30
DROPPED = float(1 << 20)

CONSTS = dict(ident=P, mask=P, tri=P, iota=EXPERTS, slot0=EXPERTS, cos=BT * HD, sin=BT * HD, token=TILES)


def columns():
    at, where = 0, {}
    for name, n in CONSTS.items():
        where[name] = (at, at + n)
        at += n
    return where, at


def constants():
    where, n = columns()
    c = np.zeros((P, n), np.float32)
    p, j = np.arange(P)[:, None], np.arange(P)[None, :]

    def put(name, value):
        c[:, where[name][0]:where[name][1]] = value

    put("ident", p == j)
    put("mask", np.where(j > p, MASKED, 0.0))
    put("tri", p < j)
    put("iota", np.arange(EXPERTS)[None, :])
    put("slot0", np.arange(EXPERTS)[None, :] * SLOT_TILES)
    i = np.arange(HD // 2, dtype=np.float32)
    inv = (np.float32(1.0) / np.float32(10000.0) ** (np.float32(2.0) * i / np.float32(HD))).astype(np.float32)
    th = np.arange(SEQ, dtype=np.float32)[:, None] * inv[None, :]
    s = np.float32(QKV_SCALE / PROD)
    cos = np.repeat(np.cos(th) * s, 2, 1)
    sin = np.repeat(np.sin(th) * s, 2, 1)
    sin[:, 0::2] *= -1
    for name, t in (("cos", cos), ("sin", sin)):
        put(name, t.reshape(BT, P, HD).transpose(1, 0, 2).reshape(P, BT * HD))
    put("token", np.arange(TILES)[None, :] * P + p)
    return c


def empty_slots():
    t = np.zeros((P, EXPERTS, SLOT_TILES, 2), np.int32)
    t[..., 0] = TOK + np.arange(P)[:, None, None] + P * np.arange(SLOT_TILES)[None, None, :]
    return t.reshape(EXPERTS * CAP, 2)


def wait(engine, sem, value):
    if not (isinstance(value, int) and value <= 0):
        engine.wait_ge(sem, value)


def pairs(engine, n, emit, base=0):
    emit(base, 0, True, False)
    emit(base + 1, 1, False, False)
    with engine.Fori(1, n // 2 - 1) as m:
        emit(m * 2 + base, 0, False, False)
        emit(m * 2 + base + 1, 1, False, False)
    emit(base + n - 2, 0, False, False)
    emit(base + n - 1, 1, False, True)


def g_known(g):
    return g if isinstance(g, int) else None


def peeled(engine, n, emit):
    emit(0)
    with engine.Fori(1, n) as m:
        emit(m)


def loads(g, par):
    return (g - par) * 8 + 16


def adaln_program(nc, t):
    fp32, fp16, bf16 = mybir.dt.float32, mybir.dt.float16, mybir.dt.bfloat16
    i32, u32 = mybir.dt.int32, mybir.dt.uint32
    ALU, ACT, AX = mybir.AluOpType, mybir.ActivationFunctionType, mybir.AxisListType
    where, n_const = columns()
    top = ExitStack()
    with top:
        PS = top.enter_context(nc.psum_tensor("PS", [P, 8, BANK], fp32))

        def sems(stack, names):
            made = [nc.alloc_semaphore(n) for n in names.split()]
            stack.callback(nc.all_engine_barrier)
            stack.callback(nc.clear_and_free_semaphores, made)
            return made

        consts = top.enter_context(nc.sbuf_tensor("consts", [P, n_const], fp32))

        def const(name):
            return consts[:, where[name][0]:where[name][1]]

        ident32 = const("ident")
        cb = top.enter_context(nc.sbuf_tensor("cb", [P, 4, P], bf16))
        ident16 = top.enter_context(nc.sbuf_tensor("ident16", [P, P], fp16))
        stat1 = top.enter_context(nc.sbuf_tensor("stat1", [P, TILES, 2], fp32))
        mod_d = nc.dram_tensor("mod_d", [BATCH, 6 * DIM], fp32).ap()
        overflow = top.enter_context(nc.sbuf_tensor("overflow", [P, 1], i32))
        (tick,) = sems(top, "tick")

        stat2 = top.enter_context(nc.sbuf_tensor("stat2", [P, TILES, 2], fp32))

        def deviation(dve, raw6, small, stat, step, root):
            me, qe, mo, qo = (raw6[:, :, c] for c in (1, 2, 4, 5))
            nc.vector.tensor_tensor(small[:, 0, :], me, mo, ALU.add).then_inc(step, 1)
            nc.vector.tensor_tensor(small[:, 1, :], me, mo, ALU.subtract).then_inc(step, 1)
            nc.vector.tensor_tensor(small[:, 2, :], qe, qo, ALU.add).then_inc(step, 1)
            dve.wait_ge(step, 3)
            nc.vector.tensor_scalar(stat[:, :, 0], small[:, 0, :], 0.5, None, ALU.mult).then_inc(step, 1)
            nc.vector.scalar_tensor_tensor(small[:, 5, :], small[:, 1, :], 0.25, small[:, 1, :],
                                           ALU.mult, ALU.mult).then_inc(step, 1)
            nc.vector.tensor_scalar(small[:, 6, :], small[:, 2, :], 1.0 / DIM, EPS,
                                    ALU.mult, ALU.add).then_inc(step, 1)
            dve.wait_ge(step, 6)
            nc.vector.tensor_tensor(small[:, 3, :], small[:, 5, :], small[:, 6, :], ALU.add).then_inc(step, 1)
            dve.wait_ge(root, 1)
            nc.vector.reciprocal(small[:, 5, :], small[:, 4, :]).then_inc(step, 1)
            dve.wait_ge(step, 8)
            nc.vector.tensor_tensor(small[:, 6, :], small[:, 5, :], small[:, 5, :], ALU.mult).then_inc(step, 1)
            dve.wait_ge(step, 9)
            nc.vector.scalar_tensor_tensor(small[:, 7, :], small[:, 6, :], -0.5, small[:, 3, :],
                                           ALU.mult, ALU.mult).then_inc(step, 1)
            dve.wait_ge(step, 10)
            nc.vector.scalar_tensor_tensor(stat[:, :, 1], small[:, 7, :], 1.5, small[:, 5, :],
                                           ALU.add, ALU.mult).then_inc(step, 1)

        s2 = ExitStack()
        wqkv_hi = s2.enter_context(nc.sbuf_tensor("wqkv_hi", [P, KC, 3 * DIM], fp16))
        wqkv_lo = s2.enter_context(nc.sbuf_tensor("wqkv_lo", [P, KC, 3 * DIM], fp16))
        with ExitStack() as st:
            def sb(name, shape, dt):
                return st.enter_context(nc.sbuf_tensor(name, shape, dt))

            c_in = sb("c_in", [P, KC * BATCH], fp32)
            c_silu = sb("c_silu", [P, KC, BATCH], fp32)
            wmod = sb("wmod", [P, KC, 6 * DIM], fp32)
            wqkv = sb("wqkv", [P, KC, 3 * DIM], fp32)
            xall = sb("xall", [P, TILES, DIM], fp32)
            rows = sb("rows", [BATCH, 6, DIM], fp32)
            sign = sb("sign", [BATCH, DIM], fp32)
            minus = sb("minus", [BATCH, DIM], fp32)
            size = sb("size", [BATCH, DIM], fp32)
            raw6 = sb("raw6", [P, TILES, 6], fp32)
            small = sb("small", [P, 8, TILES], fp32)
            wmod_loaded = sems(st, " ".join(f"wmod_loaded{g}" for g in range(6)))
            wqkv_loaded = sems(st, " ".join(f"wqkv_loaded{k}" for k in range(KC)))
            (c_loaded, const_loaded, x_loaded, c_ready, mod_done, row_ready, gate_step,
             rows_stored, cb_ready, wq_hi, wq_lo, stats, step, root) = sems(
                st, "c_loaded const_loaded x_loaded c_ready mod_done row_ready gate_step "
                    "rows_stored cb_ready wq_hi wq_lo stats step root")
            block = st.enter_context(nc.Block())

            @block.sync
            def _(sp):
                sp.dma_start(c_in[:, :], t["c"]).then_inc(c_loaded, 16)
                for g in range(6):
                    sp.dma_start(wmod[:, :, g * DIM:(g + 1) * DIM],
                                 t["wmod"][:, :, g * DIM:(g + 1) * DIM]).then_inc(wmod_loaded[g], 16)
                for k in range(KC):
                    sp.dma_start(wqkv[:, k, :], t["wqkv"][:, k, :]).then_inc(wqkv_loaded[k], 16)
                sp.wait_ge(row_ready, 6)
                sp.dma_start(mod_d, rows[:, :, :].rearrange("b s d -> b (s d)")).then_inc(rows_stored, 16)
                sp.wait_ge(rows_stored, 16)

            @block.scalar
            def _(act):
                act.dma_start(consts[:, :], t["consts"]).then_inc(const_loaded, 16)
                act.dma_start(xall[:, :, :], t["x"].rearrange("(n p) d -> p n d", p=P)).then_inc(x_loaded, 16)
                act.wait_ge(c_loaded, 16)
                nc.scalar.activation(c_silu[:, :, :].rearrange("p k b -> p (k b)"), c_in[:, :],
                                     ACT.Silu).then_inc(c_ready, 1)
                act.wait_ge(step, 7)
                nc.scalar.activation(small[:, 4, :], small[:, 3, :], ACT.Sqrt).then_inc(root, 1)
                for k in range(KC):
                    act.wait_ge(wqkv_loaded[k], 16)
                    nc.scalar.activation(wqkv_hi[:, k, :], wqkv[:, k, :], ACT.Copy,
                                         scale=W_SCALE).then_inc(wq_hi, 1)

            @block.tensor
            def _(pe):
                pe.wait_ge(c_ready, 1)
                for g in range(6):
                    pe.wait_ge(wmod_loaded[g], 16)
                    for k in range(KC):
                        last = nc.tensor.matmul(PS[0:BATCH, g, :], c_silu[:, k, :],
                                                wmod[:, k, g * DIM:(g + 1) * DIM], start=k == 0, stop=k == KC - 1)
                    last.then_inc(mod_done, 1)

            @block.vector
            def _(dve):
                dve.wait_ge(const_loaded, 16)
                nc.vector.tensor_copy(ident16[:, :], ident32).then_inc(cb_ready, 1)
                for n, name in enumerate(("ident", "mask", "tri")):
                    nc.vector.tensor_copy(cb[:, n, :], const(name)).then_inc(cb_ready, 1)
                nc.vector.memset(cb[:, 3, :], 1.0).then_inc(cb_ready, 1)
                dve.wait_ge(x_loaded, 16)
                with dve.Fori(0, TILES) as n:
                    nc.vector.bn_stats(raw6[:, bass.ds(n, 1), :], xall[:, bass.ds(n, 1), :]).then_inc(stats, 1)
                dve.wait_ge(stats, TILES)
                deviation(dve, raw6, small, stat1, step, root)
                gates = 0
                for g in range(6):
                    dve.wait_ge(mod_done, g + 1)
                    if g % 3 < 2:
                        nc.vector.tensor_scalar(rows[:, g, :], PS[0:BATCH, g, :], float(g % 3), None,
                                                ALU.add).then_inc(row_ready, 1)
                    else:
                        if gates:
                            dve.wait_ge(row_ready, g)
                        nc.vector.tensor_scalar(sign[:, :], PS[0:BATCH, g, :], 0.0, 2.0, ALU.is_ge,
                                                ALU.mult).then_inc(gate_step, 1)
                        nc.vector.tensor_scalar(minus[:, :], PS[0:BATCH, g, :], -1.0, None,
                                                ALU.mult).then_inc(gate_step, 1)
                        dve.wait_ge(gate_step, gates + 2)
                        nc.vector.scalar_tensor_tensor(size[:, :], PS[0:BATCH, g, :], 0.25, minus[:, :],
                                                       ALU.max, ALU.max).then_inc(gate_step, 1)
                        gates += 3
                        dve.wait_ge(gate_step, gates)
                        nc.vector.scalar_tensor_tensor(rows[:, g, :], sign[:, :], -1.0, size[:, :],
                                                       ALU.add, ALU.mult).then_inc(row_ready, 1)
                for k in range(KC):
                    dve.wait_ge(wq_hi, k + 1)
                    nc.vector.scalar_tensor_tensor(wqkv_lo[:, k, :], wqkv[:, k, :], W_SCALE, wqkv_hi[:, k, :],
                                                   ALU.mult, ALU.subtract).then_inc(wq_lo, 1)


        attn_d = nc.dram_tensor("attn_d", [TOK, DIM], fp32).ap()
        with s2:
            def sb(name, shape, dt):
                return s2.enter_context(nc.sbuf_tensor(name, shape, dt))

            QT = sb("QT", [QK_ROWS, HEADS, SEQ], fp16)
            KT = sb("KT", [QK_ROWS, HEADS, SEQ], fp16)
            V = sb("V", [P, BT, HEADS, VW], fp16)
            hT_hi = sb("hT_hi", [P, 2, KC, P], fp16)
            hT_lo = sb("hT_lo", [P, 2, KC, P], fp16)
            mod1 = sb("mod1", [P, BATCH, 2, DIM], fp32)
            xin = sb("xin", [P, 2, DIM], fp32)
            z = sb("z", [P, 2, DIM], fp32)
            h = sb("h", [P, 2, DIM], fp32)
            qk16 = sb("qk16", [P, 2, 2 * HEADS, 3, HD], fp16)
            O = sb("O", [P, BT, DIM], fp32)
            PT = sb("PT", [P, 4, SEQ], fp32)
            by_head = PT[:, :, :].rearrange("p s (h d) -> p s h d", d=HD)
            rot, qk = by_head[:, 0:2, :, :], by_head[:, 2, :, :]
            PT_hi = sb("PT_hi", [P, 4, BT, P], fp16)
            PT_lo = sb("PT_lo", [P, 4, BT, P], fp16)
            negmax = sb("negmax", [P, 4], fp32)
            dg_hi = sb("dg_hi", [P, 4, P], bf16)
            dg_lo = sb("dg_lo", [P, 4, P], bf16)
            p_bias = sb("p_bias", [P, 1], fp32)
            half = sb("half", [P, 2, BT // 2, HD], fp32)
            inv = sb("inv", [P, BT // 2], fp32)
            SCORE = 1.0 / (math.sqrt(HD) * QKV_SCALE * QKV_SCALE)
            ORDER = [p // 2 if p % 2 == 0 else BT - 1 - p // 2 for p in range(BT)]
            GROUPS = [[(0, ORDER[p] + 1)] if p % 2 == 0 else [(0, 4), (4, ORDER[p] + 1)] for p in range(BT)]
            GSTART = [sum(len(g) for g in GROUPS[:p]) for p in range(BT + 1)]
            GN = GSTART[BT]
            ST_BANK, PV_BANK = 3, 6
            H_BANK, QK_BANK = 6, 7
            LAG = 3

            (mod_in, xin_a, xin_b, set_up, z_ready, zm_ready, h_ready, hT_raw, hT_hi_ready, hT_lo_ready,
             qkv_done, cos_done, sin_done, v_hi_ready, v_lo_ready, qk_ready, qk_hi, qk_lo, parts_copied, qkT_done,
             q_copied, k_copied, s_done, max_done, dg_hi_set, dg_lo_set, st_done, exp_done, p_hi, p_lo_dve,
             p_lo_pool, pv_done, inv_done, half_done, o_done, o_stored) = sems(
                s2, "mod_in xin_a xin_b set_up z_ready zm_ready h_ready hT_raw hT_hi_ready hT_lo_ready qkv_done "
                    "cos_done sin_done v_hi_ready v_lo_ready qk_ready qk_hi qk_lo parts_copied qkT_done q_copied "
                    "k_copied s_done max_done dg_hi_set dg_lo_set st_done exp_done p_hi p_lo_dve p_lo_pool pv_done "
                    "inv_done half_done o_done o_stored")
            xin_loaded = (xin_a, xin_b)
            block = s2.enter_context(nc.Block())

            def heads(engine, b, step, tail=None):
                def head(hh, start, end):
                    for p in range(BT):
                        step(b * HEADS + hh, hh, p, start, end)

                head(0, True, False)
                head(1, False, False)
                with engine.Fori(2, HEADS - 1) as hh:
                    head(hh, False, False)
                head(HEADS - 1, False, True)
                if tail:
                    tail(b * HEADS + HEADS - 1, HEADS - 1)

            class Turn:
                def __init__(self, g, b):
                    tile = g - b * BT
                    self.known = tile if isinstance(tile, int) else None
                    self.before = self.known != 0
                    self.two_before = self.known not in (0, 1)
                    self.own = self.known is None or self.known < BT
                    self.after = self.known is None or self.known < BT - 1

            def projections(engine, b, emit):
                pairs(engine, BT, lambda g, par, first, last: emit(g, par, Turn(g, b)), b * BT)
                emit((b + 1) * BT, 0, Turn((b + 1) * BT, b))
                emit((b + 1) * BT + 1, 1, None)

            def shifted(H, hh, p, by):
                at = p + by
                return H + at // BT, hh + at // BT, at % BT

            @block.sync
            def _(sp):
                for b in range(BATCH):
                    sp.dma_start(mod1[:, b, :, :].rearrange("p s d -> p (s d)"),
                                 mod_d[b:b + 1, 0:2 * DIM].partition_broadcast(P)).then_inc(mod_in, 16)

                def load(g, par, first=False, last=False):
                    wait(sp, z_ready, g - 1)
                    sp.dma_start(xin[:, par, :], t["x"][bass.ds(g * P, P), :]).then_inc(xin_loaded[par], 16)

                load(0, 0)
                load(1, 1)
                for b in range(BATCH):
                    with sp.Fori(1, BT // 2) as m:
                        for par in range(2):
                            load(m * 2 + b * BT + par, par)
                    if b + 1 < BATCH:
                        load((b + 1) * BT, 0)
                        load((b + 1) * BT + 1, 1)
                    for p in range(BT):
                        if p % (BT // 2) == 0:
                            sp.wait_ge(o_done, (b + 1) * HEADS * 2 - 1 + p // (BT // 2))
                        at = b * SEQ + ORDER[p] * P
                        sp.dma_start(attn_d[at:at + P, :], O[:, p, :]).then_inc(o_stored, 16)
                sp.wait_ge(o_stored, 16 * BT * BATCH)

            def score_unit(pe, H, hh, p, first):
                if not first:
                    pe.wait_ge(max_done, H * BT + p - 1)
                i, bank = ORDER[p], p % 2
                s = PS[:, bank:bank + 2, :].rearrange("p a n -> p (a n)")
                q = QT[:, bass.ds(hh, 1), i * P:(i + 1) * P]
                for at in range(0, (i + 1) * P, BANK):
                    end = min(at + BANK, (i + 1) * P)
                    diagonal = end == (i + 1) * P
                    last = nc.tensor.matmul(s[:, at:end], q, KT[:, bass.ds(hh, 1), at:end],
                                            start=True, stop=not diagonal)
                    if diagonal:
                        last = nc.tensor.matmul(s[:, i * P:end], cb[:, 0, :], cb[:, 1, :], start=False, stop=True)
                last.then_inc(s_done, 1)

            def turned_unit(pe, H, hh, p, start):
                i = ORDER[p]
                pe.wait_ge(dg_lo_set, H * BT + p + 1)
                for n, (lo, hi) in enumerate(GROUPS[p]):
                    G = GSTART[p] + n
                    if not start or G >= 3:
                        pe.wait_ge(exp_done, H * GN + G - 2)
                    out = PS[:, ST_BANK + G % 3, 0:(hi - lo) * P]
                    for m, part in enumerate((dg_hi, dg_lo)):
                        nc.tensor.matmul(out.rearrange("p (j q) -> p j q", q=P), cb[:, 3, :],
                                         part[:, p % 4:p % 4 + 1, :].broadcast_to([P, hi - lo, P]),
                                         start=m == 0, stop=False)
                    for j in range(lo, hi):
                        block_of = out[:, (j - lo) * P:(j - lo + 1) * P]
                        last = nc.tensor.matmul(block_of, KT[:, bass.ds(hh, 1), j * P:(j + 1) * P].rearrange(
                                                "p a n -> p (a n)"), QT[:, bass.ds(hh, 1), i * P:(i + 1) * P],
                                                start=False, stop=j == hi - 1 and j < i)
                        if j == i:
                            last = nc.tensor.matmul(block_of, cb[:, 1, :], cb[:, 0, :], start=False, stop=True)
                    last.then_inc(st_done, 1)

            def value_unit(pe, H, hh, p, first_head):
                pe.wait_ge(p_lo_pool, H * BT + p + 1)
                if p % 2:
                    pe.wait_ge(p_lo_dve, H * (BT // 2) + p // 2 + 1)
                side = p // (BT // 2)
                if p % (BT // 2) == 0 and not first_head:
                    pe.wait_ge(half_done, 2 * (2 * H + side - 1))
                at = p % (BT // 2) * SUMMED
                for j in range(ORDER[p] + 1):
                    for part in (PT_hi, PT_lo):
                        last = nc.tensor.matmul(
                            PS[:, PV_BANK + side, at:at + SUMMED], part[:, p % 4, j, :],
                            V[:, j, bass.ds(hh, 1), 0:SUMMED].rearrange("p h s -> p (h s)"),
                            start=j == 0 and part is PT_hi, stop=j == ORDER[p] and part is PT_lo)
                last.then_inc(pv_done, 1)

            @block.tensor
            def _(pe):
                def turn_h(g, par):
                    pe.wait_ge(h_ready, g + 1)
                    wait(pe, hT_lo_ready, g)
                    for k in range(KC):
                        done = nc.tensor.transpose(PS[:, H_BANK, k * P:(k + 1) * P], h[:, par, k * P:(k + 1) * P],
                                                   ident32)
                    done.then_inc(hT_raw, 1)

                def turn_qk(g, par, quarter):
                    if quarter == 0:
                        pe.wait_ge(parts_copied, 2 * (g + 1))
                        pe.wait_ge(qk_lo, 2 * (g + 1))
                        wait(pe, k_copied, 2 * g)
                    elif quarter == 3:
                        pe.wait_ge(k_copied, 2 * g + 1)
                    else:
                        pe.wait_ge(q_copied, 2 * g + quarter)
                    bank = PS[:, QK_BANK, :].bitcast(fp16)
                    for n in range(8):
                        last = nc.tensor.transpose(bank[0:QK_ROWS, n * P:(n + 1) * P],
                                                   qk16[:, par, quarter * 8 + n, :, :].rearrange("p s d -> p (s d)"),
                                                   ident16[:, :])
                    last.then_inc(qkT_done, 1)

                def project(g, par, between):
                    pe.wait_ge(hT_lo_ready, g + 1)
                    wait(pe, sin_done, 2 * (g - 1))
                    wait(pe, v_lo_ready, g - 1)
                    for n in range(3):
                        for k in range(KC):
                            lhs_hi, lhs_lo = hT_hi[:, par, k, :], hT_lo[:, par, k, :]
                            cols = slice(n * DIM, (n + 1) * DIM)
                            for m, (l, r) in enumerate(((lhs_hi, wqkv_hi), (lhs_hi, wqkv_lo), (lhs_lo, wqkv_hi))):
                                last = nc.tensor.matmul(PS[:, 3 * par + n, :], l, r[:, k, cols],
                                                        start=k == 0 and m == 0, stop=k == KC - 1 and m == 2)
                            if k == 1:
                                between(2 * n)
                        if n < 2:
                            between(2 * n + 1)
                    last.then_inc(qkv_done, 1)

                for b in range(BATCH):
                    def project_turn(g, par, turn):
                        def between(n):
                            if n < 4:
                                if turn.two_before:
                                    turn_qk(g - 2, par, n)
                            elif turn.after:
                                turn_h(g + 1, 1 - par)

                        if turn is not None and turn.own:
                            project(g, par, between)
                        else:
                            for quarter in range(4):
                                turn_qk(g - 2, par, quarter)

                    def step(H, hh, p, start, end):
                        if not (end and p + 2 >= BT):
                            score_unit(pe, *shifted(H, hh, p, 2), False)
                        turned_unit(pe, H, hh, p, start)
                        if not (start and p < LAG):
                            H2, hh2, p2 = shifted(H, hh, p, -LAG)
                            value_unit(pe, H2, hh2, p2, start)

                    def tail(H, hh):
                        for p in range(BT - LAG, BT):
                            value_unit(pe, H, hh, p, False)

                    turn_h(b * BT, 0)
                    projections(pe, b, project_turn)
                    pe.wait_ge(q_copied, 2 * BT * (b + 1))
                    pe.wait_ge(k_copied, 2 * BT * (b + 1))
                    for p in range(2):
                        score_unit(pe, b * HEADS, 0, p, True)
                    heads(pe, b, step, tail)

            @block.scalar
            def _(act):
                def hT_part(g, par):
                    act.wait_ge(hT_raw, g + 1)
                    wait(act, qkv_done, g - 1)
                    nc.scalar.activation(hT_hi[:, par, :, :].rearrange("p k n -> p (k n)"), PS[:, H_BANK, :],
                                         ACT.Copy, scale=ACT_SCALE).then_inc(hT_hi_ready, 1)

                def v_part(g, par, b):
                    act.wait_ge(qkv_done, g + 1)
                    nc.scalar.activation(V[:, bass.ds(g - b * BT, 1), :, 0:HD],
                                         PS[:, 3 * par + 2, :].rearrange("p (h d) -> p h d", h=HEADS),
                                         ACT.Copy, scale=QKV_SCALE / PROD).then_inc(v_hi_ready, 1)

                def qk_part(g, par):
                    act.wait_ge(qk_ready, g + 1)
                    wait(act, qkT_done, 4 * (g - 1))
                    nc.scalar.activation(qk16[:, par, :, 0, :], qk, ACT.Copy).then_inc(qk_hi, 1)

                def q_out(g, b):
                    for quarter in range(2):
                        act.wait_ge(qkT_done, 4 * g + quarter + 1)
                        nc.scalar.activation(
                            QT[:, quarter * 8:quarter * 8 + 8, bass.ds((g - b * BT) * P, P)],
                            PS[0:QK_ROWS, QK_BANK, :].bitcast(fp16).rearrange("p (h n) -> p h n", h=8),
                            ACT.Copy).then_inc(q_copied, 1)

                def step(H, hh, p, start, end):
                    for n, (lo, hi) in enumerate(GROUPS[p]):
                        G = GSTART[p] + n
                        act.wait_ge(st_done, H * GN + G + 1)
                        if n == 0 and not (start and p < 4):
                            act.wait_ge(p_lo_pool, H * BT + p - 3)
                            if p % 2:
                                act.wait_ge(p_lo_dve, H * (BT // 2) + p // 2 - 1)
                        nc.scalar.activation(PT[:, p % 4, lo * P:hi * P], PS[:, ST_BANK + G % 3, 0:(hi - lo) * P],
                                             ACT.Exp, bias=p_bias[:, :], scale=SCORE).then_inc(exp_done, 1)
                    if not (start and p < 4):
                        act.wait_ge(pv_done, H * BT + p - 3)
                    act.wait_ge(exp_done, H * GN + GSTART[p + 1])
                    cols = (ORDER[p] + 1) * P
                    nc.scalar.activation(PT_hi[:, p % 4, 0:ORDER[p] + 1, :].rearrange("p j n -> p (j n)"),
                                         PT[:, p % 4, 0:cols], ACT.Copy).then_inc(p_hi, 1)

                for b in range(BATCH):
                    def project_turn(g, par, turn):
                        if turn is None:
                            q_out(g - 2, b)
                            return
                        if turn.before:
                            v_part(g - 1, 1 - par, b)
                        if turn.two_before:
                            q_out(g - 2, b)
                        if turn.before:
                            qk_part(g - 1, 1 - par)
                        if turn.after:
                            hT_part(g + 1, 1 - par)

                    hT_part(b * BT, 0)
                    projections(act, b, project_turn)
                    if b == 0:
                        act.wait_ge(set_up, 2)
                    heads(act, b, step)

            def take_low(engine, ops, p, lo, hi, sem):
                ops.tensor_tensor(PT_lo[:, p % 4, lo:hi, :].rearrange("p j n -> p (j n)"), PT[:, p % 4, lo * P:hi * P],
                                  PT_hi[:, p % 4, lo:hi, :].rearrange("p j n -> p (j n)"),
                                  ALU.subtract).then_inc(sem, 1)

            @block.vector
            def _(dve):
                nc.vector.memset(p_bias[:, :], math.log(P_SCALE)).then_inc(set_up, 1)
                nc.vector.memset(V[:, :, :, 2 * HD:VW], QKV_SCALE).then_inc(set_up, 1)
                dve.wait_ge(mod_in, 16 * BATCH)

                def max_unit(H, p):
                    dve.wait_ge(s_done, H * BT + p + 1)
                    s = PS[:, p % 2:p % 2 + 2, :].rearrange("p a n -> p (a n)")
                    nc.vector.tensor_reduce(negmax[:, p % 4:p % 4 + 1], s[:, 0:(ORDER[p] + 1) * P], AX.X, ALU.max,
                                            negate=True).then_inc(max_done, 1)

                def diagonal_low(H, p):
                    dve.wait_ge(dg_hi_set, H * BT + p + 1)
                    nc.vector.scalar_tensor_tensor(dg_lo[:, p % 4, :], ident32, negmax[:, p % 4:p % 4 + 1],
                                                   dg_hi[:, p % 4, :], ALU.mult, ALU.subtract).then_inc(dg_lo_set, 1)

                def low(H, p):
                    if p % 2:
                        dve.wait_ge(p_hi, H * BT + p + 1)
                        take_low(dve, nc.vector, p, *GROUPS[p][0], p_lo_dve)

                def final(H, side, first):
                    dve.wait_ge(pv_done, H * BT + (side + 1) * (BT // 2))
                    if not first:
                        dve.wait_ge(o_done, 2 * H + side)
                    o = PS[:, PV_BANK + side, 0:(BT // 2) * SUMMED].rearrange("p (i s) -> p i s", s=SUMMED)
                    nc.vector.reciprocal(inv[:, :], o[:, :, 2 * HD]).then_inc(inv_done, 1)
                    dve.wait_ge(inv_done, 2 * H + side + 1)
                    for s in range(2):
                        nc.vector.tensor_tensor(half[:, s, :, :], o[:, :, s * HD:(s + 1) * HD],
                                                inv[:, :].unsqueeze(2).broadcast_to([P, BT // 2, HD]),
                                                ALU.mult).then_inc(half_done, 1)

                def step(H, hh, p, start, end):
                    if not (end and p + 1 >= BT):
                        H1, _, p1 = shifted(H, hh, p, 1)
                        diagonal_low(H1, p1)
                    if not (end and p + 2 >= BT):
                        H2, _, p2 = shifted(H, hh, p, 2)
                        max_unit(H2, p2)
                    if not (start and p < 1):
                        H1, _, p1 = shifted(H, hh, p, -1)
                        low(H1, p1)
                    if p == LAG and not start:
                        final(H - 1, 1, False)
                    if p == BT // 2 + LAG:
                        final(H, 0, start)

                def tail(H, hh):
                    low(H, BT - 1)
                    final(H, 1, False)

                for b in range(BATCH):
                    def normed(g, par):
                        dve.wait_ge(xin_loaded[par], loads(g, par))
                        wait(dve, h_ready, g - 1)
                        nc.vector.tensor_scalar(z[:, par, :], xin[:, par, :], stat1[:, bass.ds(g, 1), 0],
                                                stat1[:, bass.ds(g, 1), 1], ALU.subtract,
                                                ALU.mult).then_inc(z_ready, 1)
                        dve.wait_ge(z_ready, g + 1)
                        nc.vector.tensor_tensor(z[:, par, :], z[:, par, :], mod1[:, b, 1, :],
                                                ALU.mult).then_inc(zm_ready, 1)

                    def low_h(g, par):
                        dve.wait_ge(hT_hi_ready, g + 1)
                        nc.vector.scalar_tensor_tensor(
                            hT_lo[:, par, :, :].rearrange("p k n -> p (k n)"), PS[:, H_BANK, :], ACT_SCALE,
                            hT_hi[:, par, :, :].rearrange("p k n -> p (k n)"),
                            ALU.mult, ALU.subtract).then_inc(hT_lo_ready, 1)

                    def rotated(g, par):
                        tile = g - b * BT
                        dve.wait_ge(qkv_done, g + 1)
                        wait(dve, qk_ready, g)
                        x = PS[:, 3 * par:3 * par + 2, :].rearrange("p a (h d) -> p (a h) d", d=HD)
                        cos, sin = (const(c).rearrange("p (n d) -> p n d", d=HD)[:, bass.ds(tile, 1), :]
                                    .broadcast_to([P, 2 * HEADS, HD]) for c in ("cos", "sin"))
                        nc.vector.tensor_tensor(rot[:, 0, :, :], x, cos, ALU.mult).then_inc(cos_done, 1)
                        for a in range(2):
                            nc.vector.tensor_tensor(rot[:, 1, :, a::2], x[:, :, 1 - a::2], sin[:, :, a::2],
                                                    ALU.mult).then_inc(sin_done, 1)
                        dve.wait_ge(v_hi_ready, g + 1)
                        nc.vector.scalar_tensor_tensor(
                            V[:, bass.ds(tile, 1), :, HD:2 * HD],
                            PS[:, 3 * par + 2, :].rearrange("p (h d) -> p h d", h=HEADS), QKV_SCALE / PROD,
                            V[:, bass.ds(tile, 1), :, 0:HD], ALU.mult, ALU.subtract).then_inc(v_lo_ready, 1)

                    def copy_parts(g, par):
                        dve.wait_ge(qk_hi, g + 1)
                        for of, to in ((slice(0, HEADS), 2), (slice(HEADS, 2 * HEADS), 1)):
                            nc.vector.tensor_copy(qk16[:, par, of, to, :],
                                                  qk16[:, par, of, 0, :]).then_inc(parts_copied, 1)

                    def k_out(g):
                        for quarter in range(2):
                            dve.wait_ge(qkT_done, 4 * g + quarter + 3)
                            nc.vector.tensor_copy(
                                KT[:, quarter * 8:quarter * 8 + 8, bass.ds((g - b * BT) * P, P)],
                                PS[0:QK_ROWS, QK_BANK, :].bitcast(fp16).rearrange("p (h n) -> p h n", h=8),
                                ).then_inc(k_copied, 1)

                    def project_turn(g, par, turn):
                        if turn is None:
                            k_out(g - 2)
                            return
                        if turn.before:
                            rotated(g - 1, 1 - par)
                        if turn.after:
                            normed(g + 1, 1 - par)
                        if turn.two_before:
                            k_out(g - 2)
                        if turn.before:
                            copy_parts(g - 1, 1 - par)
                        if turn.after:
                            low_h(g + 1, 1 - par)

                    normed(b * BT, 0)
                    low_h(b * BT, 0)
                    projections(dve, b, project_turn)
                    max_unit(b * HEADS, 0)
                    max_unit(b * HEADS, 1)
                    diagonal_low(b * HEADS, 0)
                    heads(dve, b, step, tail)

            @block.gpsimd
            def _(pool):
                def diagonal(H, p, first):
                    pool.wait_ge(max_done, H * BT + p + 1)
                    if not first:
                        pool.wait_ge(st_done, H * GN + (GSTART[p - 3] if p >= 4 else GSTART[BT + p - 3] - GN))
                    nc.gpsimd.tensor_tensor(dg_hi[:, p % 4, :], ident32, negmax[:, p % 4:p % 4 + 1]
                                            .broadcast_to([P, P]), ALU.mult).then_inc(dg_hi_set, 1)

                def low(H, p):
                    pool.wait_ge(p_hi, H * BT + p + 1)
                    take_low(pool, nc.gpsimd, p, *GROUPS[p][-1], p_lo_pool)

                def weigh(H, hh, side):
                    pool.wait_ge(half_done, 2 * (2 * H + side + 1))
                    pool.sem_inc(tick, 1)
                    nc.gpsimd.tensor_tensor(O[:, side * (BT // 2):(side + 1) * (BT // 2), bass.ds(hh * HD, HD)],
                                            half[:, 0, :, :], half[:, 1, :, :], ALU.add).then_inc(o_done, 1)

                def step(H, hh, p, start, end):
                    if not (end and p + 2 >= BT):
                        H2, _, p2 = shifted(H, hh, p, 2)
                        diagonal(H2, p2, start and p < 2)
                    if not (start and p < 1):
                        H1, _, p1 = shifted(H, hh, p, -1)
                        low(H1, p1)
                    if p == LAG and not start:
                        weigh(H - 1, hh - 1, 1)
                    if p == BT // 2 + LAG:
                        weigh(H, hh, 0)

                def tail(H, hh):
                    low(H, BT - 1)
                    weigh(H, hh, 1)

                pool.wait_ge(mod_in, 16 * BATCH)
                for b in range(BATCH):
                    def shift(g, par):
                        pool.wait_ge(zm_ready, g + 1)
                        wait(pool, hT_raw, g - 1)
                        nc.gpsimd.tensor_tensor(h[:, par, :], z[:, par, :], mod1[:, b, 0, :],
                                                ALU.add).then_inc(h_ready, 1)

                    def project_turn(g, par, turn):
                        if turn is None:
                            return
                        if turn.before:
                            pool.wait_ge(sin_done, 2 * g)
                            wait(pool, qk_lo, 2 * (g - 1))
                            nc.gpsimd.tensor_tensor(qk, rot[:, 0, :, :], rot[:, 1, :, :],
                                                    ALU.add).then_inc(qk_ready, 1)
                        if turn.after:
                            shift(g + 1, 1 - par)
                        if turn.before:
                            pool.wait_ge(qk_hi, g)
                            for of, to in ((slice(0, HEADS), 1), (slice(HEADS, 2 * HEADS), 2)):
                                nc.gpsimd.tensor_tensor(qk16[:, 1 - par, of, to, :], qk[:, of, :],
                                                        qk16[:, 1 - par, of, 0, :], ALU.subtract).then_inc(qk_lo, 1)

                    shift(b * BT, 0)
                    projections(pool, b, project_turn)
                    if b:
                        pool.wait_ge(o_stored, b * BT * 16)
                    diagonal(b * HEADS, 0, True)
                    diagonal(b * HEADS, 1, True)
                    heads(pool, b, step, tail)

        x1 = top.enter_context(nc.sbuf_tensor("x1", [P, TILES, DIM], fp32))
        s4 = ExitStack()
        mod2 = s4.enter_context(nc.sbuf_tensor("mod2", [P, BATCH, 2, DIM], fp32))
        ffn_w = [s4.enter_context(nc.sbuf_tensor("ffn_w" + c, [P, FFN_COLS], fp16)) for c in ("_hi", "_lo")]
        with ExitStack() as st:
            def sb(name, shape, dt):
                return st.enter_context(nc.sbuf_tensor(name, shape, dt))

            wo = sb("wo", [P, KC, DIM], fp32)
            wo_hi = sb("wo_hi", [P, KC, DIM], fp16)
            wo_lo = sb("wo_lo", [P, KC, DIM], fp16)
            gate1 = sb("gate1", [P, BATCH, DIM], fp32)
            oin = sb("oin", [P, 2, DIM], fp32)
            oT_hi = sb("oT_hi", [P, 2, KC, P], fp16)
            oT_lo = sb("oT_lo", [P, 2, KC, P], fp16)
            gated = sb("gated", [P, 2, DIM], fp32)
            raw6 = sb("raw6b", [P, TILES, 6], fp32)
            small = sb("smallb", [P, 8, TILES], fp32)
            ffn_raw = sb("ffn_raw", [P, TILES, FFN_STEP], fp32)
            (wo_loaded, mod2_loaded, gate1_loaded, oin_0, oin_1, x_0, x_1, wo_hi_ready, wo_lo_ready, oT_raw,
             oT_hi_ready, oT_lo_ready, out_done, gated_ready, x1_ready, raw_0, raw_1, ffn_hi, ffn_lo, stats, step, root) = sems(
                st, "wo_loaded mod2_loaded gate1_loaded oin_0 oin_1 x_0 x_1 wo_hi_ready wo_lo_ready oT_raw oT_hi_ready "
                    "oT_lo_ready out_done gated_ready x1_ready raw_0 raw_1 ffn_hi ffn_lo stats3 step3 root3")
            oin_loaded, x_loaded, raw_loaded = (oin_0, oin_1), (x_0, x_1), (raw_0, raw_1)
            block = st.enter_context(nc.Block())

            @block.sync
            def _(sp):
                sp.dma_start(wo[:, :, :], t["wo"]).then_inc(wo_loaded, 16)

                def load(g, par):
                    wait(sp, oT_raw, g - 1)
                    sp.dma_start(oin[:, par, :], attn_d[bass.ds(g * P, P), :]).then_inc(oin_loaded[par], 16)

                def residual(b):
                    sp.dma_start(x1[:, b * BT:(b + 1) * BT, :],
                                 t["x"][b * SEQ:(b + 1) * SEQ, :].rearrange("(n p) d -> p n d", p=P)
                                 ).then_inc(x_loaded[b], 16)

                def weights(b):
                    sp.dma_start(ffn_raw[:, b * BT:(b + 1) * BT, :].rearrange("p n c -> p (n c)"),
                                 t["ffn"][:, b * BT * FFN_STEP:(b + 1) * BT * FFN_STEP]).then_inc(raw_loaded[b], 16)

                load(0, 0)
                load(1, 1)
                residual(0)
                weights(0)
                with sp.Fori(1, BT // 2 - 1) as m:
                    load(m * 2, 0)
                    load(m * 2 + 1, 1)
                residual(1)
                load(BT - 2, 0)
                weights(1)
                load(BT - 1, 1)
                with sp.Fori(BT // 2, TILES // 2) as m:
                    load(m * 2, 0)
                    load(m * 2 + 1, 1)

            @block.scalar
            def _(act):
                for b in range(BATCH):
                    act.dma_start(gate1[:, b, :], mod_d[b:b + 1, 2 * DIM:3 * DIM].partition_broadcast(P)
                                  .rearrange("p a d -> p (a d)")).then_inc(gate1_loaded, 16)
                for b in range(BATCH):
                    act.dma_start(mod2[:, b, :, :].rearrange("p s d -> p (s d)"),
                                  mod_d[b:b + 1, 3 * DIM:5 * DIM].partition_broadcast(P)
                                  .rearrange("p a d -> p (a d)")).then_inc(mod2_loaded, 16)
                act.wait_ge(wo_loaded, 16)
                nc.scalar.activation(wo_hi[:, :, :], wo[:, :, :], ACT.Copy, scale=W_SCALE).then_inc(wo_hi_ready, 1)

                def part(g, par):
                    act.wait_ge(oT_raw, g + 1)
                    wait(act, out_done, g - 1)
                    nc.scalar.activation(oT_hi[:, par, :, :].rearrange("p k n -> p (k n)"), PS[:, par, :], ACT.Copy,
                                         scale=ACT_SCALE).then_inc(oT_hi_ready, 1)

                def weights_hi(g, b):
                    act.wait_ge(raw_loaded[b], 16)
                    nc.scalar.activation(ffn_w[0][:, bass.ds(g * FFN_STEP, FFN_STEP)],
                                         ffn_raw[:, bass.ds(g, 1), :].rearrange("p a c -> p (a c)"), ACT.Copy,
                                         scale=W_SCALE).then_inc(ffn_hi, 1)

                def turn(g, par, b):
                    part(g, par)
                    if g_known(g) != 0 and g_known(g) != 1:
                        weights_hi(g - 2, b - 1 if g_known(g) in (BT, BT + 1) else b)

                for b in range(BATCH):
                    pairs(act, BT, lambda g, par, first, last: turn(g, par, b), b * BT)
                for g in (TILES - 2, TILES - 1):
                    weights_hi(g, BATCH - 1)
                act.wait_ge(step, 7)
                nc.scalar.activation(small[:, 4, :], small[:, 3, :], ACT.Sqrt).then_inc(root, 1)
                act.wait_ge(mod2_loaded, 16 * BATCH)

            @block.tensor
            def _(pe):
                def turn(g, par):
                    pe.wait_ge(oin_loaded[par], loads(g, par))
                    wait(pe, oT_lo_ready, g - 1)
                    for k in range(KC):
                        last = nc.tensor.transpose(PS[:, par, k * P:(k + 1) * P], oin[:, par, k * P:(k + 1) * P],
                                                   ident32)
                    last.then_inc(oT_raw, 1)

                def project(g, par):
                    pe.wait_ge(oT_lo_ready, g + 1)
                    wait(pe, gated_ready, g - 1)
                    for k in range(KC):
                        for m, (l, r) in enumerate(((oT_hi, wo_hi), (oT_hi, wo_lo), (oT_lo, wo_hi))):
                            last = nc.tensor.matmul(PS[:, 2 + par, :], l[:, par, k, :], r[:, k, :],
                                                    start=k == 0 and m == 0, stop=k == KC - 1 and m == 2)
                    last.then_inc(out_done, 1)

                def both(g, par, first, last):
                    if first and g == 0:
                        turn(g, par)
                    if not (last and g == TILES - 1):
                        turn(g + 1, 1 - par)
                    if first and g == 0:
                        pe.wait_ge(wo_lo_ready, 1)
                    project(g, par)

                for b in range(BATCH):
                    pairs(pe, BT, both, b * BT)

            @block.vector
            def _(dve):
                dve.wait_ge(wo_hi_ready, 1)
                nc.vector.scalar_tensor_tensor(wo_lo[:, :, :].rearrange("p k d -> p (k d)"),
                                               wo[:, :, :].rearrange("p k d -> p (k d)"), W_SCALE,
                                               wo_hi[:, :, :].rearrange("p k d -> p (k d)"),
                                               ALU.mult, ALU.subtract).then_inc(wo_lo_ready, 1)
                dve.wait_ge(gate1_loaded, 16 * BATCH)

                def part(g, par):
                    dve.wait_ge(oT_hi_ready, g + 1)
                    nc.vector.scalar_tensor_tensor(oT_lo[:, par, :, :].rearrange("p k n -> p (k n)"), PS[:, par, :],
                                                   ACT_SCALE, oT_hi[:, par, :, :].rearrange("p k n -> p (k n)"),
                                                   ALU.mult, ALU.subtract).then_inc(oT_lo_ready, 1)

                def weights_lo(g):
                    dve.wait_ge(ffn_hi, g + 1)
                    nc.vector.scalar_tensor_tensor(ffn_w[1][:, bass.ds(g * FFN_STEP, FFN_STEP)],
                                                   ffn_raw[:, bass.ds(g, 1), :].rearrange("p a c -> p (a c)"),
                                                   W_SCALE, ffn_w[0][:, bass.ds(g * FFN_STEP, FFN_STEP)],
                                                   ALU.mult, ALU.subtract).then_inc(ffn_lo, 1)

                def both(g, par, first, last, b):
                    if first and b == 0:
                        part(g, par)
                    if not (last and b == BATCH - 1):
                        part(g + 1, 1 - par)
                    dve.wait_ge(out_done, g + 1)
                    wait(dve, x1_ready, g - 1)
                    nc.vector.scalar_tensor_tensor(gated[:, par, :], PS[:, 2 + par, :], 1.0 / PROD, gate1[:, b, :],
                                                   ALU.mult, ALU.mult).then_inc(gated_ready, 1)
                    if g_known(g) != 0 and g_known(g) != 1:
                        weights_lo(g - 2)
                    if not (first and b == 0):
                        dve.wait_ge(x1_ready, g)
                        nc.vector.bn_stats(raw6[:, bass.ds(g - 1, 1), :], x1[:, bass.ds(g - 1, 1), :]
                                           ).then_inc(stats, 1)

                for b in range(BATCH):
                    pairs(dve, BT, lambda g, par, first, last: both(g, par, first, last, b), b * BT)
                weights_lo(TILES - 2)
                weights_lo(TILES - 1)
                dve.wait_ge(x1_ready, TILES)
                nc.vector.bn_stats(raw6[:, TILES - 1, :], x1[:, TILES - 1, :]).then_inc(stats, 1)
                dve.wait_ge(stats, TILES)
                deviation(dve, raw6, small, stat2, step, root)

            @block.gpsimd
            def _(pool):
                def add(g, par):
                    pool.wait_ge(gated_ready, g + 1)
                    pool.sem_inc(tick, 1)
                    nc.gpsimd.tensor_tensor(x1[:, bass.ds(g, 1), :], gated[:, par:par + 1, :],
                                            x1[:, bass.ds(g, 1), :],
                                            ALU.add).then_inc(x1_ready, 1)

                for b in range(BATCH):
                    pool.wait_ge(x_loaded[b], 16)
                    pairs(pool, BT, lambda g, par, first, last: add(g, par), b * BT)

        h2_d = nc.dram_tensor("h2_d", [TOK + CAP, 2 * DIM], fp16).ap()
        y_d = nc.dram_tensor("y_d", [TOK + CAP, DIM], fp32).ap()
        slots_d = nc.dram_tensor("slots_d", [EXPERTS * CAP, 2], i32).ap()
        with ExitStack() as st:
            def sb(name, shape, dt):
                return st.enter_context(nc.sbuf_tensor(name, shape, dt))

            h2T_hi = sb("h2T_hi", [P, KC, TOK], fp16)
            h2T_lo = sb("h2T_lo", [P, KC, TOK], fp16)
            gt_w, sg_w, su_w, sd_w = (
                [w[:, at:at + k * n].rearrange("p (k n) -> p k n", k=k) for w in ffn_w]
                for at, k, n in zip(FFN_AT, (KC, KC, KC, SCH), (EXPERTS, SHP, SHP, DIM)))
            zeros = sb("zeros", [P, DIM], fp32)
            z = sb("z2", [P, 2, DIM], fp32)
            h2 = sb("h2", [P, 2, DIM], fp32)
            h2p = sb("h2p", [P, 2, 2, DIM], fp16)
            logits = sb("logits", [P, TILES, EXPERTS], fp32)
            top8 = sb("top8", [P, TILES, 8], fp32)
            top8i = sb("top8i", [P, TILES, 8], u32)
            idx = sb("idx", [P, TILES, 8], fp32)
            e8 = sb("e8", [P, TILES, 8], fp32)
            ez = sb("ez", [P, TILES, EXPERTS], fp32)
            sums = sb("sums", [P, 4, TILES], fp32)
            onehot = sb("onehot", [P, TILES, TOPK, EXPERTS], bf16)
            mask = sb("mask", [P, TILES, EXPERTS], bf16)
            total = sb("total", [P, EXPERTS, TILES], fp32)
            keep = sb("keep", [P, EXPERTS, TILES], fp32)
            cum = sb("cum", [P, EXPERTS, TILES], fp32)
            pos, row = ez, logits
            term = sb("term", [P, TILES, EXPERTS], fp32)
            rowk = sb("rowk", [P, TILES, TOPK], fp32)
            row_i = sb("row_i", [P, TILES * TOPK], i32)
            pair = sb("pair", [P, TILES, TOPK, 2], i32)
            silu = sb("silu", [P, 2, GT * P], fp32)
            hf = sb("hf", [P, 2, GT * P], fp32)
            hs_hi = sb("hs_hi", [P, SCH, GT * P], fp16)
            hs_lo = sb("hs_lo", [P, SCH, GT * P], fp16)
            ysh = sb("ysh", [P, 2, DIM], fp32)
            (slots_set, pad_stored, zero_set, z_ready, zm_ready, h2_ready, h2_hi, h2_lo, h2s_a, h2s_b, hT_raw, hT_hi_r,
             hT_lo_r, logit_done, logit_ready, rt, keep_set, shifted, mask_r, counts_out, exp_r, count_done, pairs_ready,
             scattered, gu_done, silu_r, hf_r, hs_hi_r, hs_lo_r, dn_done, y_r, ys_a, ys_b) = sems(
                st, "slots_set pad_stored zero_set z_ready4 zm_ready4 h2_ready h2_hi h2_lo h2s_a h2s_b hT_raw4 hT_hi_r "
                    "hT_lo_r logit_done logit_ready rt keep_set shifted mask_r counts_out exp_r count_done pairs_ready "
                    "scattered gu_done silu_r hf_r hs_hi_r hs_lo_r dn_done y_r ys_a ys_b")
            h2_stored, y_stored = (h2s_a, h2s_b), (ys_a, ys_b)
            GROUP = TILES // GT
            EXP_AT, COUNT_AT = 1, 5
            block = st.enter_context(nc.Block())

            @block.sync
            def _(sp):
                sp.dma_start(slots_d, t["slots"]).then_inc(slots_set, 16)
                sp.wait_ge(zero_set, 1)
                for n in range(SLOT_TILES):
                    for d, zero in ((h2_d, zeros[:, :].bitcast(fp16)), (y_d, zeros[:, :])):
                        sp.dma_start(d[TOK + n * P:TOK + (n + 1) * P, :], zero).then_inc(pad_stored, 16)

                def store_h2(g, par):
                    sp.wait_ge(h2_lo, g + 1)
                    sp.dma_start(h2_d[bass.ds(g * P, P), :], h2p[:, par, :, :].rearrange("p s d -> p (s d)")
                                 ).then_inc(h2_stored[par], 16)

                def store_y(g, par):
                    sp.wait_ge(y_r, g + 1)
                    sp.dma_start(y_d[bass.ds(g * P, P), :], ysh[:, par, :]).then_inc(y_stored[par], 16)

                pairs(sp, TILES, lambda g, par, first, last: store_h2(g, par))
                pairs(sp, TILES, lambda g, par, first, last: store_y(g, par))
                sp.wait_ge(pad_stored, 16 * 2 * SLOT_TILES)
                for par in range(2):
                    sp.wait_ge(h2_stored[par], 16 * TILES // 2)
                    sp.wait_ge(y_stored[par], 16 * TILES // 2)

            @block.scalar
            def _(act):
                def split_hi(g, par):
                    act.wait_ge(h2_ready, g + 1)
                    wait(act, hT_raw, g - 1)
                    if not isinstance(g, int) or g >= 2:
                        act.wait_ge(h2_stored[par], (g - par) * 8)
                    nc.scalar.activation(h2p[:, par, 0, :], h2[:, par, :], ACT.Copy,
                                         scale=ACT_SCALE).then_inc(h2_hi, 1)

                def part(g, par, first, last):
                    if first:
                        split_hi(g, par)
                    if not last:
                        split_hi(g + 1, 1 - par)
                    act.wait_ge(hT_raw, g + 1)
                    nc.scalar.activation(h2T_hi[:, :, bass.ds(g * P, P)],
                                         PS[:, par, :].bitcast(fp16)[:, 0:DIM].rearrange("p (k n) -> p k n", k=KC),
                                         ACT.Copy).then_inc(hT_hi_r, 1)

                pairs(act, TILES, part)

                def exponents():
                    act.wait_ge(shifted, 2)
                    nc.scalar.activation(ez[:, :, :], ez[:, :, :], ACT.Exp).then_inc(exp_r, 1)
                    nc.scalar.activation(e8[:, :, :], e8[:, :, :], ACT.Exp).then_inc(exp_r, 1)

                def take_counts():
                    act.wait_ge(count_done, 4)
                    nc.scalar.activation(term[:, :, :].rearrange("p n e -> p (n e)"),
                                         PS[:, 4:6, :].rearrange("p a n -> p (a n)"), ACT.Copy).then_inc(counts_out, 1)
                    nc.scalar.activation(total[:, :, :], PS[:, 6:8, :].rearrange("p a (n e) -> p e (a n)", e=EXPERTS),
                                         ACT.Copy).then_inc(counts_out, 1)

                def shared(q):
                    for j in range(SCH):
                        n = q * SCH + j
                        act.wait_ge(gu_done, n + 1)
                        wait(act, hf_r, n - 1)
                        nc.scalar.activation(silu[:, j % 2, :], PS[:, 2 * (j % 2), :], ACT.Silu,
                                             scale=1.0 / PROD).then_inc(silu_r, 1)
                        act.wait_ge(hf_r, n + 1)
                        wait(act, dn_done, q * GT)
                        nc.scalar.activation(hs_hi[:, j, :], hf[:, j % 2, :], ACT.Copy).then_inc(hs_hi_r, 1)
                        if isinstance(q, int):
                            if j == EXP_AT:
                                exponents()
                            if j == COUNT_AT:
                                take_counts()
                    for c in range(GT):
                        g = q * GT + c
                        act.wait_ge(dn_done, g + 1)
                        wait(act, y_stored[c % 2], (g - c % 2) * 8)
                        nc.scalar.activation(ysh[:, c % 2, :], PS[:, 4 + c % 2, :], ACT.Copy,
                                             scale=1.0 / (H_SCALE * W_SCALE)).then_inc(y_r, 1)

                peeled(act, GROUP, shared)

            @block.tensor
            def _(pe):
                def turn(g, par):
                    pe.wait_ge(h2_lo, g + 1)
                    wait(pe, hT_lo_r, g - 1)
                    for s in range(2):
                        for k in range(KC):
                            last = nc.tensor.transpose(
                                PS[:, par, :].bitcast(fp16)[:, (s * KC + k) * P:(s * KC + k + 1) * P],
                                h2p[:, par, s, k * P:(k + 1) * P], ident16[:, :])
                    last.then_inc(hT_raw, 1)

                def route(g, par):
                    pe.wait_ge(hT_lo_r, g + 1)
                    wait(pe, logit_ready, g - 1)
                    for k in range(KC):
                        for m, (l, r) in enumerate(((h2T_hi, gt_w[0]), (h2T_hi, gt_w[1]), (h2T_lo, gt_w[0]))):
                            last = nc.tensor.matmul(PS[:, 2 + par, 0:EXPERTS], l[:, k, bass.ds(g * P, P)], r[:, k, :],
                                                    start=k == 0 and m == 0, stop=k == KC - 1 and m == 2)
                    last.then_inc(logit_done, 1)

                def both(g, par, first, last):
                    if first:
                        turn(g, par)
                    if not last:
                        turn(g + 1, 1 - par)
                    route(g, par)

                pairs(pe, TILES, both)
                pe.wait_ge(logit_ready, TILES)

                def counts():
                    pe.wait_ge(mask_r, 2)
                    flat = mask[:, :, :].rearrange("p n e -> p (n e)")
                    for m, bank in ((cb[:, 2, :], 4), (cb[:, 3, :], 6)):
                        for side in range(2):
                            nc.tensor.matmul(PS[:, bank + side, :], m, flat[:, side * BANK:(side + 1) * BANK],
                                             start=True, stop=True).then_inc(count_done, 1)

                def shared(q):
                    for j in range(SCH):
                        n = q * SCH + j
                        wait(pe, hf_r, n - 1)
                        for bank, w in enumerate((sg_w, su_w)):
                            for k in range(KC):
                                cols = slice(j * P, (j + 1) * P)
                                toks = bass.ds(q * GT * P, GT * P)
                                for m, (l, r) in enumerate(((w[0], h2T_hi), (w[0], h2T_lo), (w[1], h2T_hi))):
                                    last = nc.tensor.matmul(PS[:, 2 * (j % 2) + bank, :], l[:, k, cols],
                                                            r[:, k, toks], start=k == 0 and m == 0,
                                                            stop=k == KC - 1 and m == 2)
                        last.then_inc(gu_done, 1)
                        if j == COUNT_AT and isinstance(q, int):
                            counts()
                    pe.wait_ge(hs_lo_r, q * SCH + SCH - 1)
                    pe.wait_ge(counts_out, 2)
                    for c in range(GT):
                        wait(pe, y_r, q * GT + c - 1)
                        for j in range(SCH):
                            if c == 0 and j == SCH - 1:
                                pe.wait_ge(hs_lo_r, (q + 1) * SCH)
                            for m, (l, r) in enumerate(((hs_hi, sd_w[0]), (hs_hi, sd_w[1]), (hs_lo, sd_w[0]))):
                                last = nc.tensor.matmul(PS[:, 4 + c % 2, :], l[:, j, c * P:(c + 1) * P], r[:, j, :],
                                                        start=j == 0 and m == 0, stop=j == SCH - 1 and m == 2)
                        last.then_inc(dn_done, 1)

                peeled(pe, GROUP, shared)

            @block.vector
            def _(dve):
                nc.vector.memset(zeros[:, :], 0.0).then_inc(zero_set, 1)

                def normed(g, par, b):
                    wait(dve, h2_ready, g - 1)
                    nc.vector.tensor_scalar(z[:, par, :], x1[:, bass.ds(g, 1), :].rearrange("p a d -> p (a d)"),
                                            stat2[:, bass.ds(g, 1), 0], stat2[:, bass.ds(g, 1), 1],
                                            ALU.subtract, ALU.mult).then_inc(z_ready, 1)
                    dve.wait_ge(z_ready, g + 1)
                    nc.vector.tensor_tensor(z[:, par, :], z[:, par, :], mod2[:, b, 1, :],
                                            ALU.mult).then_inc(zm_ready, 1)

                def low_h2(g, par):
                    dve.wait_ge(h2_hi, g + 1)
                    nc.vector.scalar_tensor_tensor(h2p[:, par, 1, :], h2[:, par, :], ACT_SCALE, h2p[:, par, 0, :],
                                                   ALU.mult, ALU.subtract).then_inc(h2_lo, 1)

                def low_out(g, par):
                    dve.wait_ge(hT_hi_r, g + 1)
                    nc.vector.tensor_copy(
                        h2T_lo[:, :, bass.ds(g * P, P)],
                        PS[:, par, :].bitcast(fp16)[:, DIM:2 * DIM].rearrange("p (k n) -> p k n", k=KC)
                        ).then_inc(hT_lo_r, 1)

                def keep_logits(g, par):
                    dve.wait_ge(logit_done, g + 1)
                    nc.vector.tensor_scalar(logits[:, bass.ds(g, 1), :].rearrange("p a e -> p (a e)"),
                                            PS[:, 2 + par, 0:EXPERTS], 1.0 / PROD, None,
                                            ALU.mult).then_inc(logit_ready, 1)

                def turn(g, par, first, last, b):
                    if first and b == 0:
                        normed(0, 0, 0)
                        normed(1, 1, 0)
                        low_h2(0, 0)
                    two_after = g + 2 - b * BT
                    crosses = isinstance(two_after, int) and two_after >= BT
                    if not (crosses and b == BATCH - 1):
                        normed(g + 2, par, b + 1 if crosses else b)
                    if not (last and b == BATCH - 1):
                        low_h2(g + 1, 1 - par)
                    low_out(g, par)
                    if not (first and b == 0):
                        keep_logits(g - 1, 1 - par)

                for b in range(BATCH):
                    pairs(dve, BT, lambda g, par, first, last: turn(g, par, first, last, b), b * BT)
                keep_logits(TILES - 1, 1)
                dve.wait_ge(logit_ready, TILES)

                steps = [0]

                def step(ins):
                    steps[0] += 1
                    ins.then_inc(rt, 1)

                def link(ins):
                    step(ins)
                    dve.wait_ge(rt, steps[0])

                best = top8[:, :, 0:1]

                def mark_ranks(lo, hi):
                    shape = [P, TILES, hi - lo, EXPERTS]
                    return nc.vector.tensor_tensor(onehot[:, :, lo:hi, :],
                                                   const("iota").unsqueeze(1).unsqueeze(1).broadcast_to(shape),
                                                   idx[:, :, lo:hi].unsqueeze(3).broadcast_to(shape), ALU.is_equal)

                def choose():
                    for g in range(TILES):
                        step(nc.vector.max(top8[:, g, :], logits[:, g, :]))
                    dve.wait_ge(rt, steps[0])
                    for g in range(TILES):
                        step(nc.vector.max_index(top8i[:, g, :], top8[:, g, :], logits[:, g, :]))
                    dve.wait_ge(rt, steps[0])
                    nc.vector.tensor_tensor(ez[:, :, :], logits[:, :, :], best.broadcast_to([P, TILES, EXPERTS]),
                                            ALU.subtract).then_inc(shifted, 1)
                    nc.vector.tensor_tensor(e8[:, :, :], top8[:, :, :], best.broadcast_to([P, TILES, 8]),
                                            ALU.subtract).then_inc(shifted, 1)
                    link(nc.vector.tensor_copy(idx[:, :, :], top8i[:, :, :]))

                def mark():
                    step(mark_ranks(0, TOPK // 2))

                def mark_rest():
                    link(mark_ranks(TOPK // 2, TOPK))

                def merge(lo, hi):
                    nc.vector.tensor_reduce(mask[:, lo:hi, :],
                                            onehot[:, lo:hi, :, :].rearrange("p n k e -> p n e k"), AX.X,
                                            ALU.max).then_inc(mask_r, 1)

                def first_half():
                    merge(0, TILES // 2)

                def second_half():
                    merge(TILES // 2, TILES)

                def weights():
                    dve.wait_ge(exp_r, 2)
                    link(nc.vector.tensor_reduce(sums[:, 0, :], ez[:, :, :], AX.X, ALU.add))
                    link(nc.vector.reciprocal(sums[:, 1, :], sums[:, 0, :]))
                    link(nc.vector.tensor_tensor(e8[:, :, :], e8[:, :, :],
                                                 sums[:, 1, :].unsqueeze(2).broadcast_to([P, TILES, 8]), ALU.mult))
                    link(nc.vector.tensor_reduce(sums[:, 2, :], e8[:, :, 0:TOPK], AX.X, ALU.add))
                    link(nc.vector.tensor_scalar(sums[:, 2, :], sums[:, 2, :], 1e-20, None, ALU.add))
                    link(nc.vector.reciprocal(sums[:, 3, :], sums[:, 2, :]))
                    link(nc.vector.scalar_tensor_tensor(
                        pair[:, :, :, 1].bitcast(fp32), e8[:, :, 0:TOPK], 1.0 / (H_SCALE * W_SCALE),
                        sums[:, 3, :].unsqueeze(2).broadcast_to([P, TILES, TOPK]), ALU.mult, ALU.mult))
                    link(nc.vector.tensor_copy(pair[:, :, :, 0],
                                               const("token").unsqueeze(2).broadcast_to([P, TILES, TOPK])))

                def places():
                    weights()
                    positions()
                    rows()

                def positions():
                    dve.wait_ge(keep_set, 2)
                    dve.wait_ge(counts_out, 2)
                    flat = "p e n -> p (e n)"
                    link(nc.vector.tensor_tensor_scan(cum[:, :, :].rearrange(flat), keep[:, :, :].rearrange(flat),
                                                      total[:, :, :].rearrange(flat), 0.0, ALU.mult, ALU.add))
                    link(nc.vector.tensor_reduce(sums[:, 0, 0:1], cum[:, :, TILES - 1], AX.X, ALU.max))
                    link(nc.vector.tensor_scalar(overflow[:, :], sums[:, 0, 0:1], float(MAIN_TILES * P), None,
                                                 ALU.is_gt))
                    link(nc.vector.tensor_tensor(cum[:, :, :], cum[:, :, :], total[:, :, :], ALU.subtract))
                    link(nc.vector.tensor_tensor(pos[:, :, :], term[:, :, :],
                                                 cum[:, :, :].rearrange("p e n -> p n e"), ALU.add))

                def rows():
                    step_back = float(1 - EXPERTS * SLOT_TILES * P)
                    link(nc.vector.scalar_tensor_tensor(row[:, :, :], pos[:, :, :], float(EXPERTS * SLOT_TILES),
                                                        const("slot0").unsqueeze(1).broadcast_to([P, TILES, EXPERTS]),
                                                        ALU.mult, ALU.add))
                    for edge, value in ((P, step_back), (2 * P, step_back), (CAP, DROPPED)):
                        link(nc.vector.tensor_scalar(term[:, :, :], pos[:, :, :], float(edge), value, ALU.is_ge,
                                                     ALU.mult))
                        link(nc.vector.tensor_tensor(row[:, :, :], row[:, :, :], term[:, :, :], ALU.add))
                    for k in range(TOPK):
                        link(nc.vector.tensor_tensor(term[:, :, :], onehot[:, :, k, :], row[:, :, :], ALU.mult))
                        link(nc.vector.tensor_reduce(rowk[:, :, k], term[:, :, :], AX.X, ALU.add))
                    nc.vector.tensor_copy(row_i[:, :], rowk[:, :, :].rearrange("p n k -> p (n k)")
                                          ).then_inc(pairs_ready, 1)

                router = (choose, mark, mark_rest, first_half, second_half, places)

                def shared(q):
                    for j in range(SCH):
                        n = q * SCH + j
                        dve.wait_ge(silu_r, n + 1)
                        wait(dve, hs_lo_r, n - 1)
                        nc.vector.scalar_tensor_tensor(hf[:, j % 2, :], PS[:, 2 * (j % 2) + 1, :], H_SCALE / PROD,
                                                       silu[:, j % 2, :], ALU.mult, ALU.mult).then_inc(hf_r, 1)
                        dve.wait_ge(hs_hi_r, n + 1)
                        nc.vector.tensor_tensor(hs_lo[:, j, :], hf[:, j % 2, :], hs_hi[:, j, :],
                                                ALU.subtract).then_inc(hs_lo_r, 1)
                        if isinstance(q, int):
                            router[j]()

                peeled(dve, GROUP, shared)

            @block.gpsimd
            def _(pool):

                def shift(g, par, b):
                    pool.wait_ge(zm_ready, g + 1)
                    wait(pool, h2_lo, g - 1)
                    nc.gpsimd.tensor_tensor(h2[:, par, :], z[:, par, :], mod2[:, b, 0, :],
                                            ALU.add).then_inc(h2_ready, 1)

                for b in range(BATCH):
                    pairs(pool, BT, lambda g, par, first, last: shift(g, par, b), b * BT)
                nc.gpsimd.memset(keep[:, :, 1:TILES], 1.0).then_inc(keep_set, 1)
                nc.gpsimd.memset(keep[:, :, 0:1], 0.0).then_inc(keep_set, 1)
                pool.wait_ge(slots_set, 16)
                pool.wait_ge(pairs_ready, 1)
                for n in range(TILES * TOPK):
                    nc.gpsimd.indirect_dma_start(
                        out=slots_d, out_offset=bass.IndirectOffsetOnAxis(ap=row_i[:, n:n + 1], axis=0),
                        in_=pair[:, n // TOPK, n % TOPK, :], in_offset=None, bounds_check=EXPERTS * CAP - 1,
                        oob_is_err=False).then_inc(scattered, 16)
                pool.wait_ge(scattered, 16 * TILES * TOPK)
        s4.close()

        up_shape, dn_shape = [P, 2, KC, 2 * FF], [P, 2, FCH, DIM]
        with ExitStack() as st:
            def sb(name, shape, dt):
                return st.enter_context(nc.sbuf_tensor(name, shape, dt))

            raw_up, raw_dn = sb("raw_up", up_shape, fp32), sb("raw_dn", dn_shape, fp32)
            up_hi, up_lo = sb("up_hi", up_shape, fp16), sb("up_lo", up_shape, fp16)
            dn_hi, dn_lo = sb("dn_hi", dn_shape, fp16), sb("dn_lo", dn_shape, fp16)
            slots = sb("slots", [P, EXPERTS * SLOT_TILES, 2], i32)
            from_row = sb("from_row", [P, 2, MAIN_TILES], i32)
            to_row = sb("to_row", [P, 2, MAIN_TILES], i32)
            xg = sb("xg", [P, 2, MAIN_TILES, 2 * KC, P], fp16)
            xT = sb("xT", [P, 2, 2 * KC, MAIN_TILES, P], fp16)
            silu = sb("silu5", [P, FCH, MAIN_TILES * P], fp32)
            hf = sb("hf5", [P, FCH, MAIN_TILES * P], fp32)
            h_hi = sb("h_hi", [P, 2, FCH, MAIN_TILES * P], fp16)
            h_lo = sb("h_lo", [P, 2, FCH, MAIN_TILES * P], fp16)
            y = sb("y", [P, 2, MAIN_TILES, DIM], fp32)
            WIDTH = [min(P, FF - j * P) for j in range(FCH)]
            HALVES = 2
            KH = KC // HALVES
            UP_BANK, DN_BANK, X_BANK = 0, FCH, FCH + MAIN_TILES

            def expert_pass(tiles, tag, rare):
                NT = len(tiles)
                N = NT * P
                with ExitStack() as ps:
                    names = ("slots_in rows_set ru_a ru_b rd_a rd_b xg_a xg_b add_a add_b turned x_even x_odd up_hi_r "
                             "up_lo_r dn_hi_r dn_lo_r gu_done silu_r hf_r h_hi_r h_lo_r dn_done y_r").split()
                    (slots_in, rows_set, ru_a, ru_b, rd_a, rd_b, xg_a, xg_b, add_a, add_b, turned, x_even, x_odd, up_hi_r,
                     up_lo_r, dn_hi_r, dn_lo_r, gu_done, silu_r, hf_r, h_hi_r, h_lo_r, dn_done, y_r) = sems(
                        ps, " ".join(n + tag for n in names))
                    up_loaded, dn_loaded, gathered, added = (ru_a, ru_b), (rd_a, rd_b), (xg_a, xg_b), (add_a, add_b)
                    block = ps.enter_context(nc.Block())

                    def all_of(e, par):
                        return (e - par) * 8 * NT + 16 * NT

                    def guarded(engine, body):
                        if not rare:
                            body()
                        else:
                            late = engine.value_load(overflow[0:1, 0:1], min_val=0, max_val=1)
                            with engine.If(late > 0):
                                body()

                    def weight_of(e, c):
                        return slots[:, bass.ds(e * SLOT_TILES + c, 1), 1].bitcast(fp32)

                    def weights_of(e, lo, hi):
                        return t["experts"][bass.ds(e, 1), :, lo:hi].rearrange("a p n -> (a p) n")

                    def x_out(e, par, i):
                        return (xT[:, par, :, i, :],
                                PS[:, X_BANK + i, :].bitcast(fp16).rearrange("p (k n) -> p k n", k=2 * KC))

                    @block.sync
                    def _(sp):
                        def load(e, par, first, last):
                            wait(sp, up_lo_r, (e - 1) * HALVES)
                            sp.dma_start(raw_up[:, par, :, :].rearrange("p k n -> p (k n)"),
                                         weights_of(e, 0, UP)).then_inc(up_loaded[par], 16)
                            if first:
                                for turn in range(2):
                                    sp.wait_ge(gathered[turn], 16 * NT)
                            wait(sp, dn_lo_r, e - 1)
                            sp.dma_start(raw_dn[:, par, :, :].rearrange("p k n -> p (k n)"),
                                         weights_of(e, UP, UP + DOWN)).then_inc(dn_loaded[par], 16)

                        sp.dma_start(slots[:, :, :].rearrange("p n w -> p (n w)"),
                                     slots_d.rearrange("(p n) w -> p (n w)", p=P)).then_inc(slots_in, 16)
                        guarded(sp, lambda: pairs(sp, EXPERTS, load))

                    @block.gpsimd
                    def _(pool):
                        def rows(to, e, par, count):
                            nc.gpsimd.tensor_copy(to[:, par, 0:NT], slots[:, bass.ds(e * SLOT_TILES + tiles[0], NT), 0]
                                                  ).then_inc(rows_set, 1)
                            pool.wait_ge(rows_set, count)
                            pool.sem_inc(tick, 1)

                        def gather(e, par, count):
                            wait(pool, turned, (e - 1) * NT)
                            pool.sem_inc(tick, 1)
                            rows(from_row, e, par, count)
                            for i, c in enumerate(tiles):
                                nc.gpsimd.indirect_dma_start(
                                    out=xg[:, par, i, :, :].rearrange("p k n -> p (k n)"), out_offset=None, in_=h2_d,
                                    in_offset=bass.IndirectOffsetOnAxis(
                                        ap=from_row[:, par, i:i + 1], axis=0)
                                ).then_inc(gathered[par], 16)

                        def low_parts(e, par):
                            for j in range(FCH):
                                pool.wait_ge(h_hi_r, e * FCH + j + 1)
                                nc.gpsimd.tensor_tensor(h_lo[0:WIDTH[j], par, j, 0:N], hf[0:WIDTH[j], j, 0:N],
                                                        h_hi[0:WIDTH[j], par, j, 0:N],
                                                        ALU.subtract).then_inc(h_lo_r, 1)

                        def add(e, par, count):
                            wait(pool, added[1 - par], all_of(e - 1, 1 - par))
                            pool.sem_inc(tick, 1)
                            rows(to_row, e, par, count)
                            pool.wait_ge(y_r, (e + 1) * NT)
                            pool.sem_inc(tick, 1)
                            for i, c in enumerate(tiles):
                                nc.gpsimd.indirect_dma_start(
                                    out=y_d, out_offset=bass.IndirectOffsetOnAxis(
                                        ap=to_row[:, par, i:i + 1], axis=0),
                                    in_=y[:, par, i, :], in_offset=None, compute_op=ALU.add,
                                    bounds_check=TOK + CAP - 1, oob_is_err=True).then_inc(added[par], 16)

                        def turn(e, par, first, last):
                            if first:
                                gather(e, par, 1)
                                gather(e + 1, 1 - par, 2)
                            if not isinstance(e, int) or e + 2 < EXPERTS:
                                gather(e + 2, par, e * 2 + 2 + (1 if first else 0))
                            low_parts(e, par)
                            if not first:
                                late = max(0, e + 3 - EXPERTS) if isinstance(e, int) else 0
                                add(e - 1, 1 - par, e * 2 + 3 - late)

                        def body():
                            pool.wait_ge(slots_in, 16)
                            pairs(pool, EXPERTS, turn)
                            add(EXPERTS - 1, 1, 2 * EXPERTS)
                            for par in range(2):
                                pool.wait_ge(added[par], 8 * NT * EXPERTS)

                        guarded(pool, body)

                    @block.tensor
                    def _(pe):
                        def turn_x(e, par, i):
                            pe.wait_ge(gathered[par], all_of(e, par))
                            wait(pe, (x_even, x_odd)[i], e)
                            for k in range(2 * KC):
                                last = nc.tensor.transpose(x_out(e, par, i)[1][:, k, :], xg[:, par, i, k, :],
                                                           ident16[:, :])
                            last.then_inc(turned, 1)

                        def up(e, par, j):
                            w = WIDTH[j]
                            wait(pe, hf_r, e * FCH + j + 1 - FCH)
                            for side in range(2):
                                cols = slice(side * FF + j * P, side * FF + j * P + w)
                                for k in range(KC):
                                    for m, (l, r) in enumerate(((up_hi, k), (up_hi, KC + k), (up_lo, k))):
                                        last = nc.tensor.matmul(
                                            PS[0:w, UP_BANK + j, side * N:(side + 1) * N], l[:, par, k, cols],
                                            xT[:, par, r, 0:NT, :],
                                            start=k == 0 and m == 0, stop=k == KC - 1 and m == 2)
                            last.then_inc(gu_done, 1)

                        def down(e, par):
                            pe.wait_ge(h_lo_r, (e + 1) * FCH)
                            pe.wait_ge(dn_lo_r, e + 1)
                            for i in range(NT):
                                wait(pe, y_r, (e - 1) * NT + i + 1)
                                for j in range(FCH):
                                    w = WIDTH[j]
                                    for m, (l, r) in enumerate(((h_hi, dn_hi), (h_hi, dn_lo), (h_lo, dn_hi))):
                                        last = nc.tensor.matmul(PS[:, DN_BANK + i, :],
                                                                l[0:w, par, j, i * P:(i + 1) * P], r[0:w, par, j, :],
                                                                start=j == 0 and m == 0, stop=j == FCH - 1 and m == 2)
                                last.then_inc(dn_done, 1)

                        def turn(e, par, first, last):
                            if first:
                                for i in range(NT):
                                    turn_x(e, par, i)
                            pe.wait_ge(x_even, e + 1)
                            if NT > 1:
                                pe.wait_ge(x_odd, e + 1)
                            pe.wait_ge(up_lo_r, (e + 1) * HALVES)
                            for j in range(FCH):
                                up(e, par, j)
                                if j < NT and not last:
                                    turn_x(e + 1, 1 - par, j)
                            if not first:
                                down(e - 1, 1 - par)

                        def body():
                            pairs(pe, EXPERTS, turn)
                            down(EXPERTS - 1, 1)

                        guarded(pe, body)

                    @block.scalar
                    def _(act):
                        def x_part(e, par):
                            act.wait_ge(turned, e * NT + 1)
                            to, src = x_out(e, par, 0)
                            nc.scalar.activation(to, src, ACT.Copy).then_inc(x_even, 1)

                        def up_part(e, par, half):
                            act.wait_ge(up_loaded[par], loads(e, par))
                            ks = slice(half * KH, (half + 1) * KH)
                            nc.scalar.activation(up_hi[:, par, ks, :], raw_up[:, par, ks, :], ACT.Copy,
                                                 scale=W_SCALE).then_inc(up_hi_r, 1)

                        def gate(e, par, j):
                            n, w = e * FCH + j, WIDTH[j]
                            act.wait_ge(gu_done, n + 1)
                            wait(act, hf_r, n + 1 - FCH)
                            nc.scalar.activation(silu[0:w, j, 0:N], PS[0:w, UP_BANK + j, 0:N], ACT.Silu,
                                                 scale=1.0 / PROD).then_inc(silu_r, 1)

                        def h_part(e, par, j):
                            act.wait_ge(hf_r, e * FCH + j + 1)
                            nc.scalar.activation(h_hi[0:WIDTH[j], par, j, 0:N], hf[0:WIDTH[j], j, 0:N],
                                                 ACT.Copy).then_inc(h_hi_r, 1)

                        def weigh(e, par):
                            wait(act, added[par], all_of(e - 2, par))
                            for i, c in enumerate(tiles):
                                act.wait_ge(dn_done, e * NT + i + 1)
                                nc.scalar.activation(
                                    y[:, par, i, :], PS[:, DN_BANK + i, :], ACT.Copy,
                                    scale=weight_of(e, c)).then_inc(y_r, 1)

                        def dn_part(e, par):
                            act.wait_ge(dn_loaded[par], loads(e, par))
                            nc.scalar.activation(dn_hi[:, par, :, :], raw_dn[:, par, :, :], ACT.Copy,
                                                 scale=W_SCALE).then_inc(dn_hi_r, 1)

                        def turn(e, par, first, last):
                            if first:
                                x_part(e, par)
                                for half in range(HALVES):
                                    up_part(e, par, half)
                            if not last:
                                up_part(e + 1, 1 - par, 0)
                            gate(e, par, 0)
                            if not last:
                                x_part(e + 1, 1 - par)
                                up_part(e + 1, 1 - par, 1)
                            gate(e, par, 1)
                            h_part(e, par, 0)
                            dn_part(e, par)
                            gate(e, par, 2)
                            h_part(e, par, 1)
                            h_part(e, par, 2)
                            if not first:
                                weigh(e - 1, 1 - par)

                        def body():
                            act.wait_ge(slots_in, 16)
                            pairs(act, EXPERTS, turn)
                            weigh(EXPERTS - 1, 1)

                        if rare:
                            act.wait_ge(slots_in, 16)
                        guarded(act, body)

                    @block.vector
                    def _(dve):
                        def x_part(e, par):
                            if NT > 1:
                                dve.wait_ge(turned, e * NT + 2)
                                to, src = x_out(e, par, 1)
                                nc.vector.tensor_copy(to, src).then_inc(x_odd, 1)

                        def up_part(e, par, half):
                            dve.wait_ge(up_hi_r, e * HALVES + half + 1)
                            flat, ks = "p k n -> p (k n)", slice(half * KH, (half + 1) * KH)
                            nc.vector.scalar_tensor_tensor(up_lo[:, par, ks, :].rearrange(flat),
                                                           raw_up[:, par, ks, :].rearrange(flat), W_SCALE,
                                                           up_hi[:, par, ks, :].rearrange(flat), ALU.mult,
                                                           ALU.subtract).then_inc(up_lo_r, 1)

                        def hidden(e, par, j):
                            n, w = e * FCH + j, WIDTH[j]
                            dve.wait_ge(silu_r, n + 1)
                            wait(dve, h_lo_r, n + 1 - FCH)
                            nc.vector.scalar_tensor_tensor(hf[0:w, j, 0:N], PS[0:w, UP_BANK + j, N:2 * N],
                                                           H_SCALE / PROD, silu[0:w, j, 0:N],
                                                           ALU.mult, ALU.mult).then_inc(hf_r, 1)

                        def dn_part(e, par):
                            dve.wait_ge(dn_hi_r, e + 1)
                            flat = "p k n -> p (k n)"
                            nc.vector.scalar_tensor_tensor(dn_lo[:, par, :, :].rearrange(flat),
                                                           raw_dn[:, par, :, :].rearrange(flat), W_SCALE,
                                                           dn_hi[:, par, :, :].rearrange(flat), ALU.mult,
                                                           ALU.subtract).then_inc(dn_lo_r, 1)

                        def turn(e, par, first, last):
                            if first:
                                x_part(e, par)
                                for half in range(HALVES):
                                    up_part(e, par, half)
                            if not last:
                                up_part(e + 1, 1 - par, 0)
                            hidden(e, par, 0)
                            hidden(e, par, 1)
                            if not last:
                                x_part(e + 1, 1 - par)
                                up_part(e + 1, 1 - par, 1)
                            dn_part(e, par)
                            hidden(e, par, 2)

                        guarded(dve, lambda: pairs(dve, EXPERTS, turn))

            expert_pass(range(MAIN_TILES), "_m", False)
            expert_pass(range(MAIN_TILES, SLOT_TILES), "_r", True)

        with ExitStack() as st:
            def sb(name, shape, dt):
                return st.enter_context(nc.sbuf_tensor(name, shape, dt))

            gate2 = sb("gate2", [P, BATCH, DIM], fp32)
            yin = sb("yin", [P, TILES, DIM], fp32)
            STEPS = 8
            PER = TILES // STEPS
            yin_loaded = sems(st, " ".join(f"yin{n}" for n in range(STEPS)))
            gate2_loaded, dve_scaled, pool_scaled, dve_done, pool_done, stored = sems(
                st, "gate2_loaded dve_scaled pool_scaled dve_done pool_done stored6")
            POOL_TILES = range(1, TILES - 2, 3)
            DVE_TILES = [n for n in range(TILES) if n not in POOL_TILES]
            block = st.enter_context(nc.Block())

            @block.sync
            def _(sp):
                for n in range(STEPS):
                    sp.dma_start(yin[:, n * PER:(n + 1) * PER, :],
                                 y_d[n * PER * P:(n + 1) * PER * P, :].rearrange("(n p) d -> p n d", p=P)
                                 ).then_inc(yin_loaded[n], 16)

            @block.scalar
            def _(act):
                for b in range(BATCH):
                    act.dma_start(gate2[:, b, :], mod_d[b:b + 1, 5 * DIM:6 * DIM].partition_broadcast(P)
                                  .rearrange("p a d -> p (a d)")).then_inc(gate2_loaded, 16)
                for n in range(STEPS):
                    for sem, mine in ((dve_done, DVE_TILES), (pool_done, POOL_TILES)):
                        act.wait_ge(sem, max(1, sum(tile < (n + 1) * PER for tile in mine)))
                    act.dma_start(t["out"][n * PER * P:(n + 1) * PER * P, :].rearrange("(n p) d -> p n d", p=P),
                                  x1[:, n * PER:(n + 1) * PER, :]).then_inc(stored, 16)
                act.wait_ge(stored, 16 * STEPS)

            def finish(engine, ops, mine, scaled, done):
                engine.wait_ge(gate2_loaded, 16 * BATCH)
                for at, n in enumerate(mine):
                    engine.wait_ge(yin_loaded[n // PER], 16)
                    ops.tensor_tensor(yin[:, n, :], yin[:, n, :], gate2[:, n // BT, :], ALU.mult).then_inc(scaled, 1)
                    engine.wait_ge(scaled, at + 1)
                    ops.tensor_tensor(x1[:, n, :], x1[:, n, :], yin[:, n, :], ALU.add).then_inc(done, 1)

            @block.vector
            def _(dve):
                finish(dve, nc.vector, DVE_TILES, dve_scaled, dve_done)

            @block.gpsimd
            def _(pool):
                finish(pool, nc.gpsimd, POOL_TILES, pool_scaled, pool_done)


_OUT = (BATCH, SEQ, DIM)


def laid_out(inputs):
    def split(w, chunks):
        return np.ascontiguousarray(w.reshape(chunks, P, -1).transpose(1, 0, 2))

    def padded(w, rows):
        return np.concatenate([w, np.zeros((rows - w.shape[0], w.shape[1]), w.dtype)], 0)

    a = {k[3:]: np.asarray(v) for k, v in inputs.items()}
    wg = a["ffn_w_gate"].transpose(0, 2, 1).reshape(EXPERTS, KC, P, 1, FF)
    wu = a["ffn_w_up"].transpose(0, 2, 1).reshape(EXPERTS, KC, P, 1, FF)
    up = np.concatenate([wg, wu], 3).transpose(0, 2, 1, 3, 4).reshape(EXPERTS, P, UP)
    wd = a["ffn_w_down"].transpose(0, 2, 1)
    wd = np.concatenate([wd, np.zeros((EXPERTS, FCH * P - FF, DIM), wd.dtype)], 1)
    down = wd.reshape(EXPERTS, FCH, P, DIM).transpose(0, 2, 1, 3).reshape(EXPERTS, P, DOWN)
    return {
        "x": np.ascontiguousarray(a["attn_x"].reshape(TOK, DIM)),
        "c": np.ascontiguousarray(a["c"].T.reshape(KC, P, BATCH).transpose(1, 0, 2).reshape(P, KC * BATCH)),
        "wmod": split(a["wmod"], KC),
        "wqkv": split(a["attn_Wqkv"], KC),
        "wo": split(a["attn_Wo"], KC),
        "ffn": np.concatenate([w.reshape(P, -1) for w in (
            split(a["ffn_gate_w"].T, KC), split(padded(a["ffn_sh_gate"], SHP).T, KC),
            split(padded(a["ffn_sh_up"], SHP).T, KC), split(padded(a["ffn_sh_down"].T, SHP), SCH))], 1),
        "experts": np.ascontiguousarray(np.concatenate([up, down], 2)),
        "consts": constants(),
        "slots": empty_slots(),
    }


def kernel(**inputs):
    import concourse.bacc as bacc
    from concourse.bass_utils import run_bass_kernel_spmd

    nc = bacc.Bacc("TRN2", target_bir_lowering=False, num_devices=1)
    arrays = laid_out(inputs)
    t = {k: nc.dram_tensor("in_" + k, v.shape, mybir.dt.from_np(v.dtype), kind="ExternalInput").ap()
         for k, v in arrays.items()}
    t["out"] = nc.dram_tensor("out", (TOK, DIM), mybir.dt.float32, kind="ExternalOutput").ap()
    adaln_program(nc, t)
    r = run_bass_kernel_spmd(nc, [{"in_" + k: v for k, v in arrays.items()}], core_ids=[0])
    return r.results[0]["out"].reshape(_OUT)
```
